# Optimizing a Trainium2 kernel written in Bass

```python
import numpy as np
import jax
import jax.numpy as jnp

def _softmax(x, axis=-1):
    return jax.nn.softmax(x, axis=axis)

def _gelu(x):
    return jax.nn.gelu(x, approximate=True)

def _silu(x):
    return jax.nn.silu(x)

def _sigmoid(x):
    return jax.nn.sigmoid(x)

def _layernorm(x, axis=-1, eps=1e-05):
    m = jnp.mean(x, axis=axis, keepdims=True)
    v = jnp.var(x, axis=axis, keepdims=True)
    return (x - m) / jnp.sqrt(v + eps)

def _scatter_add(tgt, idx, src, axis=0):
    return tgt.at[idx].add(src)

def _segment_sum(src, seg, n):
    return jax.ops.segment_sum(src, seg, n)
kernel_name = 'mk_lm_tower_d2_tok_ids1024_r4_280da3'

def setup_inputs(seed: int=0):
    np.random.seed(seed)
    _w = jnp.asarray

    def _rec_inputs():
        import jax
        import jax.numpy as jnp
        _rk = jax.random.key(seed)
        x = jax.random.randint(jax.random.fold_in(_rk, 1), (8, 512), 0, 250, jnp.int32)
        return x
    x = _rec_inputs()

    def _L0_tok_setup():
        import math
        import jax, jax.numpy as jnp
        import numpy as np
        PAD_IDX = 1
        SEP_ID = 4
        STARTPOS = 1025
        BSZ, SEQ_LEN, EMBED_DIM = (32, 1024, 256)

        def _build_table(num_cons, dim, padding_idx, startpos):
            half = dim // 2
            freqs = jnp.exp(jnp.arange(half, dtype=jnp.float32) * -(math.log(10000.0) / (half - 1)))
            ang = jnp.arange(startpos, startpos + num_cons, dtype=jnp.float32)[:, None] * freqs[None, :]
            tab = jnp.concatenate([jnp.sin(ang), jnp.cos(ang)], axis=1)
            return tab.at[padding_idx].set(0.0)

        def _positions(tokens):
            L = tokens.shape[1]
            valid = jnp.cumprod((tokens != PAD_IDX).astype(jnp.int32), axis=1).astype(bool)
            j = jnp.arange(L, dtype=jnp.int32)
            sep_j = jnp.where(tokens == SEP_ID, j, 0)
            last_sep = jax.lax.associative_scan(jnp.maximum, sep_j, axis=1)
            pos = j - last_sep + 2
            return jnp.where(valid, pos, 1)
        key = jax.random.key(seed)
        tokens = jax.random.randint(key, (BSZ, SEQ_LEN), 0, 250, dtype=jnp.int64)
        num_cons = PAD_IDX + 1 + SEQ_LEN
        weights = _build_table(num_cons, EMBED_DIM, PAD_IDX, STARTPOS)
        return {'input': tokens, 'weights': weights}
    _L0_tok_all = _L0_tok_setup()
    _L0_tok_in = {k: v for k, v in _L0_tok_all.items() if k in ('weights',)}
    del _L0_tok_all

    def _L0_attn_setup():
        import jax, jax.numpy as jnp
        import numpy as np
        BITS = 8
        NUM_HEADS = 16
        EPS = 0.01

        def _max_scale_rp(x, axis):
            m = jnp.maximum(jnp.max(jnp.abs(x), axis=axis), EPS)
            return jnp.exp2(jnp.ceil(jnp.log2(m)))

        def _dmd_dequant(x):
            half = float(1 << BITS - 1)
            s1 = _max_scale_rp(x, -2)
            x = x / s1[..., None, :]
            s2 = _max_scale_rp(x, -1)
            x = x / s2[..., None]
            q = jnp.clip(jnp.round(x * half), -half, half - 1.0)
            return s1[..., None, :] * q * (s2 / half)[..., None]

        def qmatmul(x, y):
            return jnp.matmul(_dmd_dequant(x), _dmd_dequant(y))
        key = jax.random.key(seed)
        k1, k2, k3 = jax.random.split(key, 3)
        B, S, E = (4, 256, 256)
        hidden_states = jax.random.normal(k1, (B, S, E), dtype=jnp.float32)
        w_attn = jax.random.normal(k2, (E, 3 * E), dtype=jnp.float32) * 0.02
        b_attn = jnp.zeros((3 * E,), dtype=jnp.float32)
        w_proj = jax.random.normal(k3, (E, E), dtype=jnp.float32) * 0.02
        b_proj = jnp.zeros((E,), dtype=jnp.float32)
        return {'hidden_states': hidden_states, 'w_attn': w_attn, 'b_attn': b_attn, 'w_proj': w_proj, 'b_proj': b_proj}
    _L0_attn_all = _L0_attn_setup()
    _L0_attn_in = {k: v for k, v in _L0_attn_all.items() if k in ('w_attn', 'b_attn', 'w_proj', 'b_proj')}
    del _L0_attn_all

    def _L0_ffn_setup():
        import jax, jax.numpy as jnp
        import numpy as np
        DIM = 256
        HIDDEN = 768
        SCALE = 1.0 / 127.0

        def _dequant(w_int, dtype):
            return w_int.astype(dtype) * jnp.asarray(SCALE, dtype)
        key = jax.random.key(seed)
        k_x, k_g, k_u, k_d = jax.random.split(key, 4)
        x = jax.random.normal(k_x, (4, 512, DIM), dtype=jnp.float32)
        w_gate = jax.random.randint(k_g, (HIDDEN, DIM), -127, 128, dtype=jnp.int32)
        w_up = jax.random.randint(k_u, (HIDDEN, DIM), -127, 128, dtype=jnp.int32)
        w_down = jax.random.randint(k_d, (DIM, HIDDEN), -127, 128, dtype=jnp.int32)
        return {'x': x, 'w_gate': w_gate, 'w_up': w_up, 'w_down': w_down}
    _L0_ffn_all = _L0_ffn_setup()
    _L0_ffn_in = {k: v for k, v in _L0_ffn_all.items() if k in ('w_gate', 'w_up', 'w_down')}
    del _L0_ffn_all

    def _L1_attn_setup():
        import jax, jax.numpy as jnp
        import numpy as np
        import math
        B, N, D, K = (4, 1024, 256, 8)
        key = jax.random.key(seed)
        ks = jax.random.split(key, 9)
        s = 0.02
        return {'summaries': jax.random.normal(ks[0], (B, N, D), dtype=jnp.float32), 'Wq': jax.random.normal(ks[1], (D, D), dtype=jnp.float32) * s, 'bq': jnp.zeros((D,), dtype=jnp.float32), 'Wk': jax.random.normal(ks[2], (D, D), dtype=jnp.float32) * s, 'bk': jnp.zeros((D,), dtype=jnp.float32), 'Wv': jax.random.normal(ks[3], (D, D), dtype=jnp.float32) * s, 'bv': jnp.zeros((D,), dtype=jnp.float32), 'Wo': jax.random.normal(ks[4], (D, D), dtype=jnp.float32) * s, 'bo': jnp.zeros((D,), dtype=jnp.float32)}
    _L1_attn_all = _L1_attn_setup()
    _L1_attn_in = {k: v for k, v in _L1_attn_all.items() if k in ('Wq', 'bq', 'Wk', 'bk', 'Wv', 'bv', 'Wo', 'bo')}
    del _L1_attn_all

    def _L1_ffn_setup():
        import jax, jax.numpy as jnp
        import numpy as np
        B, K, D = (128, 32, 256)
        E = 32
        H = int(D * 0.25)

        def _rsqrt_uniform(key, shape, d):
            bound = d ** (-0.5)
            return jax.random.uniform(key, shape, jnp.float32, -bound, bound)
        key = jax.random.key(seed)
        ks = jax.random.split(key, 7)
        return {'x': jax.random.normal(ks[0], (B, K, D), jnp.float32), 'router_w': _rsqrt_uniform(ks[1], (E, D), D), 'router_b': _rsqrt_uniform(ks[2], (E,), D), 'weights1': _rsqrt_uniform(ks[3], (E, D, H), H), 'bias1': _rsqrt_uniform(ks[4], (E, H), H), 'weights2': _rsqrt_uniform(ks[5], (E, H, D), D), 'bias2': _rsqrt_uniform(ks[6], (E, D), D)}
    _L1_ffn_all = _L1_ffn_setup()
    _L1_ffn_in = {k: v for k, v in _L1_ffn_all.items() if k in ('router_w', 'router_b', 'weights1', 'bias1', 'weights2', 'bias2')}
    del _L1_ffn_all
    return {'x': x, 'L0_tok_weights': _L0_tok_in['weights'], 'L0_attn_w_attn': _L0_attn_in['w_attn'], 'L0_attn_b_attn': _L0_attn_in['b_attn'], 'L0_attn_w_proj': _L0_attn_in['w_proj'], 'L0_attn_b_proj': _L0_attn_in['b_proj'], 'L0_ffn_w_gate': _L0_ffn_in['w_gate'], 'L0_ffn_w_up': _L0_ffn_in['w_up'], 'L0_ffn_w_down': _L0_ffn_in['w_down'], 'L1_attn_Wq': _L1_attn_in['Wq'], 'L1_attn_bq': _L1_attn_in['bq'], 'L1_attn_Wk': _L1_attn_in['Wk'], 'L1_attn_bk': _L1_attn_in['bk'], 'L1_attn_Wv': _L1_attn_in['Wv'], 'L1_attn_bv': _L1_attn_in['bv'], 'L1_attn_Wo': _L1_attn_in['Wo'], 'L1_attn_bo': _L1_attn_in['bo'], 'L1_ffn_router_w': _L1_ffn_in['router_w'], 'L1_ffn_router_b': _L1_ffn_in['router_b'], 'L1_ffn_weights1': _L1_ffn_in['weights1'], 'L1_ffn_bias1': _L1_ffn_in['bias1'], 'L1_ffn_weights2': _L1_ffn_in['weights2'], 'L1_ffn_bias2': _L1_ffn_in['bias2']}

def reference(x, L0_tok_weights, L0_attn_w_attn, L0_attn_b_attn, L0_attn_w_proj, L0_attn_b_proj, L0_ffn_w_gate, L0_ffn_w_up, L0_ffn_w_down, L1_attn_Wq, L1_attn_bq, L1_attn_Wk, L1_attn_bk, L1_attn_Wv, L1_attn_bv, L1_attn_Wo, L1_attn_bo, L1_ffn_router_w, L1_ffn_router_b, L1_ffn_weights1, L1_ffn_bias1, L1_ffn_weights2, L1_ffn_bias2):
    import jax
    import jax.numpy as jnp

    def _L0_tok_ref(input, weights):
        import math
        import jax, jax.numpy as jnp
        import numpy as np
        PAD_IDX = 1
        SEP_ID = 4
        STARTPOS = 1025
        BSZ, SEQ_LEN, EMBED_DIM = (32, 1024, 256)

        def _build_table(num_cons, dim, padding_idx, startpos):
            half = dim // 2
            freqs = jnp.exp(jnp.arange(half, dtype=jnp.float32) * -(math.log(10000.0) / (half - 1)))
            ang = jnp.arange(startpos, startpos + num_cons, dtype=jnp.float32)[:, None] * freqs[None, :]
            tab = jnp.concatenate([jnp.sin(ang), jnp.cos(ang)], axis=1)
            return tab.at[padding_idx].set(0.0)

        def _positions(tokens):
            L = tokens.shape[1]
            valid = jnp.cumprod((tokens != PAD_IDX).astype(jnp.int32), axis=1).astype(bool)
            j = jnp.arange(L, dtype=jnp.int32)
            sep_j = jnp.where(tokens == SEP_ID, j, 0)
            last_sep = jax.lax.associative_scan(jnp.maximum, sep_j, axis=1)
            pos = j - last_sep + 2
            return jnp.where(valid, pos, 1)
        pos = _positions(input)
        return jnp.take(weights, pos, axis=0)

    def _L0_attn_ref(hidden_states, w_attn, b_attn, w_proj, b_proj):
        import jax, jax.numpy as jnp
        import numpy as np
        BITS = 8
        NUM_HEADS = 16
        EPS = 0.01

        def _max_scale_rp(x, axis):
            m = jnp.maximum(jnp.max(jnp.abs(x), axis=axis), EPS)
            return jnp.exp2(jnp.ceil(jnp.log2(m)))

        def _dmd_dequant(x):
            half = float(1 << BITS - 1)
            s1 = _max_scale_rp(x, -2)
            x = x / s1[..., None, :]
            s2 = _max_scale_rp(x, -1)
            x = x / s2[..., None]
            q = jnp.clip(jnp.round(x * half), -half, half - 1.0)
            return s1[..., None, :] * q * (s2 / half)[..., None]

        def qmatmul(x, y):
            return jnp.matmul(_dmd_dequant(x), _dmd_dequant(y))
        B, S, E = hidden_states.shape
        H = NUM_HEADS
        D = E // H
        qkv = qmatmul(hidden_states.reshape(-1, E), w_attn) + b_attn
        qkv = qkv.reshape(B, S, 3 * E)
        q, k, v = jnp.split(qkv, 3, axis=-1)
        split_heads = lambda t: t.reshape(B, S, H, D).transpose(0, 2, 1, 3)
        q, k, v = (split_heads(q), split_heads(k), split_heads(v))
        aw = qmatmul(q, jnp.swapaxes(k, -1, -2)) / jnp.asarray(D ** 0.5, jnp.float32)
        causal = jnp.tril(jnp.ones((S, S), dtype=bool))
        aw = jnp.where(causal, aw, jnp.finfo(aw.dtype).min)
        aw = jax.nn.softmax(aw, axis=-1)
        out = qmatmul(aw, v)
        out = out.transpose(0, 2, 1, 3).reshape(B, S, E)
        out = qmatmul(out.reshape(-1, E), w_proj) + b_proj
        return out.reshape(B, S, E)

    def _L0_ffn_ref(x, w_gate, w_up, w_down):
        import jax, jax.numpy as jnp
        import numpy as np
        DIM = 256
        HIDDEN = 768
        SCALE = 1.0 / 127.0

        def _dequant(w_int, dtype):
            return w_int.astype(dtype) * jnp.asarray(SCALE, dtype)
        wg = _dequant(w_gate, x.dtype)
        wu = _dequant(w_up, x.dtype)
        wd = _dequant(w_down, x.dtype)
        gate = jnp.einsum('bsd,hd->bsh', x, wg)
        up = jnp.einsum('bsd,hd->bsh', x, wu)
        h = jax.nn.silu(gate) * up
        return jnp.einsum('bsh,dh->bsd', h, wd)

    def _L1_attn_ref(summaries, Wq, bq, Wk, bk, Wv, bv, Wo, bo):
        import jax, jax.numpy as jnp
        import numpy as np
        import math
        B, N, D, K = (4, 1024, 256, 8)
        b_, n_, d_ = summaries.shape
        q = summaries @ Wq + bq
        k = summaries @ Wk + bk
        v = summaries @ Wv + bv
        scores = jnp.einsum('bnd,bmd->bnm', q, k) / math.sqrt(d_)
        causal = jnp.triu(jnp.full((n_, n_), -jnp.inf, dtype=scores.dtype), k=1)
        scores = scores + causal
        topk_vals, topk_idx = jax.lax.top_k(scores, K)
        bi = jnp.arange(b_)[:, None, None]
        ri = jnp.arange(n_)[None, :, None]
        sparse = jnp.full_like(scores, -jnp.inf).at[bi, ri, topk_idx].set(topk_vals)
        attn = jax.nn.softmax(sparse, axis=-1)
        out = jnp.einsum('bnm,bmd->bnd', attn, v)
        return out @ Wo + bo

    def _L1_ffn_ref(x, router_w, router_b, weights1, bias1, weights2, bias2):
        import jax, jax.numpy as jnp
        import numpy as np
        B, K, D = (128, 32, 256)
        E = 32
        H = int(D * 0.25)

        def _rsqrt_uniform(key, shape, d):
            bound = d ** (-0.5)
            return jax.random.uniform(key, shape, jnp.float32, -bound, bound)
        b, k, d = x.shape
        x_flat = x.reshape(-1, d)
        n = x_flat.shape[0]
        logits = x_flat @ router_w.T + router_b
        routed_idx = jnp.argmax(logits, axis=-1)

        def expert_mlp(w1, b1, w2, b2):
            h = jax.nn.relu(x_flat @ w1 + b1)
            return jax.nn.relu(h @ w2 + b2)
        y_all = jax.vmap(expert_mlp)(weights1, bias1, weights2, bias2)
        out_flat = y_all[routed_idx, jnp.arange(n)]
        return out_flat.reshape(b, k, d)
    h = _L0_tok_ref(x, L0_tok_weights)
    h = h + _L0_attn_ref(_layernorm(h, axis=-1), L0_attn_w_attn, L0_attn_b_attn, L0_attn_w_proj, L0_attn_b_proj)
    h = h + _L0_ffn_ref(_layernorm(h, axis=-1), L0_ffn_w_gate, L0_ffn_w_up, L0_ffn_w_down)
    h = h + _L1_attn_ref(_layernorm(h, axis=-1), L1_attn_Wq, L1_attn_bq, L1_attn_Wk, L1_attn_bk, L1_attn_Wv, L1_attn_bv, L1_attn_Wo, L1_attn_bo)
    h = h + _L1_ffn_ref(_layernorm(h, axis=-1), L1_ffn_router_w, L1_ffn_router_b, L1_ffn_weights1, L1_ffn_bias1, L1_ffn_weights2, L1_ffn_bias2)
    return h

_drawn_inputs = setup_inputs


def setup_inputs(seed=0):
    import zlib

    import numpy as np

    out = dict(_drawn_inputs(seed))
    spreads = {'L0_attn_b_attn': (0.0, 0.1),
     'L0_attn_b_proj': (0.0, 0.1),
     'L1_attn_bq': (0.0, 2.0),
     'L1_attn_bk': (0.0, 0.8),
     'L1_attn_bv': (0.0, 2.0),
     'L1_attn_bo': (0.0, 2.0)}
    factors = {'L1_attn_Wq': 64.0,
     'L1_attn_Wk': 64.0,
     'L1_attn_Wv': 64.0,
     'L1_attn_Wo': 64.0,
     'L1_ffn_router_w': 47.74,
     'L1_ffn_router_b': 64.0,
     'L1_ffn_weights1': 59.562,
     'L1_ffn_bias1': 64.0,
     'L1_ffn_weights2': 51.363,
     'L1_ffn_bias2': 64.0}
    for name, (base, spread) in spreads.items():
        noise = np.random.default_rng([zlib.crc32(name.encode()), seed]).standard_normal(out[name].shape)
        drawn = base * np.exp(spread * noise) if base else spread * noise
        out[name] = jnp.asarray(drawn.astype(out[name].dtype))
    for name, factor in factors.items():
        out[name] = (out[name] * factor).astype(out[name].dtype)
    return out
```

```python
from contextlib import ExitStack

import numpy as np
import concourse.bass as bass
from concourse import mybir

F32, BF16, I32 = mybir.dt.float32, mybir.dt.bfloat16, mybir.dt.int32
ALU = mybir.AluOpType
ACT = mybir.ActivationFunctionType
AX = mybir.AxisListType.X
ABSMAX = bass.bass_isa.ReduceOp.absmax

P = 128
B, S, E = 8, 512, 256
T = B * S // P
TB = S // P
EC = E // P
HEADS, HD = 16, 16
HG = 4
NG = B * HEADS // HG
STRIP = 32
PAD_ID, SEP_ID = 1, 4
ROUND = 1.5 * 2.0 ** 23
PRED = 1.0 - 2.0 ** -24
SLACK = 1.0 - 2.0 ** -16
EPS_Q = 0.01
EPS_LN = 1e-5
NEG = -1e30


class Steps:

    def __init__(self, eng, sem, i=None, per=0, base=0):
        self.eng, self.sem, self.n, self.i, self.per, self.base = eng, sem, 0, i, per, base

    def link(self, ins):
        self.n += 1
        ins.then_inc(self.sem, 1)
        at = self.base + self.n
        self.eng.wait_ge(self.sem, at if self.i is None else self.i * self.per + at)

    def close(self):
        assert self.i is None or self.n == self.per, (self.n, self.per)


def row(ap):
    return ap.rearrange("(a n) -> a n", a=1).broadcast_to([P, ap.shape[0]])


def pow2_up(nc, st, out, inv, x, low, tmp, slack=PRED):
    st.link(nc.vector.tensor_scalar(tmp, x, low, slack, ALU.max, ALU.mult))
    st.link(nc.vector.tensor_single_scalar(tmp.bitcast(I32), tmp.bitcast(I32), -(1 << 23), ALU.bitwise_and))
    if inv is not None:
        st.link(nc.vector.tensor_scalar(inv.bitcast(I32), tmp.bitcast(I32), -1.0, float(253 << 23), ALU.mult, ALU.add))
    st.link(nc.vector.tensor_scalar(out, tmp, 2.0, None, ALU.mult))


def constants_and_tokens(nc, g, tokens, table):
    with ExitStack() as c:
        sb = lambda n, s, d: c.enter_context(nc.sbuf_tensor(n, s, d))
        tok = sb("tok", [B, S], I32)
        place = sb("place", [B, S], I32)
        placef = sb("placef", [B, S], F32)
        sep_at = sb("sep_at", [B, S], F32)
        last_sep = sb("last_sep", [B, S], F32)
        not_pad = sb("not_pad", [B, S], F32)
        valid = sb("valid", [B, S], F32)
        back = sb("back", [B, S], F32)
        pos = sb("pos", [B, S], F32)
        rows = sb("rows", [P, T], I32)
        tokens_in = g.sem("tokens_in")
        made = g.sem("made")
        chain = g.sem("tok_chain")
        pos_ready = g.sem("pos_ready")
        pos_turned = g.sem("pos_turned")
        rows_ready = g.sem("rows_ready")
        gathered = g.sem("gathered")
        block = c.enter_context(nc.Block())

        @block.sync
        def _(sp):
            sp.dma_start(tok[:], tokens).then_inc(tokens_in, 16)

        @block.gpsimd
        def _(pool):
            st = Steps(pool, made)
            st.link(nc.gpsimd.iota(place[:], pattern=[[1, S]], base=0, channel_multiplier=0))
            st.link(nc.gpsimd.memset(g.ident[:], 1.0))
            st.link(nc.gpsimd.affine_select(out=g.ident[:], in_=g.ident[:], compare_op=ALU.is_equal, fill=0.0,
                                            base=0, pattern=[[-1, P]], channel_multiplier=1))
            st.link(nc.gpsimd.memset(g.identf[:], 1.0))
            st.link(nc.gpsimd.affine_select(out=g.identf[:], in_=g.identf[:], compare_op=ALU.is_equal, fill=0.0,
                                            base=0, pattern=[[-1, P]], channel_multiplier=1))
            st.link(nc.gpsimd.memset(g.mask_q[:], 0.0))
            st.link(nc.gpsimd.affine_select(out=g.mask_q[:], in_=g.mask_q[:], compare_op=ALU.is_ge, fill=NEG,
                                            base=0, pattern=[[-1, P]], channel_multiplier=1))
            st.link(nc.gpsimd.memset(g.mask_k[:], 0.0))
            st.link(nc.gpsimd.affine_select(out=g.mask_k[:], in_=g.mask_k[:], compare_op=ALU.is_ge, fill=NEG,
                                            base=0, pattern=[[1, P]], channel_multiplier=-1))
            pool.wait_ge(rows_ready, 1)
            for t in range(T):
                nc.gpsimd.indirect_dma_start(out=g.H[:, t, :], out_offset=None, in_=table,
                                             in_offset=bass.IndirectOffsetOnAxis(ap=rows[:, t:t + 1], axis=0)
                                             ).then_inc(gathered, 16)
            pool.wait_ge(gathered, 16 * T)

        @block.vector
        def _(dve):
            st = Steps(dve, chain)
            dve.wait_ge(made, 1)
            dve.wait_ge(tokens_in, 16)
            st.link(nc.vector.tensor_copy(placef[:], place[:]))
            st.link(nc.vector.scalar_tensor_tensor(out=sep_at[:], in0=tok[:], scalar=float(SEP_ID), in1=placef[:],
                                                   op0=ALU.is_equal, op1=ALU.mult))
            st.link(nc.vector.tensor_tensor_scan(last_sep[:], sep_at[:], sep_at[:], 0.0, ALU.max, ALU.max))
            st.link(nc.vector.tensor_single_scalar(not_pad[:], tok[:], float(PAD_ID), ALU.not_equal))
            st.link(nc.vector.tensor_tensor_scan(valid[:], not_pad[:], not_pad[:], 1.0, ALU.mult, ALU.min))
            st.link(nc.vector.tensor_tensor(back[:], placef[:], last_sep[:], ALU.subtract))
            st.link(nc.vector.scalar_tensor_tensor(out=back[:], in0=back[:], scalar=1.0, in1=valid[:],
                                                   op0=ALU.add, op1=ALU.mult))
            nc.vector.tensor_single_scalar(pos[:], back[:], 1.0, ALU.add).then_inc(pos_ready, 1)
            dve.wait_ge(pos_turned, 1)
            nc.vector.tensor_copy(rows[:].rearrange("p (b t) -> p t b", b=B),
                                  g.PS[:, 0, 0:T].rearrange("p (t b) -> p t b", b=B)).then_inc(rows_ready, 1)

        @block.tensor
        def _(pe):
            pe.wait_ge(made, 5)
            pe.wait_ge(pos_ready, 1)
            for t in range(TB):
                last = nc.tensor.transpose(g.PS[:, 0, t * B:(t + 1) * B], pos[:, t * P:(t + 1) * P], g.identf[0:B, 0:B])
            last.then_inc(pos_turned, 1)


def moments(nc, g, tag):
    with ExitStack() as c:
        sb = lambda n, s=[P, T]: c.enter_context(nc.sbuf_tensor(tag + n, s, F32))
        stats, diff, ve, root, half = sb("stats", [P, T, 6]), sb("diff"), sb("ve"), sb("root"), sb("half")
        chain, stat_n, var_ready, root_ready = (g.sem(tag + n) for n in ("ln_chain", "stat_n", "var_ready", "root_ready"))
        block = c.enter_context(nc.Block())

        @block.scalar
        def _(act):
            nc.scalar.preload_act_table(ACT.Sqrt)
            act.wait_ge(var_ready, 1)
            nc.scalar.activation(root[:], ve[:], ACT.Sqrt).then_inc(root_ready, 1)

        @block.vector
        def _(dve):
            with dve.Fori(0, T) as t:
                nc.vector.bn_stats(stats[:, bass.ds(t, 1), :], g.H[:, bass.ds(t, 1), :]).then_inc(stat_n, 1)
            dve.wait_ge(stat_n, T)
            mean_even, m2_even, mean_odd, m2_odd = (stats[:, :, n] for n in (1, 2, 4, 5))
            st = Steps(dve, chain)
            st.link(nc.vector.tensor_tensor(diff[:], mean_even, mean_odd, ALU.subtract))
            st.link(nc.vector.tensor_tensor(g.mean[:], mean_even, mean_odd, ALU.add))
            st.link(nc.vector.tensor_single_scalar(g.mean[:], g.mean[:], 0.5, ALU.mult))
            st.link(nc.vector.tensor_tensor(half[:], m2_even, m2_odd, ALU.add))
            st.link(nc.vector.tensor_tensor(diff[:], diff[:], diff[:], ALU.mult))
            st.link(nc.vector.tensor_scalar(diff[:], diff[:], 0.25, EPS_LN, ALU.mult, ALU.add))
            nc.vector.scalar_tensor_tensor(out=ve[:], in0=half[:], scalar=1.0 / E, in1=diff[:], op0=ALU.mult,
                                           op1=ALU.add).then_inc(var_ready, 1)
            dve.wait_ge(root_ready, 1)
            st.link(nc.vector.reciprocal(half[:], root[:]))
            st.link(nc.vector.tensor_tensor(half[:], half[:], ve[:], ALU.mult))
            st.link(nc.vector.tensor_tensor(half[:], half[:], root[:], ALU.add))
            st.link(nc.vector.tensor_single_scalar(half[:], half[:], 0.5, ALU.mult))
            st.link(nc.vector.reciprocal(g.rstd[:], half[:]))


def normalise(nc, g, out, t):
    return nc.vector.tensor_scalar(out, g.H[:, bass.ds(t, 1), :].rearrange("p a e -> p (a e)"),
                                   g.mean[:, bass.ds(t, 1)],
                                   g.rstd[:, bass.ds(t, 1)], ALU.subtract, ALU.mult)


def layernorm(nc, g, Y, tag):
    moments(nc, g, tag)
    with nc.Block() as block:
        @block.vector
        def _(dve):
            with dve.Fori(0, T) as t:
                normalise(nc, g, Y[:, bass.ds(t, 1), :].rearrange("p a e -> p (a e)"), t)


def quantise(nc, g, X, out, n, width, scale2, fold, tag):
    with ExitStack() as c:
        sb = lambda nm, s, d=F32: c.enter_context(nc.sbuf_tensor(tag + nm, s, d))
        col = sb("col", [P, width])
        colb = sb("colb", [P, width])
        tmpc = sb("tmpc", [P, width])
        s1 = sb("s1", [P, width])
        s1i = sb("s1i", [P, width])
        rmax = sb("rmax", [P, n])
        tmpr = sb("tmpr", [P, n])
        s2i = sb("s2i", [P, n])
        chain = g.sem(tag + "q_chain")
        col_ready = g.sem(tag + "col_ready")
        col_all = g.sem(tag + "col_all")
        block = c.enter_context(nc.Block())
        full = [P, n, width]
        by_col = lambda a: a[:].unsqueeze(1).broadcast_to(full)
        by_row = lambda a: a.unsqueeze(2).broadcast_to(full)

        @block.gpsimd
        def _(pool):
            pool.wait_ge(col_ready, 1)
            nc.gpsimd.partition_all_reduce(colb[:], col[:], P, ABSMAX).then_inc(col_all, 1)

        @block.vector
        def _(dve):
            st = Steps(dve, chain)
            nc.vector.tensor_reduce(col[:], X.rearrange("p t e -> p e t"), AX, ALU.max,
                                    apply_absolute_value=True).then_inc(col_ready, 1)
            dve.wait_ge(col_all, 1)
            pow2_up(nc, st, s1[:], s1i[:], colb[:], EPS_Q, tmpc[:])
            st.link(nc.vector.tensor_tensor(X, X, by_col(s1i), ALU.mult))
            st.link(nc.vector.tensor_reduce(rmax[:], X, AX, ALU.max, apply_absolute_value=True))
            pow2_up(nc, st, scale2, s2i[:], rmax[:], EPS_Q, tmpr[:])
            st.link(nc.vector.tensor_single_scalar(scale2, scale2, 1.0 / 128, ALU.mult))
            st.link(nc.vector.tensor_tensor(X, X, by_row(s2i[:]), ALU.mult))
            st.link(nc.vector.tensor_scalar(X, X, 128.0, ROUND, ALU.mult, ALU.add))
            st.link(nc.vector.tensor_scalar(X, X, ROUND, 127.0, ALU.subtract, ALU.min))
            if fold:
                st.link(nc.vector.tensor_tensor(X, X, by_row(scale2), ALU.mult))
            st.link(nc.vector.tensor_tensor(out, X, by_col(s1), ALU.mult))


def weights_quantised(nc, g, w_attn, w_proj):
    with ExitStack() as c:
        wa = c.enter_context(nc.sbuf_tensor("wa_f", [P, EC, 3 * E], F32))
        wp = c.enter_context(nc.sbuf_tensor("wp_f", [P, EC, E], F32))
        sa = c.enter_context(nc.sbuf_tensor("wa_s", [P, EC], F32))
        sp_ = c.enter_context(nc.sbuf_tensor("wp_s", [P, EC], F32))
        w_in = g.sem("w_in")
        with nc.Block() as block:
            @block.sync
            def _(sp):
                sp.dma_start(wa[:], w_attn.rearrange("(c p) n -> p c n", p=P)).then_inc(w_in, 16)
                sp.dma_start(wp[:], w_proj.rearrange("(c p) n -> p c n", p=P)).then_inc(w_in, 16)
                sp.wait_ge(w_in, 32)
        quantise(nc, g, wa[:], g.WA[:], EC, 3 * E, sa[:], True, "wa_")
        quantise(nc, g, wp[:], g.WP[:], EC, E, sp_[:], True, "wp_")


def qkv_quantised(nc, g, XQ, xs, b_attn):
    with ExitStack() as c:
        sb = lambda n, s, d=F32: c.enter_context(nc.sbuf_tensor(n, s, d))
        sem = lambda n: g.sem(n)
        bias = sb("bias_a", [P, 3 * E])
        xT = sb("xT", [P, 2, EC, P], BF16)
        R = sb("R", [P, TB, 3 * E])
        col = sb("r_col", [P, 3 * E])
        colb = sb("r_colb", [P, 3 * E])
        tmpc = sb("r_tmpc", [P, 3 * E])
        cs = sb("r_cs", [P, 3 * E])
        ci = sb("r_ci", [P, 3 * E])
        rmax = sb("r_rmax", [P, TB, 3 * HEADS])
        tmpr = sb("r_tmpr", [P, TB, 3 * HEADS])
        rs = sb("r_rs", [P, TB, 3 * HEADS])
        ri = sb("r_ri", [P, TB, 3 * HEADS])
        QP = sb("QP", [P, TB, HEADS, STRIP], BF16)
        KP = sb("KP", [P, TB, HEADS, STRIP], BF16)
        turned = sb("turned", [P, 2, HG, S], BF16)
        bias_in, x_turned, xT_ready, qkv_done, r_ready, r_used = (sem(n) for n in (
            "bias_in", "x_turned", "xT_ready", "qkv_done", "r_ready", "r_used"))
        chain, pads_made, col_ready, col_all, scaled, rounded, strips_ready = (sem(n) for n in (
            "qkv_chain", "pads_made", "qkv_col_ready", "qkv_col_all", "scaled", "rounded", "strips_ready"))
        strip_turned, strip_copied, act_chain = (sem(n) for n in ("strip_turned", "strip_copied", "act_chain"))
        stored = [sem("stored0"), sem("stored1")]
        waited = g.sem("col_waited")
        block = c.enter_context(nc.Block())
        heads = lambda a: a.rearrange("p t (h d) -> p t h d", d=HD)
        LINKS = 22
        R4 = R[:].rearrange("p t (x h d) -> p t x h d", x=3, d=HD)
        rm, riv, rsv, tmv = (a[:].rearrange("p t (x h) -> p t x h", x=3) for a in (rmax, ri, rs, tmpr))
        by_head = lambda a: a.unsqueeze(3).broadcast_to([P, TB, HEADS, HD])
        bank = lambda n: g.PS[:, n, :].bitcast(BF16)

        @block.sync
        def _(sp):
            sp.dma_start(bias[:], row(b_attn)).then_inc(bias_in, 16)
            with sp.Fori(0, B) as b:
                for s, dst in enumerate((g.QT, g.KT)):
                    sp.wait_ge(strip_copied, b * 8 + 4 * s + 4)
                    sp.dma_start(dst[bass.ds(b * HG, HG), :, :].rearrange("g p c -> p g c"),
                                 turned[:, s]).then_inc(stored[s], 16)
            for s in range(2):
                sp.wait_ge(stored[s], 16 * B)

        @block.gpsimd
        def _(pool):
            nc.gpsimd.memset(QP[:], 0.0).then_inc(pads_made, 1)
            nc.gpsimd.memset(KP[:], 0.0).then_inc(pads_made, 1)
            pool.wait_ge(pads_made, 2)
            nc.gpsimd.memset(QP[:, :, :, HD + 3:HD + 6], 1.0).then_inc(pads_made, 1)
            nc.gpsimd.memset(KP[:, :, :, HD:HD + 3], 1.0).then_inc(pads_made, 1)
            with pool.Fori(0, B) as b:
                pool.wait_ge(col_ready, b + 1)
                pool.sem_inc(waited, 1)
                nc.gpsimd.partition_all_reduce(colb[:], col[:], P, ABSMAX).then_inc(col_all, 1)

        @block.tensor
        def _(pe):
            with pe.Fori(0, B) as b:
                for t in range(TB):
                    if t >= 2:
                        pe.wait_ge(xT_ready, b * TB + t - 1)
                    for e in range(EC):
                        last = nc.tensor.transpose(bank(t % 2)[:, e * P:(e + 1) * P],
                                                   XQ[:, bass.ds(b * TB + t, 1), e * P:(e + 1) * P].rearrange(
                                                       "p a c -> p (a c)"), g.ident[:])
                    last.then_inc(x_turned, 1)
                    pe.wait_ge(xT_ready, b * TB + t + 1)
                    if t >= 2:
                        pe.wait_ge(r_ready, b * TB + t - 1)
                    for e in range(EC):
                        for n, (lo, hi) in enumerate(((0, 512), (512, 768))):
                            last = nc.tensor.matmul(g.PS[:, 2 + 2 * (t % 2) + n, 0:hi - lo], xT[:, t % 2, e, :],
                                                    g.WA[:, e, lo:hi], start=(e == 0), stop=(e == EC - 1))
                    last.then_inc(qkv_done, 1)
                pe.wait_ge(strips_ready, b * 2 + 2)
                for s, strips in enumerate((QP, KP)):
                    for hg in range(HG):
                        n = 4 * s + hg
                        if n >= 2:
                            pe.wait_ge(strip_copied, b * 8 + n - 1)
                        for t in range(TB):
                            last = nc.tensor.transpose(bank(6 + n % 2)[:, t * P:(t + 1) * P],
                                                       strips[:, t, hg * HG:(hg + 1) * HG, :].rearrange(
                                                           "p h d -> p (h d)"), g.ident[:])
                        last.then_inc(strip_turned, 1)
                pe.wait_ge(strip_copied, b * 8 + 8)
                pe.wait_ge(r_ready, b * TB + TB)

        @block.scalar
        def _(act):
            with act.Fori(0, B) as b:
                for t in range(TB):
                    act.wait_ge(x_turned, b * TB + t + 1)
                    if t >= 2:
                        act.wait_ge(qkv_done, b * TB + t - 1)
                    nc.scalar.activation(xT[:, t % 2].rearrange("p c n -> p (c n)"), bank(t % 2)[:, 0:EC * P],
                                         ACT.Copy).then_inc(xT_ready, 1)
                act.wait_ge(scaled, b + 1)
                nc.scalar.activation(R[:], R[:], ACT.Copy, scale=128.0, bias=ROUND).then_inc(act_chain, 1)
                act.wait_ge(act_chain, b + 1)
                nc.scalar.activation(R[:], R[:], ACT.Copy, bias=-ROUND).then_inc(rounded, 1)
                for s in range(2):
                    if s == 0:
                        act.wait_ge(r_ready, b * TB + TB)
                    for hg in range(HG):
                        act.wait_ge(strip_turned, b * 8 + 4 * s + hg + 1)
                        nc.scalar.activation(turned[:, s, hg, :], bank(6 + hg % 2)[:, 0:S],
                                             ACT.Copy).then_inc(strip_copied, 1)
                for s in range(2):
                    act.wait_ge(stored[s], b * 16 + 16)

        @block.vector
        def _(dve):
            dve.wait_ge(bias_in, 16)
            dve.wait_ge(pads_made, 4)
            with dve.Fori(0, B) as b:
                st = Steps(dve, chain, b, LINKS)
                for t in range(TB):
                    dve.wait_ge(qkv_done, b * TB + t + 1)
                    nc.vector.scalar_tensor_tensor(
                        out=R[:, t, :], in0=g.PS[:, 2 + 2 * (t % 2):4 + 2 * (t % 2), :].rearrange(
                            "p a c -> p (a c)")[:, 0:3 * E],
                        scalar=xs[:, bass.ds(b * TB + t, 1)], in1=bias[:], op0=ALU.mult, op1=ALU.add).then_inc(r_ready, 1)
                dve.wait_ge(r_ready, b * TB + TB)
                st.link(nc.vector.tensor_reduce(rm[:, :, 1], R4[:, :, 1], AX, ALU.max, apply_absolute_value=True))
                pow2_up(nc, st, rsv[:, :, 1], riv[:, :, 1], rm[:, :, 1], EPS_Q, tmv[:, :, 1])
                st.link(nc.vector.tensor_tensor(R4[:, :, 1], R4[:, :, 1], by_head(riv[:, :, 1]), ALU.mult))
                nc.vector.tensor_reduce(col[:], R[:].rearrange("p t n -> p n t"), AX, ALU.max,
                                        apply_absolute_value=True).then_inc(col_ready, 1)
                dve.wait_ge(col_all, b + 1)
                pow2_up(nc, st, cs[:], ci[:], colb[:], EPS_Q, tmpc[:])
                st.link(nc.vector.tensor_tensor(R[:], R[:], ci[:].unsqueeze(1).broadcast_to([P, TB, 3 * E]), ALU.mult))
                for x in (0, 2):
                    st.link(nc.vector.tensor_reduce(rm[:, :, x], R4[:, :, x], AX, ALU.max, apply_absolute_value=True))
                pow2_up(nc, st, rsv[:, :, 0::2], riv[:, :, 0::2], rm[:, :, 0::2], EPS_Q, tmv[:, :, 0::2])
                for x in (0, 2):
                    st.link(nc.vector.tensor_tensor(R4[:, :, x], R4[:, :, x], by_head(riv[:, :, x]), ALU.mult))
                st.link(nc.vector.tensor_single_scalar(rs[:], rs[:], 1.0 / 128, ALU.mult))
                nc.vector.tensor_single_scalar(rsv[:, :, 0], rsv[:, :, 0], HD ** -0.5, ALU.mult).then_inc(scaled, 1)
                dve.wait_ge(rounded, b + 1)
                for t in range(TB):
                    last = nc.vector.scalar_tensor_tensor(out=R[:, t], in0=R[:, t], scalar=127.0, in1=cs[:],
                                                          op0=ALU.min, op1=ALU.mult)
                st.link(last)
                dve.wait_ge(scaled, b + 1)
                nc.vector.tensor_tensor(QP[:, :, :, 0:HD], R4[:, :, 0], by_head(rsv[:, :, 0]), ALU.mult).then_inc(strips_ready, 1)
                nc.vector.tensor_tensor(KP[:, :, :, 0:HD], R4[:, :, 1], by_head(rsv[:, :, 1]), ALU.mult).then_inc(strips_ready, 1)
                st.link(nc.vector.tensor_tensor(g.V[:, bass.ds(b * TB, TB), :].rearrange("p t (h d) -> p t h d", d=HD),
                                                R4[:, :, 2], by_head(rsv[:, :, 2]), ALU.mult))
                dve.wait_ge(strip_turned, b * 8 + 8)
                st.close()


GRID = 1.5 * 2.0 ** 16


def load_groups(sp, g, qk, loaded, ready, tiles):
    for hg in range(2):
        sp.dma_start(qk[:, hg, 0], g.QT[hg]).then_inc(loaded[hg], 16)
        sp.dma_start(qk[:, hg, 1], g.KT[hg]).then_inc(loaded[hg], 16)
    with sp.Fori(0, NG // 2 - 1) as n:
        for half in range(2):
            sp.wait_ge(ready, (n * 2 + half + 1) * tiles)
            for s, src in enumerate((g.QT, g.KT)):
                sp.dma_start(qk[:, half, s], src[bass.ds(n * 2 + half + 2, 1), :, :].rearrange("g p c -> p (g c)")
                             ).then_inc(loaded[half], 16)


def scores(nc, g, qk, half, t, by_query, heads, bank0):
    own, other = (0, 1) if by_query else (1, 0)
    lo, hi = (0, (t + 1) * P) if by_query else (t * P, S)
    for n, h in enumerate(heads):
        strip = slice(STRIP * h, STRIP * (h + 1))
        nc.tensor.matmul(g.PS[:, bank0 + n, 0:hi - lo], qk[strip, half, own, t * P:(t + 1) * P],
                         qk[strip, half, other, lo:hi], start=True, stop=False, skip_group_check=True)
    diag = hi - lo - P if by_query else 0
    for n, h in enumerate(heads):
        last = nc.tensor.matmul(g.PS[:, bank0 + n, diag:diag + P], g.ident[:],
                                g.mask_q[:] if by_query else g.mask_k[:], start=False, stop=True, skip_group_check=True)
    return last


def width(t, by_query):
    return (t + 1) * P if by_query else S - t * P


def score_maxima(nc, g, out, by_query, sums, tag):
    with ExitStack() as c:
        qk = c.enter_context(nc.sbuf_tensor(tag + "qk", [P, 2, 2, S], BF16))
        sem = lambda n: g.sem(tag + n)
        loaded = [sem("loaded0"), sem("loaded1")]
        ready, maxed, free = sem("ready"), sem("maxed"), sem("free")
        block = c.enter_context(nc.Block())

        @block.sync
        def _(sp):
            load_groups(sp, g, qk, loaded, ready, TB)

        @block.tensor
        def _(pe):
            with pe.Fori(0, B) as b:
                for hg in range(HG):
                    pe.wait_ge(loaded[hg % 2], b * 64 + 32 * (hg // 2) + 32)
                    for t in range(TB):
                        unit = b * TB * HG + hg * TB + t
                        pe.wait_ge(free, unit + 1)
                        scores(nc, g, qk, hg % 2, t, by_query, range(HG), 4 * (t % 2)).then_inc(ready, 1)

        @block.vector
        def _(dve):
            if sums is None:
                dve.sem_inc(free, 2)
            with dve.Fori(0, B) as b:
                for hg in range(HG):
                    for t in range(TB):
                        dve.wait_ge(ready, b * TB * HG + hg * TB + t + 1)
                        nc.vector.tensor_reduce(
                            out[:, t, bass.ds(b * HG + hg, 1), :].rearrange("p g h -> p (g h)"),
                            g.PS[:, 4 * (t % 2):4 * (t % 2) + 4, 0:width(t, by_query)], AX, ALU.max,
                            negate=sums is not None).then_inc(free if sums is None else maxed, 1)

        if sums is not None:
            @block.scalar
            def _(act):
                nc.scalar.preload_act_table(ACT.Exp)
                act.sem_inc(free, 2)
                with act.Fori(0, B) as b:
                    for hg in range(HG):
                        for t in range(TB):
                            act.wait_ge(maxed, b * TB * HG + hg * TB + t + 1)
                            for h in range(HG):
                                at = lambda a: a[:, t, bass.ds(b * HG + hg, 1), h:h + 1].rearrange("p g h -> p (g h)")
                                w = width(t, by_query)
                                bank = g.PS[:, 4 * (t % 2) + h, 0:w]
                                last = nc.scalar.activation(bank, bank, ACT.Exp, bias=at(out), accum_out=at(sums))
                            last.then_inc(free, 1)


def row_terms(nc, g, term, dst, first, tag):
    with ExitStack() as c:
        part = c.enter_context(nc.sbuf_tensor(tag + "part", [P, 3, TB, NG * HG], BF16))
        rest = c.enter_context(nc.sbuf_tensor(tag + "rest", [P, TB, NG * HG], F32))
        across = c.enter_context(nc.sbuf_tensor(tag + "across", [P, 3, S], BF16))
        sem = lambda n: g.sem(tag + n)
        chain, parted, turned, copied, stored = (sem(n) for n in ("chain", "parted", "turned", "copied", "stored"))
        block = c.enter_context(nc.Block())

        @block.vector
        def _(dve):
            st = Steps(dve, chain)
            whole = term.rearrange("p t g h -> p t (g h)")
            left = whole
            for j in range(3):
                nc.vector.tensor_copy(part[:, j], left).then_inc(parted, 1)
                dve.wait_ge(parted, j + 1)
                if j < 2:
                    st.link(nc.vector.tensor_tensor(rest[:], left, part[:, j], ALU.subtract))
                    left = rest[:]

        @block.tensor
        def _(pe):
            for j in range(3):
                pe.wait_ge(parted, j + 1)
                for t in range(TB):
                    last = nc.tensor.transpose(g.PS[:, j, :].bitcast(BF16)[:, t * P:(t + 1) * P], part[:, j, t], g.ident[:])
                last.then_inc(turned, 1)

        @block.scalar
        def _(act):
            for j in range(3):
                act.wait_ge(turned, j + 1)
                nc.scalar.activation(across[:, j], g.PS[:, j, :].bitcast(BF16)[:, 0:S], ACT.Copy).then_inc(copied, 1)

        @block.sync
        def _(sp):
            for j in range(3):
                sp.wait_ge(copied, j + 1)
                sp.dma_start(dst.rearrange("g (h r) c -> (g h) r c", r=STRIP)[:, first + j, :],
                             across[:, j]).then_inc(stored, 16)
            sp.wait_ge(stored, 48)


def log_sums(nc, g, lse, neg_max, sums):
    ln_ready = g.sem("ln_ready")
    with nc.sbuf_tensor("lns", [P, TB, NG, HG], F32) as lns, nc.Block() as block:
        @block.scalar
        def _(act):
            nc.scalar.activation(lns[:], sums, ACT.Ln).then_inc(ln_ready, 1)

        @block.vector
        def _(dve):
            dve.wait_ge(ln_ready, 1)
            nc.vector.tensor_tensor(lse, neg_max, lns[:], ALU.subtract)


def log_scales(nc, g, scale, neg_ln, logs, extra, tag):
    with ExitStack() as c:
        tmp = c.enter_context(nc.sbuf_tensor(tag + "tmp", [P, TB, NG, HG], F32))
        sem = lambda n: g.sem(tag + n)
        chain, exp_ready, scale_ready, ln_ready = (sem(n) for n in ("chain", "exp_ready", "scale_ready", "ln_ready"))
        block = c.enter_context(nc.Block())

        @block.scalar
        def _(act):
            nc.scalar.activation(scale, logs, ACT.Exp).then_inc(exp_ready, 1)
            act.wait_ge(scale_ready, 1)
            nc.scalar.activation(neg_ln, scale, ACT.Ln).then_inc(ln_ready, 1)

        @block.vector
        def _(dve):
            st = Steps(dve, chain)
            dve.wait_ge(exp_ready, 1)
            st.link(nc.vector.tensor_scalar(tmp[:], scale, EPS_Q, SLACK, ALU.max, ALU.mult))
            st.link(nc.vector.tensor_single_scalar(tmp[:].bitcast(I32), tmp[:].bitcast(I32), -(1 << 23), ALU.bitwise_and))
            nc.vector.tensor_single_scalar(scale, tmp[:], 2.0, ALU.mult).then_inc(scale_ready, 1)
            dve.wait_ge(ln_ready, 1)
            if extra is None:
                nc.vector.tensor_single_scalar(neg_ln, neg_ln, -1.0, ALU.mult)
            else:
                nc.vector.scalar_tensor_tensor(out=neg_ln, in0=neg_ln, scalar=-1.0, in1=extra, op0=ALU.mult, op1=ALU.add)


def scale_values(nc, g, s1):
    with nc.Block() as block:
        @block.vector
        def _(dve):
            for b in range(B):
                for t in range(TB):
                    v = g.V[:, b * TB + t, :].rearrange("p (h d) -> p h d", d=HD)
                    s = s1[:, t, b * HG:(b + 1) * HG, :].rearrange("p g h -> p (g h)").unsqueeze(2).broadcast_to([P, HEADS, HD])
                    nc.vector.tensor_tensor(v, v, s, ALU.mult)


def weighted_values(nc, g, O, s2):
    with ExitStack() as c:
        qk = c.enter_context(nc.sbuf_tensor("d_qk", [P, 2, 2, S], BF16))
        probs = c.enter_context(nc.sbuf_tensor("probs", [P, 3, 2, S], F32))
        steps = c.enter_context(nc.sbuf_tensor("steps", [P, 2, TB, HG, S], BF16))
        sem = lambda n: g.sem("d_" + n)
        loaded = [sem("loaded0"), sem("loaded1")]
        ready, exped, rounded, clipped, summed, read = (sem(n) for n in (
            "ready", "exped", "rounded", "clipped", "summed", "read"))
        block = c.enter_context(nc.Block())
        PER = HG * TB * 2
        prev = lambda u: u - 3 if u >= 3 else (-2, -1, -2)[u]

        @block.sync
        def _(sp):
            load_groups(sp, g, qk, loaded, ready, 2 * TB)

        @block.tensor
        def _(pe):
            def sum_up(b, hg):
                pe.wait_ge(clipped, (b * HG + hg + 1) * TB)
                pe.wait_ge(read, b * HG + hg + 1)
                for q in range(TB):
                    for h in range(HG):
                        for k in range(q + 1):
                            last = nc.tensor.matmul(
                                g.PS[:, 6 + hg % 2, (q * HG + h) * HD:(q * HG + h + 1) * HD],
                                steps[:, hg % 2, k, h, (q - k) * P:(q - k + 1) * P],
                                g.V[:, bass.ds(b * TB + k, 1), (hg * HG + h) * HD:(hg * HG + h + 1) * HD].rearrange(
                                    "p a c -> p (a c)"), start=(k == 0), stop=(k == q))
                last.then_inc(summed, 1)

            pe.sem_inc(summed, 2)
            with pe.Fori(0, B) as b:
                for hg in range(HG):
                    pe.wait_ge(loaded[hg % 2], b * 64 + 32 * (hg // 2) + 32)
                    for t in range(TB):
                        for n in range(2):
                            u = (hg * TB + t) * 2 + n
                            pe.wait_ge(exped, b * PER + prev(u) + 3)
                            scores(nc, g, qk, hg % 2, t, False, (2 * n, 2 * n + 1), 2 * (u % 3)).then_inc(ready, 1)
                    if hg > 0:
                        sum_up(b, hg - 1)
                sum_up(b, HG - 1)

        @block.scalar
        def _(act):
            nc.scalar.preload_act_table(ACT.Exp)
            act.sem_inc(exped, 2)
            with act.Fori(0, B) as b:
                for u in range(PER):
                    w = width(u // 2 % TB, False)
                    act.wait_ge(ready, b * PER + u + 1)
                    act.wait_ge(rounded, b * PER + prev(u) + 3)
                    nc.scalar.activation(probs[:, u % 3, :, 0:w], g.PS[:, 2 * (u % 3):2 * (u % 3) + 2, 0:w],
                                         ACT.Exp).then_inc(exped, 1)

        @block.vector
        def _(dve):
            def read_out(b, hg):
                at = b * HG + hg
                dve.wait_ge(summed, at + 3)
                tiles = [P, TB, HG, HD]
                nc.vector.tensor_tensor(
                    O[:, bass.ds(b * TB, TB), hg * HG * HD:(hg + 1) * HG * HD].rearrange("p t (h d) -> p t h d", d=HD),
                    g.PS[:, 6 + hg % 2, 0:TB * HG * HD].rearrange("p (t h d) -> p t h d", h=HG, d=HD),
                    s2[:, :, bass.ds(at, 1), :].rearrange("p t g h -> p t (g h)").unsqueeze(3).broadcast_to(tiles),
                    ALU.mult).then_inc(read, 1)

            dve.sem_inc(rounded, 2)
            dve.sem_inc(read, 2)
            with dve.Fori(0, B) as b:
                for hg in range(HG):
                    dve.wait_ge(summed, b * HG + hg + 1)
                    for t in range(TB):
                        w = width(t, False)
                        for n in range(2):
                            u = (hg * TB + t) * 2 + n
                            dve.wait_ge(exped, b * PER + u + 3)
                            nc.vector.tensor_scalar(steps[:, hg % 2, t, 2 * n:2 * n + 2, 0:w], probs[:, u % 3, :, 0:w],
                                                    GRID, GRID, ALU.add, ALU.subtract).then_inc(rounded, 1)
                        dve.wait_ge(rounded, b * PER + u + 3)
                        nc.vector.tensor_single_scalar(steps[:, hg % 2, t, :, 0:w], steps[:, hg % 2, t, :, 0:w],
                                                       127.0 / 128, ALU.min).then_inc(clipped, 1)
                    if hg > 0:
                        read_out(b, hg - 1)
                read_out(b, HG - 1)


HIDDEN = 768
HC = HIDDEN // P
FFN_SCALE = 1.0 / 127.0
EXPERTS, EH = 32, 64
PAIRS = EXPERTS * EH // P
TOPK = 8
GONE = -3e38


def projection(nc, g, OQ, os, b_proj):
    with ExitStack() as c:
        bias = c.enter_context(nc.sbuf_tensor("bias_p", [P, E], F32))
        oT = c.enter_context(nc.sbuf_tensor("oT", [P, 2, EC, P], BF16))
        sem = lambda n: g.sem("p_" + n)
        bias_in, biased, turned, copied, done, read = (sem(n) for n in (
            "bias_in", "biased", "turned", "copied", "done", "read"))
        block = c.enter_context(nc.Block())

        @block.sync
        def _(sp):
            sp.dma_start(bias[:], row(b_proj)).then_inc(bias_in, 16)

        @block.gpsimd
        def _(pool):
            pool.wait_ge(bias_in, 16)
            nc.gpsimd.tensor_tensor(g.H[:], g.H[:], bias[:].unsqueeze(1).broadcast_to([P, T, E]), ALU.add).then_inc(biased, 1)

        @block.tensor
        def _(pe):
            with pe.Fori(0, B) as b:
                for t in range(TB):
                    at = b * TB + t
                    pe.wait_ge(copied, at + 1)
                    for e in range(EC):
                        last = nc.tensor.transpose(g.PS[:, t % 2, :].bitcast(BF16)[:, e * P:(e + 1) * P],
                                                   OQ[:, bass.ds(at, 1), e * P:(e + 1) * P].rearrange("p a c -> p (a c)"),
                                                   g.ident[:])
                    last.then_inc(turned, 1)
                    pe.wait_ge(copied, at + 3)
                    pe.wait_ge(read, at + 1)
                    for e in range(EC):
                        last = nc.tensor.matmul(g.PS[:, 2 + t % 2, 0:E], oT[:, t % 2, e, :], g.WP[:, e, :],
                                                start=(e == 0), stop=(e == EC - 1))
                    last.then_inc(done, 1)

        @block.scalar
        def _(act):
            act.sem_inc(copied, 2)
            with act.Fori(0, B) as b:
                for t in range(TB):
                    at = b * TB + t
                    act.wait_ge(turned, at + 1)
                    act.wait_ge(read, at + 1)
                    nc.scalar.activation(oT[:, t % 2].rearrange("p c n -> p (c n)"),
                                         g.PS[:, t % 2, :].bitcast(BF16)[:, 0:EC * P], ACT.Copy).then_inc(copied, 1)

        @block.vector
        def _(dve):
            dve.sem_inc(read, 2)
            dve.wait_ge(biased, 1)
            with dve.Fori(0, B) as b:
                for t in range(TB):
                    at = b * TB + t
                    dve.wait_ge(done, at + 1)
                    h = g.H[:, bass.ds(at, 1), :].rearrange("p a e -> p (a e)")
                    nc.vector.scalar_tensor_tensor(out=h, in0=g.PS[:, 2 + t % 2, 0:E], scalar=os[:, bass.ds(at, 1)],
                                                   in1=h, op0=ALU.mult, op1=ALU.add).then_inc(read, 1)


def turn_batch(pe, nc, g, Y, bank, turned):
    for e in range(EC):
        for t in range(TB):
            last = nc.tensor.transpose(g.PS[:, bank + e, t * P:(t + 1) * P], Y[:, t, e * P:(e + 1) * P], g.identf[:])
        last.then_inc(turned, 1)


def feed_forward(nc, g, w_gateT, w_upT, w_downT):
    with ExitStack() as c:
        sb = lambda n, s, d=F32: c.enter_context(nc.sbuf_tensor("f_" + n, s, d))
        raw = sb("raw", [P, 2 * EC * HIDDEN + HC * E], I32)
        w = sb("w", [P, 2 * EC * HIDDEN + HC * E])
        wg, wu = (w[:, n * EC * HIDDEN:(n + 1) * EC * HIDDEN].rearrange("p (c n) -> p c n", c=EC) for n in range(2))
        wd = w[:, 2 * EC * HIDDEN:].rearrange("p (c n) -> p c n", c=HC)
        Y, yT, hT, gate = sb("Y", [P, TB, E]), sb("yT", [P, EC, S]), sb("hT", [P, HC, S]), sb("gate", [P, 2, S])
        sem = lambda n: g.sem("f_" + n)
        w_in, w_ready, normed, turned, copied, up_done, silu_done, h_ready, down_done, added = (sem(n) for n in (
            "w_in", "w_ready", "normed", "turned", "copied", "up_done", "silu_done", "h_ready", "down_done", "added"))
        block = c.enter_context(nc.Block())

        @block.sync
        def _(sp):
            for n, src in enumerate((w_gateT, w_upT)):
                sp.dma_start(raw[:, n * EC * HIDDEN:(n + 1) * EC * HIDDEN].rearrange("p (c n) -> p c n", c=EC),
                             src.rearrange("(c p) n -> p c n", p=P)).then_inc(w_in, 16)
            sp.dma_start(raw[:, 2 * EC * HIDDEN:].rearrange("p (c n) -> p c n", c=HC),
                         w_downT.rearrange("(c p) n -> p c n", p=P)).then_inc(w_in, 16)

        @block.tensor
        def _(pe):
            pe.wait_ge(w_ready, 1)
            with pe.Fori(0, B) as b:
                pe.wait_ge(normed, b * TB + TB)
                turn_batch(pe, nc, g, Y, 0, turned)
                pe.wait_ge(copied, b * EC + EC)
                for n in range(HC):
                    pe.wait_ge(h_ready, b * HC + n + 1)
                    for x, wx in enumerate((wg, wu)):
                        for e in range(EC):
                            last = nc.tensor.matmul(g.PS[:, 2 + 2 * (n % 2) + x, :], wx[:, e, n * P:(n + 1) * P], yT[:, e],
                                                    start=(e == 0), stop=(e == EC - 1))
                    last.then_inc(up_done, 1)
                pe.wait_ge(h_ready, b * HC + HC + 2)
                for t in range(TB):
                    pe.wait_ge(added, b * TB + t + 1)
                    for n in range(HC):
                        last = nc.tensor.matmul(g.PS[:, 6 + t % 2, 0:E], hT[:, n, t * P:(t + 1) * P], wd[:, n],
                                                start=(n == 0), stop=(n == HC - 1))
                    last.then_inc(down_done, 1)

        @block.scalar
        def _(act):
            nc.scalar.preload_act_table(ACT.Silu)
            with act.Fori(0, B) as b:
                for e in range(EC):
                    act.wait_ge(turned, b * EC + e + 1)
                    nc.scalar.activation(yT[:, e], g.PS[:, e, :], ACT.Copy).then_inc(copied, 1)
                for n in range(HC):
                    act.wait_ge(up_done, b * HC + n + 1)
                    act.wait_ge(h_ready, b * HC + n + 1)
                    nc.scalar.activation(gate[:, n % 2], g.PS[:, 2 + 2 * (n % 2), :], ACT.Silu, scale=FFN_SCALE
                                         ).then_inc(silu_done, 1)

        @block.vector
        def _(dve):
            dve.sem_inc(h_ready, 2)
            dve.sem_inc(added, 2)
            dve.wait_ge(w_in, 48)
            nc.vector.tensor_copy(w[:], raw[:]).then_inc(w_ready, 1)
            with dve.Fori(0, B) as b:
                for t in range(TB):
                    normalise(nc, g, Y[:, t], b * TB + t).then_inc(normed, 1)
                for n in range(HC):
                    dve.wait_ge(silu_done, b * HC + n + 1)
                    nc.vector.scalar_tensor_tensor(out=hT[:, n], in0=g.PS[:, 3 + 2 * (n % 2), :], scalar=FFN_SCALE,
                                                   in1=gate[:, n % 2], op0=ALU.mult, op1=ALU.mult).then_inc(h_ready, 1)
                for t in range(TB):
                    at = b * TB + t
                    dve.wait_ge(down_done, at + 1)
                    h = g.H[:, bass.ds(at, 1), :].rearrange("p a e -> p (a e)")
                    nc.vector.scalar_tensor_tensor(out=h, in0=g.PS[:, 6 + t % 2, 0:E], scalar=FFN_SCALE, in1=h,
                                                   op0=ALU.mult, op1=ALU.add).then_inc(added, 1)


def sparse_attention(nc, g, Wq, bq, Wk, bk, Wv, bv, Wo, bo):
    with ExitStack() as c:
        sb = lambda n, s, d=F32: c.enter_context(nc.sbuf_tensor("t_" + n, s, d))
        W = sb("W", [P, 4, EC, E])
        bqk, bvo = sb("bqk", [P, 2, EC]), sb("bvo", [P, 2, E])
        mask = sb("mask", [P, S])
        Y, yT, qkT, V1 = sb("Y", [P, TB, E]), sb("yT", [P, EC, S]), sb("qkT", [P, 2, EC, S]), sb("V1", [P, TB, E])
        sc, left, ex, pr = sb("sc", [P, S]), sb("left", [P, S]), sb("ex", [P, 2, S]), sb("pr", [P, 2, S])
        top, ntop, total, rec = sb("top", [P, TOPK]), sb("ntop", [P, 2]), sb("total", [P, TB]), sb("rec", [P, TB])
        pT, avT = sb("pT", [P, TB, S]), sb("avT", [P, EC, S])
        sem = lambda n: g.sem("t_" + n)
        w_in, masked, normed, biased, turned, copied, qk_done, qk_ready, v_done, v_ready = (sem(n) for n in (
            "w_in", "masked", "normed", "biased", "turned", "copied", "qk_done", "qk_ready", "v_done", "v_ready"))
        s_done, s_ready, top_ready, exped, p_ready, p_turned, p_copied, av_done, av_ready, o_done, added, chain, norm_ready = (
            sem(n) for n in ("s_done", "s_ready", "top_ready", "exped", "p_ready", "p_turned", "p_copied", "av_done",
                             "av_ready", "o_done", "added", "chain", "norm_ready"))
        waited = g.sem("t_waited")
        block = c.enter_context(nc.Block())
        LINKS = 2 * TB + 1

        @block.sync
        def _(sp):
            for n, src in enumerate((Wq, Wk, Wv, Wo)):
                sp.dma_start(W[:, n], src.rearrange("(c p) n -> p c n", p=P)).then_inc(w_in, 16)
            for n, src in enumerate((bq, bk)):
                sp.dma_start(bqk[:, n, :], src).then_inc(w_in, 16)
            for n, src in enumerate((bv, bo)):
                sp.dma_start(bvo[:, n, :], row(src)).then_inc(w_in, 16)

        @block.gpsimd
        def _(pool):
            st = Steps(pool, masked)
            st.link(nc.gpsimd.memset(mask[:], 0.0))
            st.link(nc.gpsimd.affine_select(out=mask[:, S - P:], in_=mask[:, S - P:], compare_op=ALU.is_ge, fill=NEG,
                                            base=0, pattern=[[-1, P]], channel_multiplier=1))
            pool.wait_ge(w_in, 16 * 8)
            with pool.Fori(0, B) as b:
                pool.wait_ge(normed, b * TB + TB)
                h = g.H[:, bass.ds(b * TB, TB), :]
                nc.gpsimd.tensor_tensor(h, h, bvo[:, 1].unsqueeze(1).broadcast_to([P, TB, E]), ALU.add).then_inc(biased, 1)

        @block.tensor
        def _(pe):
            pe.sem_inc(p_turned, 2)
            pe.wait_ge(w_in, 16 * 8)
            with pe.Fori(0, B) as b:
                pe.wait_ge(normed, b * TB + TB)
                turn_batch(pe, nc, g, Y, 0, turned)
                pe.wait_ge(copied, b * EC + EC)
                for x in range(2):
                    for d in range(EC):
                        for e in range(EC):
                            last = nc.tensor.matmul(g.PS[:, 2 + 2 * x + d, :], W[:, x, e, d * P:(d + 1) * P], yT[:, e],
                                                    start=(e == 0), stop=(e == EC - 1))
                        last.then_inc(qk_done, 1)
                for t in range(TB):
                    pe.wait_ge(v_ready, b * TB + t + 1)
                    for e in range(EC):
                        last = nc.tensor.matmul(g.PS[:, 6 + t % 2, 0:E], yT[:, e, t * P:(t + 1) * P], W[:, 2, e],
                                                start=(e == 0), stop=(e == EC - 1))
                    last.then_inc(v_done, 1)
                pe.wait_ge(qk_ready, b * 4 + 4)

                def turn_probs(t):
                    pe.wait_ge(p_ready, b * TB + t + 1)
                    pe.wait_ge(p_copied, b * TB + t + 1)
                    for k in range(t + 1):
                        last = nc.tensor.transpose(g.PS[:, 4 + t % 2, k * P:(k + 1) * P], pr[:, t % 2, k * P:(k + 1) * P],
                                                   g.identf[:])
                    last.then_inc(p_turned, 1)

                for t in range(TB):
                    w = (t + 1) * P
                    pe.wait_ge(s_ready, b * TB + t + 1)
                    for d in range(EC):
                        last = nc.tensor.matmul(g.PS[:, 2 + t % 2, 0:w], qkT[:, 0, d, t * P:w], qkT[:, 1, d, 0:w],
                                                start=(d == 0), stop=(d == EC - 1))
                    last.then_inc(s_done, 1)
                    if t:
                        turn_probs(t - 1)
                turn_probs(TB - 1)
                pe.wait_ge(p_copied, b * TB + TB + 2)
                pe.wait_ge(v_ready, b * TB + TB + 2)
                for d in range(EC):
                    for k in range(TB):
                        last = nc.tensor.matmul(g.PS[:, d, k * P:S], V1[:, k, d * P:(d + 1) * P], pT[:, k, k * P:S],
                                                start=(k == 0), stop=(k == TB - 1))
                    last.then_inc(av_done, 1)
                pe.wait_ge(av_ready, b * EC + EC)
                for t in range(TB):
                    pe.wait_ge(added, b * TB + t + 1)
                    for d in range(EC):
                        last = nc.tensor.matmul(g.PS[:, 6 + t % 2, 0:E], avT[:, d, t * P:(t + 1) * P], W[:, 3, d],
                                                start=(d == 0), stop=(d == EC - 1))
                    last.then_inc(o_done, 1)

        @block.scalar
        def _(act):
            nc.scalar.preload_act_table(ACT.Exp)
            act.sem_inc(p_copied, 2)
            act.wait_ge(w_in, 16 * 8)
            with act.Fori(0, B) as b:
                for e in range(EC):
                    act.wait_ge(turned, b * EC + e + 1)
                    nc.scalar.activation(yT[:, e], g.PS[:, e, :], ACT.Copy).then_inc(copied, 1)
                for x in range(2):
                    for d in range(EC):
                        act.wait_ge(qk_done, b * 4 + 2 * x + d + 1)
                        nc.scalar.activation(qkT[:, x, d], g.PS[:, 2 + 2 * x + d, :], ACT.Identity,
                                             bias=bqk[:, x, d:d + 1]).then_inc(qk_ready, 1)

                def copy_probs(t):
                    act.wait_ge(p_turned, b * TB + t + 3)
                    nc.scalar.activation(pT[:, 0:t + 1, t * P:(t + 1) * P],
                                         g.PS[:, 4 + t % 2, 0:(t + 1) * P].rearrange("p (k q) -> p k q", q=P),
                                         ACT.Copy).then_inc(p_copied, 1)

                for t in range(TB):
                    w = (t + 1) * P
                    act.wait_ge(top_ready, b * TB + t + 1)
                    nc.scalar.activation(ex[:, t % 2, 0:w], sc[:, 0:w], ACT.Exp, bias=ntop[:, t % 2:t % 2 + 1]).then_inc(exped, 1)
                    if t:
                        copy_probs(t - 1)
                copy_probs(TB - 1)
                for d in range(EC):
                    act.wait_ge(av_done, b * EC + d + 1)
                    nc.scalar.activation(avT[:, d], g.PS[:, d, :], ACT.Copy).then_inc(av_ready, 1)

        @block.vector
        def _(dve):
            for s in (v_ready, s_ready, added):
                dve.sem_inc(s, 2)
            dve.wait_ge(w_in, 16 * 8)
            dve.wait_ge(masked, 2)
            with dve.Fori(0, B) as b:
                st = Steps(dve, chain, b, LINKS)
                for t in range(TB):
                    normalise(nc, g, Y[:, t], b * TB + t).then_inc(normed, 1)
                for t in range(TB):
                    dve.wait_ge(v_done, b * TB + t + 1)
                    nc.vector.tensor_tensor(V1[:, t], g.PS[:, 6 + t % 2, 0:E], bvo[:, 0], ALU.add).then_inc(v_ready, 1)
                for t in range(TB):
                    w = (t + 1) * P
                    dve.wait_ge(s_done, b * TB + t + 1)
                    nc.vector.scalar_tensor_tensor(out=sc[:, 0:w], in0=g.PS[:, 2 + t % 2, 0:w], scalar=E ** -0.5,
                                                   in1=mask[:, S - w:], op0=ALU.mult, op1=ALU.add).then_inc(s_ready, 1)
                    dve.wait_ge(s_ready, b * TB + t + 3)
                    dve.sem_inc(waited, 1)
                    st.link(nc.vector.max(out=top[:], in_=sc[:, 0:w]))
                    nc.vector.tensor_single_scalar(ntop[:, t % 2:t % 2 + 1], top[:, 0:1], -1.0, ALU.mult).then_inc(top_ready, 1)
                    st.link(nc.vector.match_replace(out=left[:, 0:w], in_to_replace=top[:], in_values=sc[:, 0:w],
                                                    imm_value=GONE))
                    dve.wait_ge(exped, b * TB + t + 1)
                    dve.wait_ge(p_turned, b * TB + t + 1)
                    nc.vector.scalar_tensor_tensor(out=pr[:, t % 2, 0:w], in0=left[:, 0:w], scalar=GONE / 2, in1=ex[:, t % 2, 0:w],
                                                   op0=ALU.is_lt, op1=ALU.mult, accum_out=total[:, t:t + 1]).then_inc(p_ready, 1)
                dve.wait_ge(p_ready, b * TB + TB)
                st.link(nc.vector.reciprocal(rec[:], total[:]))
                dve.wait_ge(biased, b + 1)
                for t in range(TB):
                    at = b * TB + t
                    dve.wait_ge(o_done, at + 1)
                    h = g.H[:, bass.ds(at, 1), :].rearrange("p a e -> p (a e)")
                    nc.vector.scalar_tensor_tensor(out=h, in0=g.PS[:, 6 + t % 2, 0:E], scalar=rec[:, t:t + 1], in1=h,
                                                   op0=ALU.mult, op1=ALU.add).then_inc(added, 1)


def experts(nc, g, out, router_wT, router_b, W1, b1T, W2, b2):
    with ExitStack() as c:
        sb = lambda n, s, d=F32: c.enter_context(nc.sbuf_tensor("e_" + n, s, d))
        w1, w2 = sb("w1", [P, EC, EXPERTS * EH]), sb("w2", [P, PAIRS, E])
        b1, b2s, rw, rb = sb("b1", [P, PAIRS]), sb("b2", [EXPERTS, E]), sb("rw", [P, EC, EXPERTS]), sb("rb", [P, EXPERTS])
        sel = sb("sel", [EXPERTS, EXPERTS * EH], BF16)
        number = sb("number", [P, EXPERTS], I32)
        numberf = sb("numberf", [P, EXPERTS])
        Y, yT, hT = sb("Y", [P, TB, E]), sb("yT", [P, EC, S]), sb("hT", [P, PAIRS, S])
        logit, best, which = sb("logit", [P, TB, EXPERTS]), sb("best", [P, TB, 8]), sb("which", [P, TB, 8], mybir.dt.uint32)
        whichf, one = sb("whichf", [P, TB]), sb("one", [P, TB, EXPERTS])
        oneT, others = sb("oneT", [EXPERTS, S]), sb("others", [EXPERTS, S], BF16)
        res = sb("res", [P, TB, E])
        sem = lambda n: g.sem("e_" + n)
        w_in, made, number_ready, normed, turned, copied, l_done, one_ready, one_turned, oneT_ready, others_ready = (sem(n) for n in (
            "w_in", "made", "number_ready", "normed", "turned", "copied", "l_done", "one_ready", "one_turned", "oneT_ready", "others_ready"))
        h_done, h_ready, y_done, res_ready, stored, res_gone, chain = (sem(n) for n in (
            "h_done", "h_ready", "y_done", "res_ready", "stored", "res_gone", "chain"))
        waited = g.sem("e_waited")
        block = c.enter_context(nc.Block())
        LINKS = 1 + 3

        @block.sync
        def _(sp):
            for e in range(EC):
                sp.dma_start(w1[:, e].rearrange("p (x h) -> p x h", h=EH),
                             W1.rearrange("x (c p) h -> c p x h", p=P)[e]).then_inc(w_in, 16)
            sp.dma_start(w2[:], W2.rearrange("(j a) h e -> (a h) j e", a=2)).then_inc(w_in, 16)
            sp.dma_start(b1[:], b1T).then_inc(w_in, 16)
            sp.dma_start(b2s[:], b2).then_inc(w_in, 16)
            sp.dma_start(rw[:], router_wT.rearrange("(c p) x -> p c x", p=P)).then_inc(w_in, 16)
            sp.dma_start(rb[:], row(router_b)).then_inc(w_in, 16)
            o = out.rearrange("b (t p) e -> b p t e", p=P)
            sp.sem_inc(res_gone, 1)
            with sp.Fori(0, B) as b:
                sp.wait_ge(res_ready, b * TB + TB + 2)
                sp.dma_start(o[bass.ds(b, 1)].rearrange("b p t e -> p (b t) e"), res[:]).then_inc(stored, 16)
                sp.wait_ge(stored, b * 16 + 16)
                sp.sem_inc(res_gone, 1)

        @block.gpsimd
        def _(pool):
            nc.gpsimd.iota(number[:], pattern=[[1, EXPERTS]], base=0, channel_multiplier=0).then_inc(number_ready, 1)
            st = Steps(pool, made)
            st.link(nc.gpsimd.memset(sel[:], 1.0))
            for base, mult, step in ((0, -EH, 1), (EH - 1, EH, -1)):
                st.link(nc.gpsimd.affine_select(out=sel[:], in_=sel[:], compare_op=ALU.is_ge, fill=0.0, base=base,
                                                pattern=[[step, EXPERTS * EH]], channel_multiplier=mult))

        @block.tensor
        def _(pe):
            pe.wait_ge(w_in, 16 * 7)
            pe.wait_ge(made, 3)
            with pe.Fori(0, B) as b:
                pe.wait_ge(normed, b * TB + TB)
                turn_batch(pe, nc, g, Y, 0, turned)
                pe.wait_ge(copied, b * EC + EC)
                for t in range(TB):
                    for e in range(EC):
                        last = nc.tensor.matmul(g.PS[:, 2, t * EXPERTS:(t + 1) * EXPERTS], yT[:, e, t * P:(t + 1) * P],
                                                rw[:, e], start=(e == 0), stop=(e == EC - 1))
                last.then_inc(l_done, 1)
                pe.wait_ge(one_ready, b + 1)
                for t in range(TB):
                    last = nc.tensor.transpose(g.PS[0:EXPERTS, 3, t * P:(t + 1) * P], one[:, t], g.identf[:])
                last.then_inc(one_turned, 1)
                pe.wait_ge(others_ready, b + 1)
                for j in range(PAIRS):
                    pe.wait_ge(h_ready, b * PAIRS + j + 1)
                    bank = g.PS[:, 4 + j % 2, :]
                    for e in range(EC):
                        nc.tensor.matmul(bank, w1[:, e, j * P:(j + 1) * P], yT[:, e], start=(e == 0), stop=False)
                    nc.tensor.matmul(bank, sel[:, j * P:(j + 1) * P], others[:], start=False, stop=True).then_inc(h_done, 1)
                pe.wait_ge(h_ready, b * PAIRS + PAIRS + 2)
                for t in range(TB):
                    pe.wait_ge(res_ready, b * TB + t + 1)
                    bank = g.PS[:, 6 + t % 2, 0:E]
                    for j in range(PAIRS):
                        nc.tensor.matmul(bank, hT[:, j, t * P:(t + 1) * P], w2[:, j], start=(j == 0), stop=False)
                    nc.tensor.matmul(bank, oneT[:, t * P:(t + 1) * P], b2s[:], start=False, stop=True).then_inc(y_done, 1)

        @block.scalar
        def _(act):
            act.wait_ge(w_in, 16 * 7)
            act.sem_inc(h_ready, 2)
            with act.Fori(0, B) as b:
                for e in range(EC):
                    act.wait_ge(turned, b * EC + e + 1)
                    nc.scalar.activation(yT[:, e], g.PS[:, e, :], ACT.Copy).then_inc(copied, 1)
                act.wait_ge(one_turned, b + 1)
                nc.scalar.activation(oneT[:], g.PS[0:EXPERTS, 3, :], ACT.Copy).then_inc(oneT_ready, 1)
                for j in range(PAIRS):
                    act.wait_ge(h_done, b * PAIRS + j + 1)
                    nc.scalar.activation(hT[:, j], g.PS[:, 4 + j % 2, :], ACT.Relu, bias=b1[:, j:j + 1]).then_inc(h_ready, 1)

        @block.vector
        def _(dve):
            dve.sem_inc(res_ready, 2)
            dve.wait_ge(w_in, 16 * 7)
            dve.wait_ge(number_ready, 1)
            nc.vector.tensor_copy(numberf[:], number[:]).then_inc(chain, 1)
            dve.wait_ge(chain, 1)
            with dve.Fori(0, B) as b:
                st = Steps(dve, chain, b, LINKS, base=1)
                for t in range(TB):
                    normalise(nc, g, Y[:, t], b * TB + t).then_inc(normed, 1)
                dve.wait_ge(l_done, b + 1)
                st.link(nc.vector.tensor_tensor(logit[:], g.PS[:, 2, 0:TB * EXPERTS].rearrange("p (t x) -> p t x", t=TB),
                                                rb[:].unsqueeze(1).broadcast_to([P, TB, EXPERTS]), ALU.add))
                dve.sem_inc(waited, 1)
                for t in range(TB):
                    last = nc.vector.max(out=best[:, t], in_=logit[:, t])
                st.link(last)
                dve.sem_inc(waited, 1)
                for t in range(TB):
                    last = nc.vector.max_index(out=which[:, t], in_max=best[:, t], in_values=logit[:, t])
                st.link(last)
                st.link(nc.vector.tensor_copy(whichf[:], which[:, :, 0]))
                nc.vector.tensor_tensor(one[:], numberf[:].unsqueeze(1).broadcast_to([P, TB, EXPERTS]),
                                        whichf[:].unsqueeze(2).broadcast_to([P, TB, EXPERTS]), ALU.is_equal).then_inc(one_ready, 1)
                dve.wait_ge(oneT_ready, b + 1)
                nc.vector.tensor_scalar(others[:], oneT[:], 1.0, -NEG, ALU.subtract, ALU.mult).then_inc(others_ready, 1)
                for t in range(TB):
                    at = b * TB + t
                    dve.wait_ge(y_done, at + 1)
                    if t == 0:
                        dve.wait_ge(res_gone, b + 1)
                    nc.vector.scalar_tensor_tensor(out=res[:, t], in0=g.PS[:, 6 + t % 2, 0:E], scalar=0.0,
                                                   in1=g.H[:, bass.ds(at, 1), :].rearrange("p a e -> p (a e)"),
                                                   op0=ALU.max, op1=ALU.add).then_inc(res_ready, 1)


class Buffers:

    def __init__(self, nc):
        self.nc, self.sems = nc, []

    def sem(self, name):
        self.sems.append(self.nc.alloc_semaphore(name))
        return self.sems[-1]

    def free_sems(self):
        self.nc.clear_and_free_semaphores(self.sems)
        self.nc.all_engine_barrier()
        self.sems = []
def tower(nc, a, out):
    with ExitStack() as c:
        g=Buffers(nc)
        sb = lambda n, s, d: c.enter_context(nc.sbuf_tensor(n, s, d))
        g.H=sb('H',[P,T,E],F32); g.V=sb('V',[P,T,E],BF16)
        g.ident=sb('ident',[P,P],BF16); g.identf=sb('identf',[P,P],F32); g.mask_q=sb('mask_q',[P,P],BF16); g.mask_k=sb('mask_k',[P,P],BF16)
        g.mean=sb('mean',[P,T],F32); g.rstd=sb('rstd',[P,T],F32)
        g.WA=sb('WA',[P,EC,3*E],BF16); g.WP=sb('WP',[P,EC,E],BF16)
        g.PS=c.enter_context(nc.psum_tensor('PS',[P,8,512],F32))
        g.QT=nc.dram_tensor('QT',(NG,P,S),BF16,kind='Internal').ap()
        g.KT=nc.dram_tensor('KT',(NG,P,S),BF16,kind='Internal').ap()
        constants_and_tokens(nc,g,a['x'],a['L0_tok_weights'])
        with ExitStack() as c2:
            sb2 = lambda n, s, d: c2.enter_context(nc.sbuf_tensor(n, s, d))
            X=sb2('X',[P,T,E],F32); XQ=sb2('XQ',[P,T,E],BF16); xs=sb2('xs',[P,T],F32)
            layernorm(nc,g,X[:],'a_')
            quantise(nc,g,X[:],XQ[:],T,E,xs[:],False,'x_')
            weights_quantised(nc,g,a['L0_attn_w_attn'],a['L0_attn_w_proj'])
            qkv_quantised(nc,g,XQ,xs,a['L0_attn_b_attn'])
        with ExitStack() as c2:
            O=c2.enter_context(nc.sbuf_tensor('O',[P,T,E],F32))
            small = lambda n: c2.enter_context(nc.sbuf_tensor(n, [P,TB,NG,HG], F32))[:]
            neg_max, sums, lse, key_max, key_scale, key_ln, q_max, q_scale, q_ln = (small(n) for n in ('neg_max','sums','lse','key_max','key_scale','key_ln','q_max','q_scale','q_ln'))
            score_maxima(nc,g,neg_max,True,sums,'sa_')
            log_sums(nc,g,lse,neg_max,sums)
            row_terms(nc,g,lse,g.QT,HD,'ra_')
            score_maxima(nc,g,key_max,False,None,'sb_')
            log_scales(nc,g,key_scale,key_ln,key_max,None,'lb_')
            row_terms(nc,g,key_ln,g.KT,HD+3,'rb_')
            scale_values(nc,g,key_scale)
            score_maxima(nc,g,q_max,True,None,'sc_')
            log_scales(nc,g,q_scale,q_ln,q_max,lse,'lc_')
            row_terms(nc,g,q_ln,g.QT,HD,'rc_')
            weighted_values(nc,g,O,q_scale)
            OQ=c2.enter_context(nc.sbuf_tensor('OQ',[P,T,E],BF16)); os=c2.enter_context(nc.sbuf_tensor('os',[P,T],F32))
            quantise(nc,g,O[:],OQ[:],T,E,os[:],False,'o_')
            projection(nc,g,OQ,os,a['L0_attn_b_proj'])
        g.free_sems()
        moments(nc,g,'m1_')
        feed_forward(nc,g,a['L0_ffn_w_gate'],a['L0_ffn_w_up'],a['L0_ffn_w_down'])
        moments(nc,g,'m2_')
        sparse_attention(nc,g,*(a['L1_attn_'+n] for n in ('Wq','bq','Wk','bk','Wv','bv','Wo','bo')))
        moments(nc,g,'m3_')
        experts(nc,g,out,a['L1_ffn_router_w'],a['L1_ffn_router_b'],a['L1_ffn_weights1'],a['L1_ffn_bias1'],a['L1_ffn_weights2'],a['L1_ffn_bias2'])


def kernel(**inputs):
    import concourse.bacc as bacc
    from concourse.bass_utils import run_bass_kernel_spmd

    nc = bacc.Bacc("TRN2", target_bir_lowering=False, num_devices=1)
    arrays, args = {}, {}
    for name, value in inputs.items():
        v = np.asarray(value)
        if name in ("L0_ffn_w_gate", "L0_ffn_w_up", "L0_ffn_w_down", "L1_ffn_router_w"):
            v = v.T
        elif name in ("L1_attn_bq", "L1_attn_bk", "L1_ffn_bias1"):
            v = v.reshape(-1, P).T
        v = np.ascontiguousarray(v)
        arrays["in_" + name] = v
        args[name] = nc.dram_tensor("in_" + name, v.shape, mybir.dt.from_np(v.dtype), kind="ExternalInput").ap()
    out = nc.dram_tensor("out", (B, S, E), F32, kind="ExternalOutput").ap()
    tower(nc, args, out)
    return run_bass_kernel_spmd(nc, [arrays], core_ids=[0]).results[0]["out"]
```

```python
from contextlib import ExitStack

import numpy as np
import concourse.bass as bass
from concourse import mybir

F32, BF16, F16, I32 = mybir.dt.float32, mybir.dt.bfloat16, mybir.dt.float16, mybir.dt.int32
ALU = mybir.AluOpType
ACT = mybir.ActivationFunctionType
AX = mybir.AxisListType.X
ABSMAX = bass.bass_isa.ReduceOp.absmax

P = 128
B, S, E = 8, 512, 256
T = B * S // P
TB = S // P
EC = E // P
HEADS, HD = 16, 16
HG = 4
NG = B * HEADS // HG
STRIP = 32
PAD_ID, SEP_ID = 1, 4
ROUND = 1.5 * 2.0 ** 23
PRED = 1.0 - 2.0 ** -24
SLACK = 1.0 - 2.0 ** -16
EPS_Q = 0.01
EPS_LN = 1e-5
NEG = -1e30


class Steps:

    def __init__(self, eng, sem, i=None, per=0, base=0):
        self.eng, self.sem, self.n, self.i, self.per, self.base = eng, sem, 0, i, per, base

    def link(self, ins):
        self.n += 1
        ins.then_inc(self.sem, 1)
        at = self.base + self.n
        self.eng.wait_ge(self.sem, at if self.i is None else self.i * self.per + at)

    def close(self):
        assert self.i is None or self.n == self.per, (self.n, self.per)


def row(ap):
    return ap.rearrange("(a n) -> a n", a=1).broadcast_to([P, ap.shape[0]])


def pow2_up(nc, st, out, inv, x, low, tmp, slack=PRED):
    st.link(nc.vector.tensor_scalar(tmp, x, low, slack, ALU.max, ALU.mult))
    st.link(nc.vector.tensor_single_scalar(tmp.bitcast(I32), tmp.bitcast(I32), -(1 << 23), ALU.bitwise_and))
    if inv is not None:
        st.link(nc.vector.tensor_scalar(inv.bitcast(I32), tmp.bitcast(I32), -1.0, float(253 << 23), ALU.mult, ALU.add))
    st.link(nc.vector.tensor_scalar(out, tmp, 2.0, None, ALU.mult))


def statistics(nc, g, t):
    nc.vector.bn_stats(g.stats[:, bass.ds(t, 1), :], g.H[:, bass.ds(t, 1), :])


def constants_and_tokens(nc, g, tokens, table):
    with ExitStack() as c:
        sb = lambda n, s, d: c.enter_context(nc.sbuf_tensor(n, s, d))
        tok = sb("tok", [B, S], I32)
        place = sb("place", [B, S], I32)
        placef = sb("placef", [B, S], F32)
        sep_at = sb("sep_at", [B, S], F32)
        last_sep = sb("last_sep", [B, S], F32)
        not_pad = sb("not_pad", [B, S], F32)
        valid = sb("valid", [B, S], F32)
        back = sb("back", [B, S], F32)
        pos = sb("pos", [B, S], F32)
        rows = sb("rows", [P, T], I32)
        tokens_in = g.sem("tokens_in")
        made = g.sem("made")
        chain = g.sem("tok_chain")
        pos_ready = g.sem("pos_ready")
        pos_turned = g.sem("pos_turned")
        rows_ready = g.sem("rows_ready")
        gathered = [g.sem(f"gathered{b}") for b in range(B)]
        block = c.enter_context(nc.Block())

        @block.sync
        def _(sp):
            sp.dma_start(tok[:], tokens).then_inc(tokens_in, 16)

        @block.gpsimd
        def _(pool):
            st = Steps(pool, made)
            st.link(nc.gpsimd.iota(place[:], pattern=[[1, S]], base=0, channel_multiplier=0))
            st.link(nc.gpsimd.memset(g.ident[:], 1.0))
            st.link(nc.gpsimd.affine_select(out=g.ident[:], in_=g.ident[:], compare_op=ALU.is_equal, fill=0.0,
                                            base=0, pattern=[[-1, P]], channel_multiplier=1))
            st.link(nc.gpsimd.memset(g.identf[:], 1.0))
            st.link(nc.gpsimd.affine_select(out=g.identf[:], in_=g.identf[:], compare_op=ALU.is_equal, fill=0.0,
                                            base=0, pattern=[[-1, P]], channel_multiplier=1))
            st.link(nc.gpsimd.memset(g.mask_q[:], 0.0))
            st.link(nc.gpsimd.affine_select(out=g.mask_q[:], in_=g.mask_q[:], compare_op=ALU.is_ge, fill=NEG,
                                            base=0, pattern=[[-1, P]], channel_multiplier=1))
            st.link(nc.gpsimd.memset(g.mask_k[:], 0.0))
            st.link(nc.gpsimd.affine_select(out=g.mask_k[:], in_=g.mask_k[:], compare_op=ALU.is_ge, fill=NEG,
                                            base=0, pattern=[[1, P]], channel_multiplier=-1))
            pool.wait_ge(rows_ready, 1)
            for t in range(T):
                nc.gpsimd.indirect_dma_start(out=g.H[:, t, :], out_offset=None, in_=table,
                                             in_offset=bass.IndirectOffsetOnAxis(ap=rows[:, t:t + 1], axis=0)
                                             ).then_inc(gathered[t // TB], 16)

        @block.vector
        def _(dve):
            st = Steps(dve, chain)
            dve.wait_ge(made, 1)
            dve.wait_ge(tokens_in, 16)
            st.link(nc.vector.tensor_copy(placef[:], place[:]))
            st.link(nc.vector.scalar_tensor_tensor(out=sep_at[:], in0=tok[:], scalar=float(SEP_ID), in1=placef[:],
                                                   op0=ALU.is_equal, op1=ALU.mult))
            st.link(nc.vector.tensor_tensor_scan(last_sep[:], sep_at[:], sep_at[:], 0.0, ALU.max, ALU.max))
            st.link(nc.vector.tensor_single_scalar(not_pad[:], tok[:], float(PAD_ID), ALU.not_equal))
            st.link(nc.vector.tensor_tensor_scan(valid[:], not_pad[:], not_pad[:], 1.0, ALU.mult, ALU.min))
            st.link(nc.vector.tensor_tensor(back[:], placef[:], last_sep[:], ALU.subtract))
            st.link(nc.vector.scalar_tensor_tensor(out=back[:], in0=back[:], scalar=1.0, in1=valid[:],
                                                   op0=ALU.add, op1=ALU.mult))
            nc.vector.tensor_single_scalar(pos[:], back[:], 1.0, ALU.add).then_inc(pos_ready, 1)
            dve.wait_ge(pos_turned, 1)
            nc.vector.tensor_copy(rows[:].rearrange("p (b t) -> p t b", b=B),
                                  g.PS[:, 0, 0:T].rearrange("p (t b) -> p t b", b=B)).then_inc(rows_ready, 1)
            for b in range(B):
                dve.wait_ge(gathered[b], 16 * TB)
                for t in range(TB):
                    statistics(nc, g, b * TB + t)

        @block.tensor
        def _(pe):
            pe.wait_ge(made, 5)
            pe.wait_ge(pos_ready, 1)
            for t in range(TB):
                last = nc.tensor.transpose(g.PS[:, 0, t * B:(t + 1) * B], pos[:, t * P:(t + 1) * P], g.identf[0:B, 0:B])
            last.then_inc(pos_turned, 1)


CUT = -(1 << 12)


def exact_rsqrt(nc, st, rstd, ve, root, y, tmp):
    rh, rl, yh, yl, t, rest = tmp
    v = nc.vector

    def halves(x, hi, lo):
        st.link(v.tensor_single_scalar(hi.bitcast(I32), x.bitcast(I32), CUT, ALU.bitwise_and))
        st.link(v.tensor_tensor(lo, x, hi, ALU.subtract))

    def less(a, b, times=-1.0):
        st.link(v.tensor_tensor(t, a, b, ALU.mult))
        st.link(v.scalar_tensor_tensor(out=rest, in0=t, scalar=times, in1=rest, op0=ALU.mult, op1=ALU.add))

    st.link(v.reciprocal(y, root))
    halves(root, rh, rl)
    halves(y, yh, yl)
    st.link(v.tensor_tensor(t, rh, rh, ALU.mult))
    st.link(v.tensor_tensor(rest, ve, t, ALU.subtract))
    less(rh, rl, -2.0)
    less(rl, rl)
    st.link(v.scalar_tensor_tensor(out=rstd, in0=rest, scalar=0.5, in1=y, op0=ALU.mult, op1=ALU.mult))
    st.link(v.tensor_tensor(t, yh, rh, ALU.mult))
    st.link(v.tensor_scalar(rest, t, -1.0, 1.0, ALU.mult, ALU.add))
    less(yh, rl)
    less(yl, rh)
    less(yl, rl)
    less(y, rstd)
    st.link(v.tensor_tensor(t, y, rest, ALU.mult))
    st.link(v.tensor_tensor(rstd, y, t, ALU.add))


def moments(nc, g, tag):
    with ExitStack() as c:
        sb = lambda n, s=[P, T]: c.enter_context(nc.sbuf_tensor(tag + n, s, F32))
        diff, ve, root, half = sb("diff"), sb("ve"), sb("root"), sb("half")
        tmp = sb("tmp", [P, 6, T])
        chain, var_ready, root_ready = (g.sem(tag + n) for n in ("ln_chain", "var_ready", "root_ready"))
        block = c.enter_context(nc.Block())

        @block.scalar
        def _(act):
            nc.scalar.preload_act_table(ACT.Sqrt)
            act.wait_ge(var_ready, 1)
            nc.scalar.activation(root[:], ve[:], ACT.Sqrt).then_inc(root_ready, 1)

        @block.vector
        def _(dve):
            mean_even, m2_even, mean_odd, m2_odd = (g.stats[:, :, n] for n in (1, 2, 4, 5))
            st = Steps(dve, chain)
            st.link(nc.vector.tensor_tensor(diff[:], mean_even, mean_odd, ALU.subtract))
            st.link(nc.vector.tensor_tensor(g.mean[:], mean_even, mean_odd, ALU.add))
            st.link(nc.vector.tensor_single_scalar(g.mean[:], g.mean[:], 0.5, ALU.mult))
            st.link(nc.vector.tensor_tensor(half[:], m2_even, m2_odd, ALU.add))
            st.link(nc.vector.tensor_tensor(diff[:], diff[:], diff[:], ALU.mult))
            st.link(nc.vector.tensor_scalar(diff[:], diff[:], 0.25, EPS_LN, ALU.mult, ALU.add))
            nc.vector.scalar_tensor_tensor(out=ve[:], in0=half[:], scalar=1.0 / E, in1=diff[:], op0=ALU.mult,
                                           op1=ALU.add).then_inc(var_ready, 1)
            dve.wait_ge(root_ready, 1)
            exact_rsqrt(nc, st, g.rstd[:], ve[:], root[:], half[:], [tmp[:, n] for n in range(6)])


def normalise(nc, g, out, t):
    return nc.vector.tensor_scalar(out, g.H[:, bass.ds(t, 1), :].rearrange("p a e -> p (a e)"),
                                   g.mean[:, bass.ds(t, 1)],
                                   g.rstd[:, bass.ds(t, 1)], ALU.subtract, ALU.mult)


def layernorm(nc, g, Y, tag):
    moments(nc, g, tag)
    with nc.Block() as block:
        @block.vector
        def _(dve):
            with dve.Fori(0, B) as b:
                for t in range(TB):
                    normalise(nc, g, Y[:, bass.ds(b * TB + t, 1), :].rearrange("p a e -> p (a e)"), b * TB + t)


def quantise(nc, g, X, out, n, width, scale2, fold, tag):
    with ExitStack() as c:
        sb = lambda nm, s, d=F32: c.enter_context(nc.sbuf_tensor(tag + nm, s, d))
        col = sb("col", [P, width])
        colb = sb("colb", [P, width])
        tmpc = sb("tmpc", [P, width])
        s1 = sb("s1", [P, width])
        s1i = sb("s1i", [P, width])
        rmax = sb("rmax", [P, n])
        tmpr = sb("tmpr", [P, n])
        s2i = sb("s2i", [P, n])
        lift = sb("lift", [P, n])
        chain = g.sem(tag + "q_chain")
        col_ready = g.sem(tag + "col_ready")
        col_all = g.sem(tag + "col_all")
        lift_ready, lifted = g.sem(tag + "lift_ready"), g.sem(tag + "lifted")
        block = c.enter_context(nc.Block())
        full = [P, n, width]
        by_col = lambda a: a[:].unsqueeze(1).broadcast_to(full)

        @block.gpsimd
        def _(pool):
            pool.wait_ge(col_ready, 1)
            nc.gpsimd.partition_all_reduce(colb[:], col[:], P, ABSMAX).then_inc(col_all, 1)

        @block.scalar
        def _(act):
            act.wait_ge(lift_ready, 1)
            for t in range(n):
                nc.scalar.activation(X[:, t], X[:, t], ACT.Copy, scale=lift[:, t:t + 1], bias=ROUND).then_inc(lifted, 1)

        @block.vector
        def _(dve):
            st = Steps(dve, chain)
            nc.vector.tensor_reduce(col[:], X.rearrange("p t e -> p e t"), AX, ALU.max,
                                    apply_absolute_value=True).then_inc(col_ready, 1)
            dve.wait_ge(col_all, 1)
            pow2_up(nc, st, s1[:], s1i[:], colb[:], EPS_Q, tmpc[:])
            st.link(nc.vector.tensor_tensor(X, X, by_col(s1i), ALU.mult))
            st.link(nc.vector.tensor_reduce(rmax[:], X, AX, ALU.max, apply_absolute_value=True))
            pow2_up(nc, st, scale2, s2i[:], rmax[:], EPS_Q, tmpr[:])
            nc.vector.tensor_single_scalar(lift[:], s2i[:], 128.0, ALU.mult).then_inc(lift_ready, 1)
            st.link(nc.vector.tensor_single_scalar(scale2, scale2, 1.0 / 128, ALU.mult))
            some = min(n, 8)
            for lo in range(0, n, some):
                ts = slice(lo, lo + some)
                Xs, cols = X[:, ts], s1[:].unsqueeze(1).broadcast_to([P, some, width])
                dve.wait_ge(lifted, lo + some)
                st.link(nc.vector.tensor_single_scalar(Xs, Xs, ROUND + 127.0, ALU.min))
                back = nc.vector.scalar_tensor_tensor(out=Xs if fold else out[:, ts], in0=Xs, scalar=ROUND, in1=cols,
                                                      op0=ALU.subtract, op1=ALU.mult)
                if fold:
                    st.link(back)
                    nc.vector.tensor_tensor(out[:, ts], Xs, scale2[:, ts].unsqueeze(2).broadcast_to([P, some, width]), ALU.mult)


def weights_quantised(nc, g, w_attn, w_proj):
    with ExitStack() as c:
        wa = c.enter_context(nc.sbuf_tensor("wa_f", [P, EC, 3 * E], F32))
        wp = c.enter_context(nc.sbuf_tensor("wp_f", [P, EC, E], F32))
        sa = c.enter_context(nc.sbuf_tensor("wa_s", [P, EC], F32))
        sp_ = c.enter_context(nc.sbuf_tensor("wp_s", [P, EC], F32))
        w_in = g.sem("w_in")
        with nc.Block() as block:
            @block.sync
            def _(sp):
                sp.dma_start(wa[:], w_attn.rearrange("(c p) n -> p c n", p=P)).then_inc(w_in, 16)
                sp.dma_start(wp[:], w_proj.rearrange("(c p) n -> p c n", p=P)).then_inc(w_in, 16)
                sp.wait_ge(w_in, 32)
        quantise(nc, g, wa[:], g.WA[:], EC, 3 * E, sa[:], True, "wa_")
        quantise(nc, g, wp[:], g.WP[:], EC, E, sp_[:], True, "wp_")


def in_turn(eng, steps):
    steps(0, 0, True, False)
    with eng.Fori(0, B // 2 - 1) as n:
        steps(n * 2 + 1, 1, True, True)
        steps(n * 2 + 2, 0, True, True)
    steps(B - 1, 1, True, True)
    steps(B, 0, False, True)


def qkv_quantised(nc, g, XQ, xs, b_attn):
    with ExitStack() as c:
        sb = lambda n, s, d=F32: c.enter_context(nc.sbuf_tensor(n, s, d))
        bias = sb("bias_a", [P, 3 * E])
        xT = sb("xT", [P, 2, EC, P], BF16)
        R = sb("R", [P, 2, TB, 3 * E])
        col, colb = sb("r_col", [P, 2, 3 * E]), sb("r_colb", [P, 2, 3 * E])
        tmpc = sb("r_tmpc", [P, 3 * E])
        cs, ci = sb("r_cs", [P, 2, 3 * E]), sb("r_ci", [P, 3 * E])
        rmax, tmpr, ri = (sb(n, [P, TB, 3 * HEADS]) for n in ("r_rmax", "r_tmpr", "r_ri"))
        rs = sb("r_rs", [P, 2, TB, 3 * HEADS])
        QP = sb("QP", [P, TB, HEADS, STRIP], BF16)
        KP = sb("KP", [P, TB, HEADS, STRIP], BF16)
        turned = sb("turned", [P, 2, HG, S], BF16)
        bias_in, x_turned, xT_ready, qkv_done, r_ready, waited = (g.sem(n) for n in (
            "bias_in", "x_turned", "xT_ready", "qkv_done", "r_ready", "col_waited"))
        pads_made, col_ready, col_all, scaled, lifted, rounded = (g.sem(n) for n in (
            "pads_made", "qkv_col_ready", "qkv_col_all", "scaled", "lifted", "rounded"))
        chain_a, chain_b, chain_c, columned, q_ready, kv_ready = (g.sem(n) for n in (
            "chain_a", "chain_b", "chain_c", "columned", "q_ready", "kv_ready"))
        strip_turned, strip_copied = (g.sem(n) for n in ("strip_turned", "strip_copied"))
        stored = [g.sem("stored0"), g.sem("stored1")]
        block = c.enter_context(nc.Block())
        by_head = lambda a: a.unsqueeze(3).broadcast_to([P, TB, HEADS, HD])
        bank = lambda n: g.PS[:, n, :].bitcast(BF16)
        goes_on = lambda b: not isinstance(b, int) or b < B - 1
        products = lambda b, this: () if not this else range(TB) if isinstance(b, int) and b == 0 else (2, 3)

        def parts(half):
            R4 = R[:, half].rearrange("p t (x h d) -> p t x h d", x=3, d=HD)
            return (R4, *(a.rearrange("p t (x h) -> p t x h", x=3) for a in (rmax[:], ri[:], rs[:, half], tmpr[:])))

        @block.sync
        def _(sp):
            sp.dma_start(bias[:], row(b_attn)).then_inc(bias_in, 16)
            with sp.Fori(0, B) as b:
                for s, dst in enumerate((g.QT, g.KT)):
                    sp.wait_ge(strip_copied, b * 8 + 4 * s + 6)
                    sp.dma_start(dst[bass.ds(b * HG, HG), :, :].rearrange("g p c -> p g c"),
                                 turned[:, s]).then_inc(stored[s], 16)
            for s in range(2):
                sp.wait_ge(stored[s], 16 * B)

        @block.gpsimd
        def _(pool):
            nc.gpsimd.memset(QP[:], 0.0).then_inc(pads_made, 1)
            nc.gpsimd.memset(KP[:], 0.0).then_inc(pads_made, 1)
            pool.wait_ge(pads_made, 2)
            nc.gpsimd.memset(QP[:, :, :, HD + 3:HD + 6], 1.0).then_inc(pads_made, 1)
            nc.gpsimd.memset(KP[:, :, :, HD:HD + 3], 1.0).then_inc(pads_made, 1)
            pool.wait_ge(pads_made, 4)

            def steps(b, half, this, last):
                if this:
                    pool.wait_ge(col_ready, b + 1)
                    pool.sem_inc(waited, 1)
                    nc.gpsimd.partition_all_reduce(colb[:, half], col[:, half], P, ABSMAX).then_inc(col_all, 1)
                if last:
                    R4, _, _, rsv, _ = parts(1 - half)
                    pool.wait_ge(columned, b)
                    if not (isinstance(b, int) and b == 1):
                        pool.wait_ge(strip_copied, b * 8 - 6)
                    nc.gpsimd.tensor_tensor(KP[:, :, :, 0:HD], R4[:, :, 1], by_head(rsv[:, :, 1]), ALU.mult).then_inc(kv_ready, 1)
                    nc.gpsimd.tensor_tensor(
                        g.V[:, bass.ds(b * TB - TB, TB), :].rearrange("p t (h d) -> p t h d", d=HD),
                        R4[:, :, 2], by_head(rsv[:, :, 2]), ALU.mult).then_inc(kv_ready, 1)

            in_turn(pool, steps)

        @block.tensor
        def _(pe):
            pe.sem_inc(strip_turned, 8)

            def product(at, t):
                at = at + t
                pe.wait_ge(xT_ready, at + 1)
                for e in range(EC):
                    last = nc.tensor.transpose(bank(t % 2)[:, e * P:(e + 1) * P],
                                               XQ[:, bass.ds(at, 1), e * P:(e + 1) * P].rearrange(
                                                   "p a c -> p (a c)"), g.ident[:])
                last.then_inc(x_turned, 1)
                pe.wait_ge(xT_ready, at + 3)
                pe.wait_ge(r_ready, at + 1)
                for e in range(EC):
                    for n, (lo, hi) in enumerate(((0, 512), (512, 768))):
                        last = nc.tensor.matmul(g.PS[:, 2 + 2 * (t % 2) + n, 0:hi - lo], xT[:, t % 2, e, :],
                                                g.WA[:, e, lo:hi], start=(e == 0), stop=(e == EC - 1))
                last.then_inc(qkv_done, 1)

            def steps(b, half, this, last_batch):
                for t in products(b, this):
                    product(b * TB, t)
                for n in range(2 * HG) if last_batch else ():
                    s, hg = n // HG, n % HG
                    if n == 0:
                        pe.wait_ge(q_ready, b)
                    if n == HG:
                        pe.wait_ge(kv_ready, b * 2)
                    pe.wait_ge(strip_copied, b * 8 - 8 + n + 1)
                    for t in range(TB):
                        last = nc.tensor.transpose(bank(6 + n % 2)[:, t * P:(t + 1) * P],
                                                   (QP, KP)[s][:, t, hg * HG:(hg + 1) * HG, :].rearrange(
                                                       "p h d -> p (h d)"), g.ident[:])
                    last.then_inc(strip_turned, 1)
                for t in (0, 1) if goes_on(b) else ():
                    product(b * TB + TB, t)

            in_turn(pe, steps)

        @block.scalar
        def _(act):
            act.sem_inc(xT_ready, 2)
            act.sem_inc(strip_copied, 2)

            def copy_x(at, t):
                act.wait_ge(x_turned, at + t + 1)
                act.wait_ge(r_ready, at + t + 1)
                nc.scalar.activation(xT[:, t % 2].rearrange("p c n -> p (c n)"), bank(t % 2)[:, 0:EC * P],
                                     ACT.Copy).then_inc(xT_ready, 1)

            def steps(b, half, this, last):
                for t in products(b, this):
                    copy_x(b * TB, t)
                for n in range(2 * HG) if last else ():
                    act.wait_ge(strip_turned, b * 8 + n + 1)
                    if n % HG == 0 and not (isinstance(b, int) and b == 1):
                        act.wait_ge(stored[n // HG], b * 16 - 16)
                    nc.scalar.activation(turned[:, n // HG, n % HG, :], bank(6 + n % 2)[:, 0:S],
                                         ACT.Copy).then_inc(strip_copied, 1)
                for t in (0, 1) if goes_on(b) else ():
                    copy_x(b * TB + TB, t)
                if this:
                    act.wait_ge(scaled, b + 1)
                    nc.scalar.activation(R[:, half], R[:, half], ACT.Copy, scale=128.0, bias=ROUND).then_inc(lifted, 1)
                    act.wait_ge(lifted, b + 1)
                    nc.scalar.activation(R[:, half], R[:, half], ACT.Copy, bias=-ROUND).then_inc(rounded, 1)

            in_turn(act, steps)

        @block.vector
        def _(dve):
            dve.sem_inc(r_ready, 2)
            dve.wait_ge(bias_in, 16)
            dve.wait_ge(pads_made, 4)

            def steps(b, half, this, last):
                R4, rm, riv, rsv, tmv = parts(half)
                if this:
                    st = Steps(dve, chain_a, b, 5)
                    if not (isinstance(b, int) and b <= 1):
                        dve.wait_ge(kv_ready, b * 2 - 2)
                    for t in range(TB):
                        dve.wait_ge(qkv_done, b * TB + t + 1)
                        nc.vector.scalar_tensor_tensor(
                            out=R[:, half, t, :], in0=g.PS[:, 2 + 2 * (t % 2):4 + 2 * (t % 2), :].rearrange(
                                "p a c -> p (a c)")[:, 0:3 * E],
                            scalar=xs[:, bass.ds(b * TB + t, 1)], in1=bias[:], op0=ALU.mult, op1=ALU.add).then_inc(r_ready, 1)
                    dve.wait_ge(r_ready, b * TB + TB + 2)
                    st.link(nc.vector.tensor_reduce(rm[:, :, 1], R4[:, :, 1], AX, ALU.max, apply_absolute_value=True))
                    st.link(nc.vector.tensor_scalar(tmv[:, :, 1], rm[:, :, 1], EPS_Q, PRED, ALU.max, ALU.mult))
                    st.link(nc.vector.tensor_single_scalar(tmv[:, :, 1].bitcast(I32), tmv[:, :, 1].bitcast(I32), -(1 << 23),
                                                           ALU.bitwise_and))
                    st.link(nc.vector.tensor_scalar(riv[:, :, 1].bitcast(I32), tmv[:, :, 1].bitcast(I32), -1.0,
                                                    float(253 << 23), ALU.mult, ALU.add))
                    st.link(nc.vector.tensor_tensor(R4[:, :, 1], R4[:, :, 1], by_head(riv[:, :, 1]), ALU.mult))
                    st.close()
                    nc.vector.tensor_reduce(col[:, half], R[:, half].rearrange("p t n -> p n t"), AX, ALU.max,
                                            apply_absolute_value=True).then_inc(col_ready, 1)
                if last:
                    R4o, _, _, rso, _ = parts(1 - half)
                    dve.wait_ge(rounded, b)
                    for t in range(TB):
                        ins = nc.vector.scalar_tensor_tensor(out=R[:, 1 - half, t], in0=R[:, 1 - half, t], scalar=127.0,
                                                             in1=cs[:, 1 - half], op0=ALU.min, op1=ALU.mult)
                    ins.then_inc(columned, 1)
                    dve.wait_ge(columned, b)
                    if not (isinstance(b, int) and b == 1):
                        dve.wait_ge(strip_turned, b * 8 - 4)
                    nc.vector.tensor_tensor(QP[:, :, :, 0:HD], R4o[:, :, 0], by_head(rso[:, :, 0]), ALU.mult).then_inc(q_ready, 1)
                if this:
                    st = Steps(dve, chain_b, b, 13)
                    st.link(nc.vector.tensor_single_scalar(rsv[:, :, 1], tmv[:, :, 1], 2.0, ALU.mult))
                    dve.wait_ge(col_all, b + 1)
                    pow2_up(nc, st, cs[:, half], ci[:], colb[:, half], EPS_Q, tmpc[:])
                    st.link(nc.vector.tensor_tensor(R[:, half], R[:, half], ci[:].unsqueeze(1).broadcast_to([P, TB, 3 * E]),
                                                    ALU.mult))
                    nc.vector.tensor_reduce(rm[:, :, 0], R4[:, :, 0], AX, ALU.max, apply_absolute_value=True)
                    st.link(nc.vector.tensor_reduce(rm[:, :, 2], R4[:, :, 2], AX, ALU.max, apply_absolute_value=True))
                    pow2_up(nc, st, rsv[:, :, 0::2], riv[:, :, 0::2], rm[:, :, 0::2], EPS_Q, tmv[:, :, 0::2])
                    nc.vector.tensor_tensor(R4[:, :, 0], R4[:, :, 0], by_head(riv[:, :, 0]), ALU.mult)
                    st.link(nc.vector.tensor_tensor(R4[:, :, 2], R4[:, :, 2], by_head(riv[:, :, 2]), ALU.mult))
                    st.link(nc.vector.tensor_single_scalar(rs[:, half], rs[:, half], 1.0 / 128, ALU.mult))
                    nc.vector.tensor_single_scalar(rsv[:, :, 0], rsv[:, :, 0], HD ** -0.5, ALU.mult).then_inc(scaled, 1)
                    st.close()

            in_turn(dve, steps)


GRID = 1.5 * 2.0 ** 16


def load_groups(sp, g, qk, loaded, ready, tiles):
    for hg in range(2):
        sp.dma_start(qk[:, hg, 0], g.QT[hg]).then_inc(loaded[hg], 16)
        sp.dma_start(qk[:, hg, 1], g.KT[hg]).then_inc(loaded[hg], 16)
    with sp.Fori(0, NG // 2 - 1) as n:
        for half in range(2):
            sp.wait_ge(ready, (n * 2 + half + 1) * tiles)
            for s, src in enumerate((g.QT, g.KT)):
                sp.dma_start(qk[:, half, s], src[bass.ds(n * 2 + half + 2, 1), :, :].rearrange("g p c -> p (g c)")
                             ).then_inc(loaded[half], 16)


def scores(nc, g, qk, half, t, by_query, heads, bank0):
    own, other = (0, 1) if by_query else (1, 0)
    lo, hi = (0, (t + 1) * P) if by_query else (t * P, S)
    for n, h in enumerate(heads):
        strip = slice(STRIP * h, STRIP * (h + 1))
        nc.tensor.matmul(g.PS[:, bank0 + n, 0:hi - lo], qk[strip, half, own, t * P:(t + 1) * P],
                         qk[strip, half, other, lo:hi], start=True, stop=False, skip_group_check=True)
    diag = hi - lo - P if by_query else 0
    for n, h in enumerate(heads):
        last = nc.tensor.matmul(g.PS[:, bank0 + n, diag:diag + P], g.ident[:],
                                g.mask_q[:] if by_query else g.mask_k[:], start=False, stop=True, skip_group_check=True)
    return last


def width(t, by_query):
    return (t + 1) * P if by_query else S - t * P


def score_maxima(nc, g, out, by_query, sums, tag):
    with ExitStack() as c:
        qk = c.enter_context(nc.sbuf_tensor(tag + "qk", [P, 2, 2, S], BF16))
        sem = lambda n: g.sem(tag + n)
        loaded = [sem("loaded0"), sem("loaded1")]
        ready, maxed, free = sem("ready"), sem("maxed"), sem("free")
        block = c.enter_context(nc.Block())

        SETS = 4
        PER = HG * TB * 2

        def tiles():
            for u in range(PER):
                yield u, u // (2 * TB), u // 2 % TB, 2 * (u % 2)

        @block.sync
        def _(sp):
            load_groups(sp, g, qk, loaded, ready, 2 * TB)

        @block.tensor
        def _(pe):
            with pe.Fori(0, B) as b:
                for u, hg, t, h in tiles():
                    if u % (2 * TB) == 0:
                        pe.wait_ge(loaded[hg % 2], b * 64 + 32 * (hg // 2) + 32)
                    pe.wait_ge(free, b * PER + u + 1)
                    scores(nc, g, qk, hg % 2, t, by_query, (h, h + 1), 2 * (u % SETS)).then_inc(ready, 1)

        @block.vector
        def _(dve):
            if sums is None:
                dve.sem_inc(free, SETS)
            with dve.Fori(0, B) as b:
                for u, hg, t, h in tiles():
                    dve.wait_ge(ready, b * PER + u + 1)
                    nc.vector.tensor_reduce(
                        out[:, t, bass.ds(b * HG + hg, 1), h:h + 2].rearrange("p g h -> p (g h)"),
                        g.PS[:, 2 * (u % SETS):2 * (u % SETS) + 2, 0:width(t, by_query)], AX, ALU.max,
                        negate=sums is not None).then_inc(free if sums is None else maxed, 1)

        if sums is not None:
            @block.scalar
            def _(act):
                nc.scalar.preload_act_table(ACT.Exp)
                act.sem_inc(free, SETS)
                with act.Fori(0, B) as b:
                    for u, hg, t, h in tiles():
                        act.wait_ge(maxed, b * PER + u + 1)
                        for n in range(2):
                            at = lambda a: a[:, t, bass.ds(b * HG + hg, 1), h + n:h + n + 1].rearrange("p g h -> p (g h)")
                            bank = g.PS[:, 2 * (u % SETS) + n, 0:width(t, by_query)]
                            last = nc.scalar.activation(bank, bank, ACT.Exp, bias=at(out), accum_out=at(sums))
                        last.then_inc(free, 1)


def row_terms(nc, g, term, dst, first, tag):
    with ExitStack() as c:
        part = c.enter_context(nc.sbuf_tensor(tag + "part", [P, 3, TB, NG * HG], BF16))
        rest = c.enter_context(nc.sbuf_tensor(tag + "rest", [P, TB, NG * HG], F32))
        across = c.enter_context(nc.sbuf_tensor(tag + "across", [P, 3, S], BF16))
        sem = lambda n: g.sem(tag + n)
        chain, parted, turned, copied, stored = (sem(n) for n in ("chain", "parted", "turned", "copied", "stored"))
        block = c.enter_context(nc.Block())

        @block.vector
        def _(dve):
            st = Steps(dve, chain)
            whole = term.rearrange("p t g h -> p t (g h)")
            left = whole
            for j in range(3):
                nc.vector.tensor_copy(part[:, j], left).then_inc(parted, 1)
                dve.wait_ge(parted, j + 1)
                if j < 2:
                    st.link(nc.vector.tensor_tensor(rest[:], left, part[:, j], ALU.subtract))
                    left = rest[:]

        @block.tensor
        def _(pe):
            for j in range(3):
                pe.wait_ge(parted, j + 1)
                for t in range(TB):
                    last = nc.tensor.transpose(g.PS[:, j, :].bitcast(BF16)[:, t * P:(t + 1) * P], part[:, j, t], g.ident[:])
                last.then_inc(turned, 1)

        @block.scalar
        def _(act):
            for j in range(3):
                act.wait_ge(turned, j + 1)
                nc.scalar.activation(across[:, j], g.PS[:, j, :].bitcast(BF16)[:, 0:S], ACT.Copy).then_inc(copied, 1)

        @block.sync
        def _(sp):
            for j in range(3):
                sp.wait_ge(copied, j + 1)
                sp.dma_start(dst.rearrange("g (h r) c -> (g h) r c", r=STRIP)[:, first + j, :],
                             across[:, j]).then_inc(stored, 16)
            sp.wait_ge(stored, 48)


def log_sums(nc, g, lse, neg_max, sums):
    ln_ready = g.sem("ln_ready")
    with nc.sbuf_tensor("lns", [P, TB, NG, HG], F32) as lns, nc.Block() as block:
        @block.scalar
        def _(act):
            nc.scalar.activation(lns[:], sums, ACT.Ln).then_inc(ln_ready, 1)

        @block.vector
        def _(dve):
            dve.wait_ge(ln_ready, 1)
            nc.vector.tensor_tensor(lse, neg_max, lns[:], ALU.subtract)


def log_scales(nc, g, scale, neg_ln, logs, extra, tag):
    with ExitStack() as c:
        tmp = c.enter_context(nc.sbuf_tensor(tag + "tmp", [P, TB, NG, HG], F32))
        sem = lambda n: g.sem(tag + n)
        chain, exp_ready, scale_ready, ln_ready = (sem(n) for n in ("chain", "exp_ready", "scale_ready", "ln_ready"))
        block = c.enter_context(nc.Block())

        @block.scalar
        def _(act):
            nc.scalar.activation(scale, logs, ACT.Exp).then_inc(exp_ready, 1)
            act.wait_ge(scale_ready, 1)
            nc.scalar.activation(neg_ln, scale, ACT.Ln).then_inc(ln_ready, 1)

        @block.vector
        def _(dve):
            st = Steps(dve, chain)
            dve.wait_ge(exp_ready, 1)
            st.link(nc.vector.tensor_scalar(tmp[:], scale, EPS_Q, SLACK, ALU.max, ALU.mult))
            st.link(nc.vector.tensor_single_scalar(tmp[:].bitcast(I32), tmp[:].bitcast(I32), -(1 << 23), ALU.bitwise_and))
            nc.vector.tensor_single_scalar(scale, tmp[:], 2.0, ALU.mult).then_inc(scale_ready, 1)
            dve.wait_ge(ln_ready, 1)
            if extra is None:
                nc.vector.tensor_single_scalar(neg_ln, neg_ln, -1.0, ALU.mult)
            else:
                nc.vector.scalar_tensor_tensor(out=neg_ln, in0=neg_ln, scalar=-1.0, in1=extra, op0=ALU.mult, op1=ALU.add)


def scale_values(nc, g, s1):
    with nc.Block() as block:
        @block.vector
        def _(dve):
            for b in range(B):
                for t in range(TB):
                    v = g.V[:, b * TB + t, :].rearrange("p (h d) -> p h d", d=HD)
                    s = s1[:, t, b * HG:(b + 1) * HG, :].rearrange("p g h -> p (g h)").unsqueeze(2).broadcast_to([P, HEADS, HD])
                    nc.vector.tensor_tensor(v, v, s, ALU.mult)


def weighted_values(nc, g, O, s2):
    with ExitStack() as c:
        qk = c.enter_context(nc.sbuf_tensor("d_qk", [P, 2, 2, S], BF16))
        probs = c.enter_context(nc.sbuf_tensor("probs", [P, 3, 2, S], F32))
        steps = c.enter_context(nc.sbuf_tensor("steps", [P, 2, TB, HG, S], BF16))
        sem = lambda n: g.sem("d_" + n)
        loaded = [sem("loaded0"), sem("loaded1")]
        ready, exped, rounded, clipped, summed, read = (sem(n) for n in (
            "ready", "exped", "rounded", "clipped", "summed", "read"))
        block = c.enter_context(nc.Block())
        PER = HG * TB * 2
        prev = lambda u: u - 3 if u >= 3 else (-2, -1, -2)[u]

        @block.sync
        def _(sp):
            load_groups(sp, g, qk, loaded, ready, 2 * TB)

        @block.tensor
        def _(pe):
            def sum_up(b, hg):
                pe.wait_ge(clipped, (b * HG + hg + 1) * TB)
                pe.wait_ge(read, b * HG + hg + 1)
                for q in range(TB):
                    for h in range(HG):
                        for k in range(q + 1):
                            last = nc.tensor.matmul(
                                g.PS[:, 6 + hg % 2, (q * HG + h) * HD:(q * HG + h + 1) * HD],
                                steps[:, hg % 2, k, h, (q - k) * P:(q - k + 1) * P],
                                g.V[:, bass.ds(b * TB + k, 1), (hg * HG + h) * HD:(hg * HG + h + 1) * HD].rearrange(
                                    "p a c -> p (a c)"), start=(k == 0), stop=(k == q))
                last.then_inc(summed, 1)

            pe.sem_inc(summed, 2)
            with pe.Fori(0, B) as b:
                for hg in range(HG):
                    pe.wait_ge(loaded[hg % 2], b * 64 + 32 * (hg // 2) + 32)
                    for t in range(TB):
                        for n in range(2):
                            u = (hg * TB + t) * 2 + n
                            pe.wait_ge(exped, b * PER + prev(u) + 3)
                            scores(nc, g, qk, hg % 2, t, False, (2 * n, 2 * n + 1), 2 * (u % 3)).then_inc(ready, 1)
                    if hg > 0:
                        sum_up(b, hg - 1)
                sum_up(b, HG - 1)

        @block.scalar
        def _(act):
            nc.scalar.preload_act_table(ACT.Exp)
            act.sem_inc(exped, 2)
            with act.Fori(0, B) as b:
                for u in range(PER):
                    w = width(u // 2 % TB, False)
                    act.wait_ge(ready, b * PER + u + 1)
                    act.wait_ge(rounded, b * PER + prev(u) + 3)
                    nc.scalar.activation(probs[:, u % 3, :, 0:w], g.PS[:, 2 * (u % 3):2 * (u % 3) + 2, 0:w],
                                         ACT.Exp).then_inc(exped, 1)

        @block.vector
        def _(dve):
            def read_out(b, hg):
                at = b * HG + hg
                dve.wait_ge(summed, at + 3)
                tiles = [P, TB, HG, HD]
                nc.vector.tensor_tensor(
                    O[:, bass.ds(b * TB, TB), hg * HG * HD:(hg + 1) * HG * HD].rearrange("p t (h d) -> p t h d", d=HD),
                    g.PS[:, 6 + hg % 2, 0:TB * HG * HD].rearrange("p (t h d) -> p t h d", h=HG, d=HD),
                    s2[:, :, bass.ds(at, 1), :].rearrange("p t g h -> p t (g h)").unsqueeze(3).broadcast_to(tiles),
                    ALU.mult).then_inc(read, 1)

            dve.sem_inc(rounded, 2)
            dve.sem_inc(read, 2)
            with dve.Fori(0, B) as b:
                for hg in range(HG):
                    dve.wait_ge(summed, b * HG + hg + 1)
                    for t in range(TB):
                        w = width(t, False)
                        for n in range(2):
                            u = (hg * TB + t) * 2 + n
                            dve.wait_ge(exped, b * PER + u + 3)
                            nc.vector.tensor_scalar(steps[:, hg % 2, t, 2 * n:2 * n + 2, 0:w], probs[:, u % 3, :, 0:w],
                                                    GRID, GRID, ALU.add, ALU.subtract).then_inc(rounded, 1)
                        dve.wait_ge(rounded, b * PER + u + 3)
                        nc.vector.tensor_single_scalar(steps[:, hg % 2, t, :, 0:w], steps[:, hg % 2, t, :, 0:w],
                                                       127.0 / 128, ALU.min).then_inc(clipped, 1)
                    if hg > 0:
                        read_out(b, hg - 1)
                read_out(b, HG - 1)


HIDDEN = 768
HC = HIDDEN // P
FFN_SCALE = 1.0 / 127.0
EXPERTS, EH = 32, 64
TOPK = 8
SLOT_TILES = 64
assert T + EXPERTS - 1 < SLOT_TILES
GONE = -3e38


def projection(nc, g, OQ, os, b_proj):
    with ExitStack() as c:
        bias = c.enter_context(nc.sbuf_tensor("bias_p", [P, E], F32))
        oT = c.enter_context(nc.sbuf_tensor("oT", [P, 2, EC, P], BF16))
        sem = lambda n: g.sem("p_" + n)
        bias_in, biased, turned, copied, done, read = (sem(n) for n in (
            "bias_in", "biased", "turned", "copied", "done", "read"))
        block = c.enter_context(nc.Block())

        @block.sync
        def _(sp):
            sp.dma_start(bias[:], row(b_proj)).then_inc(bias_in, 16)

        @block.gpsimd
        def _(pool):
            pool.wait_ge(bias_in, 16)
            with pool.Fori(0, B) as b:
                h = g.H[:, bass.ds(b * TB, TB), :]
                nc.gpsimd.tensor_tensor(h, h, bias[:].unsqueeze(1).broadcast_to([P, TB, E]), ALU.add).then_inc(biased, 1)

        @block.tensor
        def _(pe):
            def turn(at, t):
                pe.wait_ge(copied, at + 1)
                for e in range(EC):
                    last = nc.tensor.transpose(g.PS[:, t % 2, :].bitcast(BF16)[:, e * P:(e + 1) * P],
                                               OQ[:, bass.ds(at, 1), e * P:(e + 1) * P].rearrange("p a c -> p (a c)"),
                                               g.ident[:])
                last.then_inc(turned, 1)

            def product(at, t):
                pe.wait_ge(copied, at + 3)
                pe.wait_ge(read, at + 1)
                for e in range(EC):
                    last = nc.tensor.matmul(g.PS[:, 2 + t % 2, 0:E], oT[:, t % 2, e, :], g.WP[:, e, :],
                                            start=(e == 0), stop=(e == EC - 1))
                last.then_inc(done, 1)

            turn(0, 0)

            def batch(b, more):
                for t in range(TB):
                    if more or t + 1 < TB:
                        turn(b * TB + t + 1, t + 1)
                    product(b * TB + t, t)

            batches(pe, batch)

        @block.scalar
        def _(act):
            act.sem_inc(copied, 2)
            with act.Fori(0, B) as b:
                for t in range(TB):
                    at = b * TB + t
                    act.wait_ge(turned, at + 1)
                    act.wait_ge(read, at + 1)
                    nc.scalar.activation(oT[:, t % 2].rearrange("p c n -> p (c n)"),
                                         g.PS[:, t % 2, :].bitcast(BF16)[:, 0:EC * P], ACT.Copy).then_inc(copied, 1)

        @block.vector
        def _(dve):
            dve.sem_inc(read, 2)
            with dve.Fori(0, B) as b:
                dve.wait_ge(biased, b + 1)
                for t in range(TB):
                    at = b * TB + t
                    dve.wait_ge(done, at + 1)
                    h = g.H[:, bass.ds(at, 1), :].rearrange("p a e -> p (a e)")
                    nc.vector.scalar_tensor_tensor(out=h, in0=g.PS[:, 2 + t % 2, 0:E], scalar=os[:, bass.ds(at, 1)],
                                                   in1=h, op0=ALU.mult, op1=ALU.add).then_inc(read, 1)
                    if t:
                        dve.wait_ge(read, at + 2)
                        statistics(nc, g, at - 1)
                dve.wait_ge(read, b * TB + TB + 2)
                statistics(nc, g, b * TB + TB - 1)


def batches(eng, batch):
    with eng.Fori(0, B - 1) as b:
        batch(b, True)
    batch(B - 1, False)


def turn_batch(pe, nc, g, Y, bank, turned):
    for e in range(EC):
        for t in range(TB):
            last = nc.tensor.transpose(g.PS[:, bank + e, t * P:(t + 1) * P], Y[:, t, e * P:(e + 1) * P], g.identf[:])
        last.then_inc(turned, 1)


def feed_forward(nc, g, w_gateT, w_upT, w_downT, YS):
    Y_UP, H_DOWN = 2048.0, 0.25
    with ExitStack() as c:
        sb = lambda n, s, d=F32: c.enter_context(nc.sbuf_tensor("f_" + n, s, d))
        raw = sb("raw", [P, 2 * EC * HIDDEN + HC * E], I32)
        w = sb("w", [P, 2 * EC * HIDDEN + HC * E], F16)
        wg, wu = (w[:, n * EC * HIDDEN:(n + 1) * EC * HIDDEN].rearrange("p (c n) -> p c n", c=EC) for n in range(2))
        wd = w[:, 2 * EC * HIDDEN:].rearrange("p (c n) -> p c n", c=HC)
        Y, yT, hT = sb("Y", [P, TB, E]), sb("yT", [P, 2, EC, S], F16), sb("hT", [P, 2, HC, S], F16)
        gate, h = sb("gate", [P, 2, S]), sb("h", [P, 2, S])
        zero = sb("zero", [P, 16, E])
        sem = lambda n: g.sem("f_" + n)
        w_in, w_ready, normed, turned, y_hi, y_lo, up_done, silu_done, h_ready, h_hi, h_lo, down_done, added = (
            sem(n) for n in ("w_in", "w_ready", "normed", "turned", "y_hi", "y_lo", "up_done", "silu_done", "h_ready",
                             "h_hi", "h_lo", "down_done", "added"))
        zero_made, zeroed = sem("zero_made"), sem("zeroed")
        block = c.enter_context(nc.Block())
        gates = 2 * EC * HIDDEN

        @block.sync
        def _(sp):
            for n, src in enumerate((w_gateT, w_upT)):
                sp.dma_start(raw[:, n * EC * HIDDEN:(n + 1) * EC * HIDDEN].rearrange("p (c n) -> p c n", c=EC),
                             src.rearrange("(c p) n -> p c n", p=P)).then_inc(w_in, 16)
            sp.dma_start(raw[:, gates:].rearrange("p (c n) -> p c n", c=HC),
                         w_downT.rearrange("(c p) n -> p c n", p=P)).then_inc(w_in, 16)
            sp.wait_ge(zero_made, 1)
            for n in range(SLOT_TILES // 16):
                sp.dma_start(YS[n * 16:(n + 1) * 16].rearrange("a p e -> p a e"), zero[:]).then_inc(zeroed, 16)
            sp.wait_ge(zeroed, SLOT_TILES)

        @block.gpsimd
        def _(pool):
            nc.gpsimd.memset(zero[:], 0.0).then_inc(zero_made, 1)

        @block.tensor
        def _(pe):
            pe.wait_ge(normed, TB)
            turn_batch(pe, nc, g, Y, 0, turned)
            pe.wait_ge(w_ready, 2)

            def batch(b, more):
                pe.wait_ge(y_hi, b * EC + EC)
                pe.wait_ge(y_lo, b * EC + EC)
                for n in range(HC):
                    pe.wait_ge(h_ready, b * HC + n + 1)
                    for x, wx in enumerate((wg, wu)):
                        for k in range(2 * EC):
                            e, part = k // 2, k % 2
                            last = nc.tensor.matmul(g.PS[:, 2 + 2 * (n % 2) + x, :], wx[:, e, n * P:(n + 1) * P],
                                                    yT[:, part, e], start=(k == 0), stop=(k == 2 * EC - 1))
                    last.then_inc(up_done, 1)
                if more:
                    pe.wait_ge(normed, b * TB + 2 * TB)
                    turn_batch(pe, nc, g, Y, 0, turned)
                pe.wait_ge(h_hi, b * HC + HC + 2)
                pe.wait_ge(h_lo, b * HC + HC + 2)
                for t in range(TB):
                    pe.wait_ge(added, b * TB + t + 1)
                    for k in range(2 * HC):
                        n, part = k // 2, k % 2
                        last = nc.tensor.matmul(g.PS[:, 6 + t % 2, 0:E], hT[:, part, n, t * P:(t + 1) * P], wd[:, n],
                                                start=(k == 0), stop=(k == 2 * HC - 1))
                    last.then_inc(down_done, 1)

            batches(pe, batch)

        @block.scalar
        def _(act):
            nc.scalar.preload_act_table(ACT.Silu)
            act.sem_inc(h_hi, 2)
            act.wait_ge(w_in, 48)
            nc.scalar.activation(w[:, gates // 2:], raw[:, gates // 2:], ACT.Copy).then_inc(w_ready, 1)

            def y_high(b):
                for e in range(EC):
                    act.wait_ge(turned, b * EC + e + 1)
                    nc.scalar.activation(yT[:, 0, e], g.PS[:, e, :], ACT.Copy, scale=Y_UP).then_inc(y_hi, 1)

            def h_high(b, n):
                act.wait_ge(h_ready, b * HC + n + 3)
                nc.scalar.activation(hT[:, 0, n], h[:, n % 2], ACT.Copy).then_inc(h_hi, 1)

            y_high(0)

            def batch(b, more):
                for n in range(HC):
                    act.wait_ge(up_done, b * HC + n + 1)
                    act.wait_ge(h_ready, b * HC + n + 1)
                    nc.scalar.activation(gate[:, n % 2], g.PS[:, 2 + 2 * (n % 2), :], ACT.Silu, scale=FFN_SCALE / Y_UP
                                         ).then_inc(silu_done, 1)
                    if n:
                        h_high(b, n - 1)
                h_high(b, HC - 1)
                if more:
                    y_high(b + 1)

            batches(act, batch)

        @block.vector
        def _(dve):
            for s in (h_ready, h_lo, added):
                dve.sem_inc(s, 2)

            def norms(b):
                for t in range(TB):
                    normalise(nc, g, Y[:, t], b * TB + t).then_inc(normed, 1)

            def y_low(b):
                for e in range(EC):
                    dve.wait_ge(y_hi, b * EC + e + 1)
                    nc.vector.scalar_tensor_tensor(out=yT[:, 1, e], in0=g.PS[:, e, :], scalar=Y_UP, in1=yT[:, 0, e],
                                                   op0=ALU.mult, op1=ALU.subtract).then_inc(y_lo, 1)

            def h_low(b, n):
                dve.wait_ge(h_ready, b * HC + n + 3)
                dve.wait_ge(h_hi, b * HC + n + 3)
                nc.vector.tensor_tensor(hT[:, 1, n], h[:, n % 2], hT[:, 0, n], ALU.subtract).then_inc(h_lo, 1)

            norms(0)
            dve.wait_ge(w_in, 48)
            nc.vector.tensor_copy(w[:, 0:gates // 2], raw[:, 0:gates // 2]).then_inc(w_ready, 1)
            y_low(0)

            def batch(b, more):
                if more:
                    dve.wait_ge(turned, b * EC + EC)
                    norms(b + 1)
                for n in range(HC):
                    dve.wait_ge(silu_done, b * HC + n + 1)
                    dve.wait_ge(h_ready, b * HC + n + 1)
                    dve.wait_ge(h_hi, b * HC + n + 1)
                    dve.wait_ge(h_lo, b * HC + n + 1)
                    nc.vector.scalar_tensor_tensor(out=h[:, n % 2], in0=g.PS[:, 3 + 2 * (n % 2), :],
                                                   scalar=FFN_SCALE / Y_UP * H_DOWN, in1=gate[:, n % 2],
                                                   op0=ALU.mult, op1=ALU.mult).then_inc(h_ready, 1)
                    if n:
                        h_low(b, n - 1)
                h_low(b, HC - 1)
                if more:
                    y_low(b + 1)
                for t in range(TB):
                    at = b * TB + t
                    dve.wait_ge(down_done, at + 1)
                    hh = g.H[:, bass.ds(at, 1), :].rearrange("p a e -> p (a e)")
                    nc.vector.scalar_tensor_tensor(out=hh, in0=g.PS[:, 6 + t % 2, 0:E], scalar=FFN_SCALE / H_DOWN, in1=hh,
                                                   op0=ALU.mult, op1=ALU.add).then_inc(added, 1)
                    if t:
                        dve.wait_ge(added, at + 2)
                        statistics(nc, g, at - 1)
                dve.wait_ge(added, b * TB + TB + 2)
                statistics(nc, g, b * TB + TB - 1)

            batches(dve, batch)


def sparse_attention(nc, g, Wq, bq, Wk, bk, Wv, bv, Wo, bo):
    with ExitStack() as c:
        sb = lambda n, s, d=F32: c.enter_context(nc.sbuf_tensor("t_" + n, s, d))
        W = sb("W", [P, 4, EC, E])
        bqk, bvo = sb("bqk", [P, 2, EC]), sb("bvo", [P, 2, E])
        mask = sb("mask", [P, S])
        Y, yT, qkT, V1 = sb("Y", [P, TB, E]), sb("yT", [P, EC, S]), sb("qkT", [P, 2, 2, EC, S]), sb("V1", [P, 2, TB, E])
        sc, left, ex, pr = sb("sc", [P, S]), sb("left", [P, S]), sb("ex", [P, 2, S]), sb("pr", [P, 2, S])
        top, ntop, total, rec = sb("top", [P, TOPK]), sb("ntop", [P, 2]), sb("total", [P, TB]), sb("rec", [P, TB])
        pT, avT = sb("pT", [P, TB, S]), sb("avT", [P, EC, S])
        sem = lambda n: g.sem("t_" + n)
        w_in, masked, normed, biased, turned, copied, qk_done, qk_ready, v_done, v_ready = (sem(n) for n in (
            "w_in", "masked", "normed", "biased", "turned", "copied", "qk_done", "qk_ready", "v_done", "v_ready"))
        s_done, s_ready, top_ready, exped, p_ready, p_turned, p_copied, av_done, av_ready, o_done, added, chain, norm_ready = (
            sem(n) for n in ("s_done", "s_ready", "top_ready", "exped", "p_ready", "p_turned", "p_copied", "av_done",
                             "av_ready", "o_done", "added", "chain", "norm_ready"))
        waited = g.sem("t_waited")
        block = c.enter_context(nc.Block())
        LINKS = 2 * TB + 1

        @block.sync
        def _(sp):
            for n, src in enumerate((Wq, Wk, Wv, Wo)):
                sp.dma_start(W[:, n], src.rearrange("(c p) n -> p c n", p=P)).then_inc(w_in, 16)
            for n, src in enumerate((bq, bk)):
                sp.dma_start(bqk[:, n, :], src).then_inc(w_in, 16)
            for n, src in enumerate((bv, bo)):
                sp.dma_start(bvo[:, n, :], row(src)).then_inc(w_in, 16)

        @block.gpsimd
        def _(pool):
            st = Steps(pool, masked)
            st.link(nc.gpsimd.memset(mask[:], 0.0))
            st.link(nc.gpsimd.affine_select(out=mask[:, S - P:], in_=mask[:, S - P:], compare_op=ALU.is_ge, fill=NEG,
                                            base=0, pattern=[[-1, P]], channel_multiplier=1))
            pool.wait_ge(w_in, 16 * 8)
            with pool.Fori(0, B) as b:
                pool.wait_ge(normed, b * TB + TB)
                h = g.H[:, bass.ds(b * TB, TB), :]
                nc.gpsimd.tensor_tensor(h, h, bvo[:, 1].unsqueeze(1).broadcast_to([P, TB, E]), ALU.add).then_inc(biased, 1)

        def in_steps(eng, step):
            step(0, 0, True, False)
            with eng.Fori(0, B // 2 - 1) as n:
                step(n * 2 + 1, 1, True, True)
                step(n * 2 + 2, 0, True, True)
            step(B - 1, 1, False, True)

        @block.tensor
        def _(pe):
            pe.sem_inc(p_turned, 2)
            pe.wait_ge(w_in, 16 * 8)

            def turn(b):
                pe.wait_ge(normed, b * TB + TB)
                pe.wait_ge(av_ready, b * EC + EC)
                turn_batch(pe, nc, g, Y, 0, turned)

            def queries_keys(b, half, x):
                for d in range(EC):
                    if x == 0:
                        pe.wait_ge(copied, b * EC + EC)
                    else:
                        pe.wait_ge(qk_ready, b * 4 + d + 1)
                    for e in range(EC):
                        last = nc.tensor.matmul(g.PS[:, d, :], W[:, x, e, d * P:(d + 1) * P], yT[:, e],
                                                start=(e == 0), stop=(e == EC - 1))
                    last.then_inc(qk_done, 1)

            def values(b):
                for n in range(2):
                    pe.wait_ge(qk_ready, b * 4 + n + 3)
                    for t in (2 * n, 2 * n + 1):
                        for e in range(EC):
                            last = nc.tensor.matmul(g.PS[:, n, t % 2 * E:(t % 2 + 1) * E], yT[:, e, t * P:(t + 1) * P],
                                                    W[:, 2, e], start=(e == 0), stop=(e == EC - 1))
                    last.then_inc(v_done, 1)

            def scores(b, half, t):
                w = (t + 1) * P
                pe.wait_ge(qk_ready, b * 4 + 4)
                pe.wait_ge(s_ready, b * TB + t + 1)
                for d in range(EC):
                    last = nc.tensor.matmul(g.PS[:, 2 + t % 2, 0:w], qkT[:, half, 0, d, t * P:w], qkT[:, half, 1, d, 0:w],
                                            start=(d == 0), stop=(d == EC - 1))
                last.then_inc(s_done, 1)

            def turn_probs(b, t):
                pe.wait_ge(p_ready, b * TB + t + 1)
                pe.wait_ge(p_copied, b * TB + t + 1)
                for k in range(t + 1):
                    last = nc.tensor.transpose(g.PS[:, 4 + t % 2, k * P:(k + 1) * P], pr[:, t % 2, k * P:(k + 1) * P],
                                               g.identf[:])
                last.then_inc(p_turned, 1)

            def weighted(b, half, ahead):
                pe.wait_ge(p_copied, b * TB + TB + 2)
                pe.wait_ge(v_ready, b * 2 + (4 if ahead else 2))
                for d in range(EC):
                    for k in range(TB):
                        last = nc.tensor.matmul(g.PS[:, d, k * P:S], V1[:, half, k, d * P:(d + 1) * P], pT[:, k, k * P:S],
                                                start=(k == 0), stop=(k == TB - 1))
                    last.then_inc(av_done, 1)

            def projected(b):
                pe.wait_ge(av_ready, b * EC + 3 * EC)
                for t in range(TB):
                    pe.wait_ge(added, b * TB + t + 1)
                    for d in range(EC):
                        last = nc.tensor.matmul(g.PS[:, 6 + t % 2, 0:E], avT[:, d, t * P:(t + 1) * P], W[:, 3, d],
                                                start=(d == 0), stop=(d == EC - 1))
                    last.then_inc(o_done, 1)

            turn(0)
            queries_keys(0, 0, 0)
            queries_keys(0, 0, 1)
            values(0)

            def step(b, half, ahead, behind):
                scores(b, half, 0)
                scores(b, half, 1)
                if behind:
                    projected(b - 1)
                if ahead:
                    turn(b + 1)
                    queries_keys(b + 1, 1 - half, 0)
                turn_probs(b, 0)
                scores(b, half, 2)
                scores(b, half, 3)
                if ahead:
                    queries_keys(b + 1, 1 - half, 1)
                turn_probs(b, 1)
                if ahead:
                    values(b + 1)
                turn_probs(b, 2)
                turn_probs(b, 3)
                weighted(b, half, ahead)

            in_steps(pe, step)
            projected(B - 1)

        @block.scalar
        def _(act):
            nc.scalar.preload_act_table(ACT.Exp)
            act.sem_inc(p_copied, 2)
            act.sem_inc(av_ready, 2 * EC)
            act.wait_ge(w_in, 16 * 8)

            def copy_y(b):
                for e in range(EC):
                    act.wait_ge(turned, b * EC + e + 1)
                    nc.scalar.activation(yT[:, e], g.PS[:, e, :], ACT.Copy).then_inc(copied, 1)

            def copy_queries_keys(b, half, x):
                for d in range(EC):
                    act.wait_ge(qk_done, b * 4 + 2 * x + d + 1)
                    nc.scalar.activation(qkT[:, half, x, d], g.PS[:, d, :], ACT.Identity,
                                         bias=bqk[:, x, d:d + 1]).then_inc(qk_ready, 1)

            def exponentials(b, t):
                w = (t + 1) * P
                act.wait_ge(top_ready, b * TB + t + 1)
                nc.scalar.activation(ex[:, t % 2, 0:w], sc[:, 0:w], ACT.Exp, bias=ntop[:, t % 2:t % 2 + 1]).then_inc(exped, 1)

            def copy_probs(b, t):
                act.wait_ge(p_turned, b * TB + t + 3)
                nc.scalar.activation(pT[:, 0:t + 1, t * P:(t + 1) * P],
                                     g.PS[:, 4 + t % 2, 0:(t + 1) * P].rearrange("p (k q) -> p k q", q=P),
                                     ACT.Copy).then_inc(p_copied, 1)

            copy_y(0)
            copy_queries_keys(0, 0, 0)
            copy_queries_keys(0, 0, 1)

            def step(b, half, ahead, behind):
                exponentials(b, 0)
                if ahead:
                    copy_y(b + 1)
                exponentials(b, 1)
                if ahead:
                    copy_queries_keys(b + 1, 1 - half, 0)
                copy_probs(b, 0)
                exponentials(b, 2)
                if ahead:
                    copy_queries_keys(b + 1, 1 - half, 1)
                copy_probs(b, 1)
                exponentials(b, 3)
                copy_probs(b, 2)
                copy_probs(b, 3)
                for d in range(EC):
                    act.wait_ge(av_done, b * EC + d + 1)
                    nc.scalar.activation(avT[:, d], g.PS[:, d, :], ACT.Copy).then_inc(av_ready, 1)

            in_steps(act, step)

        @block.vector
        def _(dve):
            for s in (s_ready, added):
                dve.sem_inc(s, 2)

            def norms(b, first=False):
                if not first:
                    dve.wait_ge(turned, b * EC)
                for t in range(TB):
                    normalise(nc, g, Y[:, t], b * TB + t).then_inc(normed, 1)

            def copy_values(b, half):
                for n in range(2):
                    dve.wait_ge(v_done, b * 2 + n + 1)
                    nc.vector.tensor_tensor(V1[:, half, 2 * n:2 * n + 2], g.PS[:, n, :].rearrange("p (t e) -> p t e", t=2),
                                            bvo[:, 0:1].broadcast_to([P, 2, E]), ALU.add).then_inc(v_ready, 1)

            def largest(b, t, st):
                w = (t + 1) * P
                dve.wait_ge(s_done, b * TB + t + 1)
                nc.vector.scalar_tensor_tensor(out=sc[:, 0:w], in0=g.PS[:, 2 + t % 2, 0:w], scalar=E ** -0.5,
                                               in1=mask[:, S - w:], op0=ALU.mult, op1=ALU.add).then_inc(s_ready, 1)
                dve.wait_ge(s_ready, b * TB + t + 3)
                dve.sem_inc(waited, 1)
                st.link(nc.vector.max(out=top[:], in_=sc[:, 0:w]))
                nc.vector.tensor_single_scalar(ntop[:, t % 2:t % 2 + 1], top[:, 0:1], -1.0, ALU.mult).then_inc(top_ready, 1)
                st.link(nc.vector.match_replace(out=left[:, 0:w], in_to_replace=top[:], in_values=sc[:, 0:w],
                                                imm_value=GONE))
                dve.wait_ge(exped, b * TB + t + 1)
                dve.wait_ge(p_turned, b * TB + t + 1)
                nc.vector.scalar_tensor_tensor(out=pr[:, t % 2, 0:w], in0=left[:, 0:w], scalar=GONE / 2, in1=ex[:, t % 2, 0:w],
                                               op0=ALU.is_lt, op1=ALU.mult, accum_out=total[:, t:t + 1]).then_inc(p_ready, 1)

            def add(b):
                dve.wait_ge(biased, b + 1)
                for t in range(TB):
                    at = b * TB + t
                    dve.wait_ge(o_done, at + 1)
                    h = g.H[:, bass.ds(at, 1), :].rearrange("p a e -> p (a e)")
                    nc.vector.scalar_tensor_tensor(out=h, in0=g.PS[:, 6 + t % 2, 0:E], scalar=rec[:, t:t + 1], in1=h,
                                                   op0=ALU.mult, op1=ALU.add).then_inc(added, 1)
                    if t:
                        dve.wait_ge(added, at + 2)
                        statistics(nc, g, at - 1)
                dve.wait_ge(added, b * TB + TB + 2)
                statistics(nc, g, b * TB + TB - 1)

            norms(0, first=True)
            dve.wait_ge(w_in, 16 * 8)
            dve.wait_ge(masked, 2)
            copy_values(0, 0)

            def step(b, half, ahead, behind):
                st = Steps(dve, chain, b, LINKS)
                if ahead:
                    norms(b + 1)
                largest(b, 0, st)
                if behind:
                    add(b - 1)
                for t in (1, 2, 3):
                    largest(b, t, st)
                if ahead:
                    copy_values(b + 1, 1 - half)
                dve.wait_ge(p_ready, b * TB + TB)
                st.link(nc.vector.reciprocal(rec[:], total[:]))

            in_steps(dve, step)
            add(B - 1)




UNROLL, LEAD = 8, 6


def choose_experts(nc, g, YA, chosen, router_wT, router_b):
    with ExitStack() as c:
        sb = lambda n, s, d=F32: c.enter_context(nc.sbuf_tensor("r_" + n, s, d))
        rw, rb = sb("rw", [P, EC, EXPERTS]), sb("rb", [P, EXPERTS])
        left, leftf = sb("left", [P, EXPERTS], I32), sb("leftf", [P, EXPERTS])
        Y, yT = sb("Y", [P, 2, TB, E]), sb("yT", [P, 2, EC, S])
        logit, best, first = sb("logit", [P, T, EXPERTS]), sb("best", [P, T]), sb("first", [P, T])
        sem = lambda n: g.sem("r_" + n)
        w_in, left_ready, normed, kept, turned, copied, l_done, l_read, chain = (sem(n) for n in (
            "w_in", "left_ready", "normed", "kept", "turned", "copied", "l_done", "l_read", "chain"))
        block = c.enter_context(nc.Block())
        full = [P, T, EXPERTS]

        @block.sync
        def _(sp):
            sp.dma_start(rw[:], router_wT.rearrange("(c p) x -> p c x", p=P)).then_inc(w_in, 16)
            sp.dma_start(rb[:], row(router_b)).then_inc(w_in, 16)

        @block.gpsimd
        def _(pool):
            nc.gpsimd.iota(left[:], pattern=[[-1, EXPERTS]], base=EXPERTS, channel_multiplier=0).then_inc(left_ready, 1)
            with pool.Fori(0, B // 2) as n:
                for half in range(2):
                    b = n * 2 + half
                    pool.wait_ge(normed, b * TB + TB)
                    nc.gpsimd.tensor_copy(YA[:, bass.ds(b * TB, TB), :], Y[:, half]).then_inc(kept, 1)

        @block.tensor
        def _(pe):
            pe.sem_inc(l_read, 2)
            pe.wait_ge(w_in, 32)

            def turn(b, half):
                pe.wait_ge(normed, b * TB + TB)
                turn_batch(pe, nc, g, Y[:, half], 2 * half, turned)

            def logits(b, half):
                pe.wait_ge(copied, b * EC + EC)
                pe.wait_ge(l_read, b + 1)
                for t in range(TB):
                    for e in range(EC):
                        last = nc.tensor.matmul(g.PS[:, 4 + half, t * EXPERTS:(t + 1) * EXPERTS],
                                                yT[:, half, e, t * P:(t + 1) * P], rw[:, e], start=(e == 0), stop=(e == EC - 1))
                last.then_inc(l_done, 1)

            turn(0, 0)
            with pe.Fori(0, B // 2 - 1) as n:
                for half in range(2):
                    turn(n * 2 + half + 1, 1 - half)
                    logits(n * 2 + half, half)
            turn(B - 1, 1)
            logits(B - 2, 0)
            logits(B - 1, 1)

        @block.scalar
        def _(act):
            with act.Fori(0, B // 2) as n:
                for half in range(2):
                    b = n * 2 + half
                    for e in range(EC):
                        act.wait_ge(turned, b * EC + 2 * EC + e + 1)
                        act.wait_ge(l_read, b + 1)
                        nc.scalar.activation(yT[:, half, e], g.PS[:, 2 * half + e, :], ACT.Copy).then_inc(copied, 1)

        @block.vector
        def _(dve):
            dve.sem_inc(kept, 2)
            dve.sem_inc(turned, 2 * EC)
            dve.wait_ge(w_in, 32)
            dve.wait_ge(left_ready, 1)
            nc.vector.tensor_copy(leftf[:], left[:]).then_inc(chain, 1)
            dve.wait_ge(chain, 1)

            def norms(b, half):
                dve.wait_ge(kept, b + 1)
                dve.wait_ge(turned, b * EC + EC)
                for t in range(TB):
                    normalise(nc, g, Y[:, half, t], b * TB + t).then_inc(normed, 1)

            def read(b, half):
                dve.wait_ge(l_done, b + 1)
                nc.vector.tensor_tensor(logit[:, bass.ds(b * TB, TB), :],
                                        g.PS[:, 4 + half, 0:TB * EXPERTS].rearrange("p (t x) -> p t x", t=TB),
                                        rb[:].unsqueeze(1).broadcast_to([P, TB, EXPERTS]), ALU.add).then_inc(l_read, 1)

            norms(0, 0)
            norms(1, 1)
            with dve.Fori(0, B // 2 - 1) as n:
                for half in range(2):
                    norms(n * 2 + half + 2, half)
                    read(n * 2 + half, half)
            read(B - 2, 0)
            read(B - 1, 1)
            dve.wait_ge(l_read, B + 2)
            st = Steps(dve, chain, base=1)
            st.link(nc.vector.tensor_reduce(best[:], logit[:], AX, ALU.max))
            st.link(nc.vector.tensor_tensor(logit[:], logit[:], best[:].unsqueeze(2).broadcast_to(full), ALU.is_ge))
            st.link(nc.vector.tensor_tensor(logit[:], logit[:], leftf[:].unsqueeze(1).broadcast_to(full), ALU.mult))
            st.link(nc.vector.tensor_reduce(first[:], logit[:], AX, ALU.max))
            nc.vector.tensor_tensor(chosen[:].rearrange("p x t -> p t x"), logit[:],
                                    first[:].unsqueeze(2).broadcast_to(full), ALU.is_equal)


def slots_by_expert(nc, g, chosen, slots, tile_expert, b1s, b1):
    with ExitStack() as c:
        sb = lambda n, s, d=F32: c.enter_context(nc.sbuf_tensor("s_" + n, s, d))
        tri, ones = sb("tri", [P, P], BF16), sb("ones", [P, P], BF16)
        number, numberf = sb("number", [P, SLOT_TILES], I32), sb("numberf", [P, SLOT_TILES])
        within = sb("within", [P, EXPERTS, T])
        upto, before = sb("upto", [P, EXPERTS, T]), sb("before", [P, EXPERTS, T])
        tiles, ends, starts, base = (sb(n, [P, EXPERTS]) for n in ("tiles", "ends", "starts", "base"))
        row_of, reached, expert = sb("row_of", [P, T]), sb("reached", [1, SLOT_TILES, EXPERTS]), sb("expert", [1, SLOT_TILES])
        bounds, hot, bias1 = sb("bounds", [EXPERTS, 2]), sb("hot", [EXPERTS, SLOT_TILES]), sb("bias1", [EXPERTS, EH])
        sem = lambda n: g.sem("s_" + n)
        b_in, made, counted, ends_ready, ends_turned, hot_ready, b_done, chain = (sem(n) for n in (
            "b_in", "made", "counted", "ends_ready", "ends_turned", "hot_ready", "b_done", "chain"))
        block = c.enter_context(nc.Block())
        flat = lambda a: a.rearrange("p x t -> p (x t)")
        banks = lambda n: g.PS[:, n:n + 2, :].rearrange("p a c -> p (a c)")
        prefix, counts = banks(0), banks(2)

        @block.sync
        def _(sp):
            sp.dma_start(bias1[:], b1).then_inc(b_in, 16)

        @block.gpsimd
        def _(pool):
            st = Steps(pool, made)
            st.link(nc.gpsimd.memset(tri[:], 1.0))
            st.link(nc.gpsimd.affine_select(out=tri[:], in_=tri[:], compare_op=ALU.is_ge, fill=0.0, base=-1,
                                            pattern=[[1, P]], channel_multiplier=-1))
            st.link(nc.gpsimd.memset(ones[:], 1.0))
            st.link(nc.gpsimd.memset(within[:], 1.0))
            st.link(nc.gpsimd.memset(within[:, :, 0:1], 0.0))
            st.link(nc.gpsimd.iota(number[:], pattern=[[1, SLOT_TILES]], base=0, channel_multiplier=0))

        @block.tensor
        def _(pe):
            pe.wait_ge(made, 3)
            for n, left in ((0, tri), (2, ones)):
                for h in range(2):
                    last = nc.tensor.matmul(g.PS[:, n + h, :], left[:], flat(chosen[:])[:, h * 512:(h + 1) * 512],
                                            start=True, stop=True)
            last.then_inc(counted, 1)
            pe.wait_ge(ends_ready, 1)
            for n, x in enumerate((ends, starts)):
                last = nc.tensor.transpose(g.PS[0:EXPERTS, 4, n * EXPERTS:(n + 1) * EXPERTS], x[0:EXPERTS, :],
                                           g.identf[0:EXPERTS, 0:EXPERTS])
            last.then_inc(ends_turned, 1)
            pe.wait_ge(hot_ready, 1)
            pe.wait_ge(b_in, 16)
            nc.tensor.matmul(g.PS[0:EH, 5, 0:SLOT_TILES], bias1[:], hot[:], start=True, stop=True).then_inc(b_done, 1)

        @block.vector
        def _(dve):
            v = nc.vector
            st = Steps(dve, chain)
            dve.wait_ge(made, 6)
            st.link(v.tensor_copy(numberf[:], number[:]))
            dve.wait_ge(counted, 1)
            st.link(v.tensor_tensor_scan(flat(upto[:]), flat(within[:]), counts, 0.0, ALU.mult, ALU.add))
            st.link(v.tensor_scalar(tiles[:], upto[:, :, T - 1], 1.0 / P, 63.5 / P, ALU.mult, ALU.add))
            st.link(v.tensor_single_scalar(tiles[:], tiles[:], ROUND, ALU.add))
            st.link(v.tensor_single_scalar(tiles[:], tiles[:], ROUND, ALU.subtract))
            st.link(v.tensor_tensor_scan(ends[:], within[:, 0, 1:2].broadcast_to([P, EXPERTS]), tiles[:], 0.0, ALU.mult, ALU.add))
            v.tensor_tensor(starts[:], ends[:], tiles[:], ALU.subtract).then_inc(ends_ready, 1)
            st.link(v.tensor_tensor(flat(before[:]), flat(upto[:]), counts, ALU.subtract))
            st.link(v.tensor_tensor(flat(before[:]), flat(before[:]), prefix, ALU.add))
            dve.wait_ge(ends_ready, 1)
            st.link(v.tensor_single_scalar(base[:], starts[:], float(P), ALU.mult))
            st.link(v.tensor_tensor(before[:], before[:], base[:].unsqueeze(2).broadcast_to([P, EXPERTS, T]), ALU.add))
            st.link(v.tensor_tensor(before[:], before[:], chosen[:], ALU.mult))
            st.link(v.tensor_reduce(row_of[:], before[:].rearrange("p x t -> p t x"), AX, ALU.add))
            v.tensor_copy(slots[:], row_of[:])
            dve.wait_ge(ends_turned, 1)
            st.link(v.tensor_copy(bounds[:], g.PS[0:EXPERTS, 4, 0:2 * EXPERTS:EXPERTS]))
            st.link(v.tensor_scalar(hot[:], numberf[0:EXPERTS, :], bounds[:, 1:2], None, ALU.is_ge))
            v.scalar_tensor_tensor(out=hot[:], in0=numberf[0:EXPERTS, :], scalar=bounds[:, 0:1], in1=hot[:],
                                   op0=ALU.is_lt, op1=ALU.mult).then_inc(hot_ready, 1)
            full = [1, SLOT_TILES, EXPERTS]
            st.link(v.tensor_tensor(reached[:], numberf[0:1].unsqueeze(2).broadcast_to(full),
                                    ends[0:1].unsqueeze(1).broadcast_to(full), ALU.is_ge))
            st.link(v.tensor_reduce(expert[:], reached[:], AX, ALU.add))
            v.tensor_single_scalar(tile_expert[:], expert[:], float(EXPERTS - 1), ALU.min)
            dve.wait_ge(b_done, 1)
            v.tensor_copy(b1s[:], g.PS[0:EH, 5, 0:SLOT_TILES])


def expert_tiles(nc, g, out, YA, YS, RS, slots, tile_expert, b1s, W1, W2):
    with ExitStack() as c:
        sb = lambda n, s, d=F32: c.enter_context(nc.sbuf_tensor("e_" + n, s, d))
        y, w1, w2 = sb("y", [P, UNROLL, E]), sb("w1", [P, UNROLL, EC, EH]), sb("w2", [EH + 1, UNROLL, E])
        yT, hT, res = sb("yT", [P, 2, EC, P]), sb("hT", [EH + 1, 2, P]), sb("res", [P, UNROLL, E])
        sem = lambda n: g.sem("e_" + n)
        scattered, ones_made, turned, copied, h_done, h_ready, y_done, res_ready = (sem(n) for n in (
            "scattered", "ones_made", "turned", "copied", "h_done", "h_ready", "y_done", "res_ready"))
        added, written = sem("added"), sem("written")
        w_in = [sem(f"w_in{j}") for j in range(UNROLL)]
        y_in, stored = ({j: sem(f"{n}{j}") for j in range(0, UNROLL, 2)} for n in ("y_in", "stored"))
        gathered = [sem(f"gathered{b}") for b in range(B)]
        block = c.enter_context(nc.Block())
        BODIES = SLOT_TILES // UNROLL
        two_tiles = lambda ap, s: ap[bass.ds(s, 2)].rearrange("a p e -> p a e")

        def bodies(eng, body):
            with eng.Fori(0, BODIES - 1) as i:
                body(i, True)
            body(BODIES - 1, False)

        @block.sync
        def _(sp):
            def load(s, j):
                e = sp.value_load(tile_expert[0:1, bass.ds(s, 1)], min_val=0, max_val=EXPERTS - 1)
                sp.wait_ge(y_done, s + 1)
                sp.dma_start(w1[:, j], W1[bass.ds(e, 1)].rearrange("a p c h -> (a p) c h")).then_inc(w_in[j], 16)
                sp.dma_start(w2[:, j], W2[bass.ds(e, 1)].rearrange("a h e -> (a h) e")).then_inc(w_in[j], 16)

            with sp.Fori(0, BODIES) as i:
                for j in range(UNROLL):
                    load(i * UNROLL + j, j)
            o = out.rearrange("b (t p) e -> b p t e", p=P)
            for b in range(B):
                sp.wait_ge(added, b + 1)
                sp.dma_start(o[b], YA[:, b * TB:(b + 1) * TB, :]).then_inc(written, 16)
            sp.wait_ge(written, 16 * B)

        @block.gpsimd
        def _(pool):
            rows = YS.rearrange("a p e -> (a p) e")
            for t in range(T):
                nc.gpsimd.indirect_dma_start(out=rows, out_offset=bass.IndirectOffsetOnAxis(ap=slots[:, t:t + 1], axis=0),
                                             in_=YA[:, t, :], in_offset=None).then_inc(scattered, 16)
            for j in range(0, UNROLL, 2):
                pool.wait_ge(stored[j], 16 * BODIES + 16)
            rows = RS.rearrange("a p e -> (a p) e")
            for t in range(T):
                nc.gpsimd.indirect_dma_start(out=YA[:, t, :], out_offset=None, in_=rows,
                                             in_offset=bass.IndirectOffsetOnAxis(ap=slots[:, t:t + 1], axis=0)
                                             ).then_inc(gathered[t // TB], 16)

        @block.tensor
        def _(pe):
            pe.sem_inc(y_done, UNROLL)
            pe.sem_inc(h_done, 2)

            def turn(i, s, j):
                pe.wait_ge(w_in[j], i * 32 + 32)
                if j % 2 == 0:
                    pe.wait_ge(y_in[j], i * 16 + 16)
                pe.wait_ge(copied, s + 1)
                for e in range(EC):
                    last = nc.tensor.transpose(g.PS[:, j % 2, e * P:(e + 1) * P], y[:, j, e * P:(e + 1) * P], g.identf[:])
                last.then_inc(turned, 1)

            def first(s, j):
                pe.wait_ge(copied, s + 3)
                pe.wait_ge(h_ready, s + 1)
                for e in range(EC):
                    last = nc.tensor.matmul(g.PS[0:EH, 2 + j % 2, 0:P], w1[:, j, e], yT[:, j % 2, e],
                                            start=(e == 0), stop=(e == EC - 1))
                last.then_inc(h_done, 1)

            def second(s, j):
                pe.wait_ge(h_ready, s + 3)
                pe.wait_ge(res_ready, s + 1)
                nc.tensor.matmul(g.PS[:, 4 + j % 2, 0:E], hT[:, j % 2], w2[:, j], start=True, stop=True).then_inc(y_done, 1)

            turn(0, 0, 0)
            turn(0, 1, 1)
            first(0, 0)

            def body(i, more):
                for j in range(UNROLL):
                    s = i * UNROLL + j
                    if more or j + 2 < UNROLL:
                        turn(i + (j + 2) // UNROLL, s + 2, (j + 2) % UNROLL)
                    if more or j + 1 < UNROLL:
                        first(s + 1, (j + 1) % UNROLL)
                    second(s, j)

            bodies(pe, body)

        @block.scalar
        def _(act):
            for j in range(0, UNROLL, 2):
                act.sem_inc(stored[j], 16)

            def load(s, j):
                act.wait_ge(y_done, s + 2)
                act.dma_start(y[:, j:j + 2], two_tiles(YS, s)).then_inc(y_in[j], 16)

            def store(s, j):
                act.wait_ge(res_ready, s + 4)
                act.dma_start(two_tiles(RS, s), res[:, j:j + 2]).then_inc(stored[j], 16)

            act.wait_ge(scattered, 16 * T)
            for s in range(0, LEAD, 2):
                load(s, s)

            def body(i, more):
                for j in range(0, UNROLL, 2):
                    s = i * UNROLL + j
                    if more or j + LEAD < UNROLL:
                        load(s + LEAD, (j + LEAD) % UNROLL)
                    store(s, j)

            bodies(act, body)

        @block.vector
        def _(dve):
            dve.sem_inc(h_ready, 2)
            dve.sem_inc(copied, 2)
            dve.sem_inc(res_ready, 2)
            nc.vector.memset(hT[EH:EH + 1], 1.0).then_inc(ones_made, 1)
            dve.wait_ge(ones_made, 1)

            def copy(s, j):
                dve.wait_ge(turned, s + 1)
                dve.wait_ge(h_done, s + 1)
                nc.vector.tensor_copy(yT[:, j % 2], g.PS[:, j % 2, 0:E].rearrange("p (c n) -> p c n", c=EC)).then_inc(copied, 1)

            def relu(s, j):
                dve.wait_ge(h_done, s + 3)
                dve.wait_ge(y_done, s + UNROLL - 1)
                nc.vector.tensor_scalar(hT[0:EH, j % 2], g.PS[0:EH, 2 + j % 2, 0:P], b1s[:, bass.ds(s, 1)], 0.0,
                                        ALU.add, ALU.max).then_inc(h_ready, 1)

            copy(0, 0)
            copy(1, 1)
            relu(0, 0)

            def body(i, more):
                for j in range(UNROLL):
                    s = i * UNROLL + j
                    if more or j + 2 < UNROLL:
                        copy(s + 2, (j + 2) % UNROLL)
                    if more or j + 1 < UNROLL:
                        relu(s + 1, (j + 1) % UNROLL)
                    dve.wait_ge(y_done, s + UNROLL + 1)
                    if j % 2 == 0:
                        dve.wait_ge(stored[j], i * 16 + 16)
                    nc.vector.tensor_single_scalar(res[:, j], g.PS[:, 4 + j % 2, 0:E], 0.0, ALU.max).then_inc(res_ready, 1)

            bodies(dve, body)
            for b in range(B):
                dve.wait_ge(gathered[b], 16 * TB)
                ts = slice(b * TB, (b + 1) * TB)
                nc.vector.tensor_tensor(YA[:, ts], YA[:, ts], g.H[:, ts], ALU.add).then_inc(added, 1)


def routed_experts(nc, g, out, YS, router_wT, router_b, W1, b1, W2):
    with ExitStack() as c:
        sb = lambda n, s, d=F32: c.enter_context(nc.sbuf_tensor(n, s, d))
        YA, chosen = sb("YA", [P, T, E]), sb("chosen", [P, EXPERTS, T], BF16)
        slots, tile_expert, b1s = sb("slots", [P, T], I32), sb("tile_expert", [1, SLOT_TILES], I32), sb("b1s", [EH, SLOT_TILES])
        RS = nc.dram_tensor("RS", (SLOT_TILES, P, E), F32, kind="Internal").ap()
        choose_experts(nc, g, YA, chosen, router_wT, router_b)
        slots_by_expert(nc, g, chosen, slots, tile_expert, b1s, b1)
        expert_tiles(nc, g, out, YA, YS, RS, slots, tile_expert, b1s, W1, W2)


class Buffers:

    def __init__(self, nc):
        self.nc, self.sems = nc, []

    def sem(self, name):
        self.sems.append(self.nc.alloc_semaphore(name))
        return self.sems[-1]

    def free_sems(self):
        self.nc.clear_and_free_semaphores(self.sems)
        self.nc.all_engine_barrier()
        self.sems = []
def tower(nc, a, out):
    with ExitStack() as c:
        g=Buffers(nc)
        sb = lambda n, s, d: c.enter_context(nc.sbuf_tensor(n, s, d))
        g.H=sb('H',[P,T,E],F32); g.V=sb('V',[P,T,E],BF16)
        g.ident=sb('ident',[P,P],BF16); g.identf=sb('identf',[P,P],F32); g.mask_q=sb('mask_q',[P,P],BF16); g.mask_k=sb('mask_k',[P,P],BF16)
        g.stats=sb('stats',[P,T,6],F32); g.mean=sb('mean',[P,T],F32); g.rstd=sb('rstd',[P,T],F32)
        g.WA=sb('WA',[P,EC,3*E],BF16); g.WP=sb('WP',[P,EC,E],BF16)
        g.PS=c.enter_context(nc.psum_tensor('PS',[P,8,512],F32))
        g.QT=nc.dram_tensor('QT',(NG,P,S),BF16,kind='Internal').ap()
        g.KT=nc.dram_tensor('KT',(NG,P,S),BF16,kind='Internal').ap()
        constants_and_tokens(nc,g,a['x'],a['L0_tok_weights'])
        with ExitStack() as c2:
            sb2 = lambda n, s, d: c2.enter_context(nc.sbuf_tensor(n, s, d))
            X=sb2('X',[P,T,E],F32); XQ=sb2('XQ',[P,T,E],BF16); xs=sb2('xs',[P,T],F32)
            layernorm(nc,g,X[:],'a_')
            quantise(nc,g,X[:],XQ[:],T,E,xs[:],False,'x_')
            weights_quantised(nc,g,a['L0_attn_w_attn'],a['L0_attn_w_proj'])
            qkv_quantised(nc,g,XQ,xs,a['L0_attn_b_attn'])
        with ExitStack() as c2:
            O=c2.enter_context(nc.sbuf_tensor('O',[P,T,E],F32))
            small = lambda n: c2.enter_context(nc.sbuf_tensor(n, [P,TB,NG,HG], F32))[:]
            neg_max, sums, lse, key_max, key_scale, key_ln, q_max, q_scale, q_ln = (small(n) for n in ('neg_max','sums','lse','key_max','key_scale','key_ln','q_max','q_scale','q_ln'))
            score_maxima(nc,g,neg_max,True,sums,'sa_')
            log_sums(nc,g,lse,neg_max,sums)
            row_terms(nc,g,lse,g.QT,HD,'ra_')
            score_maxima(nc,g,key_max,False,None,'sb_')
            log_scales(nc,g,key_scale,key_ln,key_max,None,'lb_')
            row_terms(nc,g,key_ln,g.KT,HD+3,'rb_')
            scale_values(nc,g,key_scale)
            score_maxima(nc,g,q_max,True,None,'sc_')
            log_scales(nc,g,q_scale,q_ln,q_max,lse,'lc_')
            row_terms(nc,g,q_ln,g.QT,HD,'rc_')
            weighted_values(nc,g,O,q_scale)
            OQ=c2.enter_context(nc.sbuf_tensor('OQ',[P,T,E],BF16)); os=c2.enter_context(nc.sbuf_tensor('os',[P,T],F32))
            quantise(nc,g,O[:],OQ[:],T,E,os[:],False,'o_')
            projection(nc,g,OQ,os,a['L0_attn_b_proj'])
        g.free_sems()
        YS=nc.dram_tensor('YS',(SLOT_TILES,P,E),F32,kind='Internal').ap()
        moments(nc,g,'m1_')
        feed_forward(nc,g,a['L0_ffn_w_gate'],a['L0_ffn_w_up'],a['L0_ffn_w_down'],YS)
        moments(nc,g,'m2_')
        sparse_attention(nc,g,*(a['L1_attn_'+n] for n in ('Wq','bq','Wk','bk','Wv','bv','Wo','bo')))
        moments(nc,g,'m3_')
        routed_experts(nc,g,out,YS,*(a['L1_ffn_'+n] for n in ('router_w','router_b','weights1','bias1','weights2')))


def kernel(**inputs):
    import concourse.bacc as bacc
    from concourse.bass_utils import run_bass_kernel_spmd

    nc = bacc.Bacc("TRN2", target_bir_lowering=False, num_devices=1)
    arrays, args = {}, {}
    for name, value in inputs.items():
        v = np.asarray(value)
        if name in ("L0_ffn_w_gate", "L0_ffn_w_up", "L0_ffn_w_down", "L1_ffn_router_w"):
            v = v.T
        elif name in ("L1_attn_bq", "L1_attn_bk"):
            v = v.reshape(-1, P).T
        elif name == "L1_ffn_weights1":
            v = v.reshape(EXPERTS, EC, P, EH).transpose(0, 2, 1, 3)
        elif name == "L1_ffn_weights2":
            v = np.concatenate([v, np.asarray(inputs["L1_ffn_bias2"])[:, None, :]], axis=1)
        elif name == "L1_ffn_bias2":
            continue
        v = np.ascontiguousarray(v)
        arrays["in_" + name] = v
        args[name] = nc.dram_tensor("in_" + name, v.shape, mybir.dt.from_np(v.dtype), kind="ExternalInput").ap()
    out = nc.dram_tensor("out", (B, S, E), F32, kind="ExternalOutput").ap()
    tower(nc, args, out)
    return run_bass_kernel_spmd(nc, [arrays], core_ids=[0]).results[0]["out"]
```

```python
from contextlib import ExitStack

import numpy as np
import concourse.bass as bass
from concourse import mybir

F32, BF16, F16, I32 = mybir.dt.float32, mybir.dt.bfloat16, mybir.dt.float16, mybir.dt.int32
ALU = mybir.AluOpType
ACT = mybir.ActivationFunctionType
AX = mybir.AxisListType.X
ABSMAX = bass.bass_isa.ReduceOp.absmax

P = 128
B, S, E = 8, 512, 256
T = B * S // P
TB = S // P
EC = E // P
HEADS, HD = 16, 16
HG = 4
NG = B * HEADS // HG
STRIP = 32
PAD_ID, SEP_ID = 1, 4
ROUND = 1.5 * 2.0 ** 23
PRED = 1.0 - 2.0 ** -24
SLACK = 1.0 - 2.0 ** -16
EPS_Q = 0.01
EPS_LN = 1e-5
NEG = -1e30


class Steps:

    def __init__(self, eng, sem, i=None, per=0, base=0):
        self.eng, self.sem, self.n, self.i, self.per, self.base = eng, sem, 0, i, per, base

    def link(self, ins):
        self.n += 1
        ins.then_inc(self.sem, 1)
        at = self.base + self.n
        self.eng.wait_ge(self.sem, at if self.i is None else self.i * self.per + at)

    def close(self):
        assert self.i is None or self.n == self.per, (self.n, self.per)


def row(ap):
    return ap.rearrange("(a n) -> a n", a=1).broadcast_to([P, ap.shape[0]])


def pow2_up(nc, st, out, inv, x, low, tmp, slack=PRED):
    st.link(nc.vector.tensor_scalar(tmp, x, low, slack, ALU.max, ALU.mult))
    st.link(nc.vector.tensor_single_scalar(tmp.bitcast(I32), tmp.bitcast(I32), -(1 << 23), ALU.bitwise_and))
    if inv is not None:
        st.link(nc.vector.tensor_scalar(inv.bitcast(I32), tmp.bitcast(I32), -1.0, float(253 << 23), ALU.mult, ALU.add))
    st.link(nc.vector.tensor_scalar(out, tmp, 2.0, None, ALU.mult))


def statistics(nc, g, t):
    nc.vector.bn_stats(g.stats[:, bass.ds(t, 1), :], g.H[:, bass.ds(t, 1), :])


def constants_and_tokens(nc, g, tokens, table, wa, wp, w_attn, w_proj):
    with ExitStack() as c:
        sb = lambda n, s, d: c.enter_context(nc.sbuf_tensor(n, s, d))
        tok = sb("tok", [B, S], I32)
        place = sb("place", [B, S], I32)
        placef = sb("placef", [B, S], F32)
        sep_at = sb("sep_at", [B, S], F32)
        last_sep = sb("last_sep", [B, S], F32)
        not_pad = sb("not_pad", [B, S], F32)
        valid = sb("valid", [B, S], F32)
        back = sb("back", [B, S], F32)
        pos = sb("pos", [B, S], F32)
        rows = sb("rows", [P, T], I32)
        tokens_in, w_in = g.sem("tokens_in"), g.sem("w_in")
        made = g.sem("made")
        chain = g.sem("tok_chain")
        pos_ready = g.sem("pos_ready")
        pos_turned = g.sem("pos_turned")
        rows_ready = g.sem("rows_ready")
        gathered = [g.sem(f"gathered{b}") for b in range(B)]
        block = c.enter_context(nc.Block())

        def gather(tiles):
            for t in tiles:
                nc.gpsimd.indirect_dma_start(out=g.H[:, t, :], out_offset=None, in_=table,
                                             in_offset=bass.IndirectOffsetOnAxis(ap=rows[:, t:t + 1], axis=0)
                                             ).then_inc(gathered[t // TB], 16)

        @block.sync
        def _(sp):
            sp.dma_start(tok[:], tokens).then_inc(tokens_in, 16)
            sp.dma_start(wa[:], w_attn.rearrange("(c p) n -> p c n", p=P)).then_inc(w_in, 16)
            sp.dma_start(wp[:], w_proj.rearrange("(c p) n -> p c n", p=P)).then_inc(w_in, 16)
            sp.wait_ge(w_in, 32)

        @block.gpsimd
        def _(pool):
            st = Steps(pool, made)
            st.link(nc.gpsimd.iota(place[:], pattern=[[1, S]], base=0, channel_multiplier=0))
            st.link(nc.gpsimd.memset(g.ident[:], 1.0))
            st.link(nc.gpsimd.affine_select(out=g.ident[:], in_=g.ident[:], compare_op=ALU.is_equal, fill=0.0,
                                            base=0, pattern=[[-1, P]], channel_multiplier=1))
            st.link(nc.gpsimd.memset(g.identf[:], 1.0))
            st.link(nc.gpsimd.affine_select(out=g.identf[:], in_=g.identf[:], compare_op=ALU.is_equal, fill=0.0,
                                            base=0, pattern=[[-1, P]], channel_multiplier=1))
            st.link(nc.gpsimd.memset(g.mask_q[:], 0.0))
            st.link(nc.gpsimd.affine_select(out=g.mask_q[:], in_=g.mask_q[:], compare_op=ALU.is_ge, fill=NEG,
                                            base=0, pattern=[[-1, P]], channel_multiplier=1))
            st.link(nc.gpsimd.memset(g.mask_k[:], 0.0))
            st.link(nc.gpsimd.affine_select(out=g.mask_k[:], in_=g.mask_k[:], compare_op=ALU.is_ge, fill=NEG,
                                            base=0, pattern=[[1, P]], channel_multiplier=-1))
            pool.wait_ge(rows_ready, 1)
            gather(range(T // 4))

        @block.vector
        def _(dve):
            st = Steps(dve, chain)
            dve.wait_ge(made, 1)
            dve.wait_ge(tokens_in, 16)
            st.link(nc.vector.tensor_copy(placef[:], place[:]))
            st.link(nc.vector.scalar_tensor_tensor(out=sep_at[:], in0=tok[:], scalar=float(SEP_ID), in1=placef[:],
                                                   op0=ALU.is_equal, op1=ALU.mult))
            st.link(nc.vector.tensor_tensor_scan(last_sep[:], sep_at[:], sep_at[:], 0.0, ALU.max, ALU.max))
            st.link(nc.vector.tensor_single_scalar(not_pad[:], tok[:], float(PAD_ID), ALU.not_equal))
            st.link(nc.vector.tensor_tensor_scan(valid[:], not_pad[:], not_pad[:], 1.0, ALU.mult, ALU.min))
            st.link(nc.vector.tensor_tensor(back[:], placef[:], last_sep[:], ALU.subtract))
            st.link(nc.vector.scalar_tensor_tensor(out=back[:], in0=back[:], scalar=1.0, in1=valid[:],
                                                   op0=ALU.add, op1=ALU.mult))
            nc.vector.tensor_single_scalar(pos[:], back[:], 1.0, ALU.add).then_inc(pos_ready, 1)
            dve.wait_ge(pos_turned, 1)
            nc.vector.tensor_copy(rows[:].rearrange("p (b t) -> p t b", b=B),
                                  g.PS[:, 0, 0:T].rearrange("p (t b) -> p t b", b=B)).then_inc(rows_ready, 1)
            dve.wait_ge(w_in, 32)

        @block.tensor
        def _(pe):
            pe.wait_ge(made, 5)
            pe.wait_ge(pos_ready, 1)
            for t in range(TB):
                last = nc.tensor.transpose(g.PS[:, 0, t * B:(t + 1) * B], pos[:, t * P:(t + 1) * P], g.identf[0:B, 0:B])
            last.then_inc(pos_turned, 1)

        sa, sp_ = sb("wa_s", [P, EC], F32), sb("wp_s", [P, EC], F32)
        quantise(nc, g, wa[:], g.WA[:], EC, 3 * E, sa[:], True, "wa_", block, c)

        @block.gpsimd
        def _(pool):
            gather(range(T // 4, T * 3 // 4))

        quantise(nc, g, wp[:], g.WP[:], EC, E, sp_[:], True, "wp_", block, c)

        @block.gpsimd
        def _(pool):
            gather(range(T * 3 // 4, T))

        @block.vector
        def _(dve):
            for b in range(B):
                dve.wait_ge(gathered[b], 16 * TB)
                for t in range(TB):
                    statistics(nc, g, b * TB + t)


CUT = -(1 << 12)


def exact_rsqrt(nc, st, rstd, ve, root, y, tmp):
    rh, rl, yh, yl, t, rest = tmp
    v = nc.vector

    def halves(x, hi, lo):
        st.link(v.tensor_single_scalar(hi.bitcast(I32), x.bitcast(I32), CUT, ALU.bitwise_and))
        st.link(v.tensor_tensor(lo, x, hi, ALU.subtract))

    def less(a, b, times=-1.0):
        st.link(v.tensor_tensor(t, a, b, ALU.mult))
        st.link(v.scalar_tensor_tensor(out=rest, in0=t, scalar=times, in1=rest, op0=ALU.mult, op1=ALU.add))

    st.link(v.reciprocal(y, root))
    halves(root, rh, rl)
    halves(y, yh, yl)
    st.link(v.tensor_tensor(t, rh, rh, ALU.mult))
    st.link(v.tensor_tensor(rest, ve, t, ALU.subtract))
    less(rh, rl, -2.0)
    less(rl, rl)
    st.link(v.scalar_tensor_tensor(out=rstd, in0=rest, scalar=0.5, in1=y, op0=ALU.mult, op1=ALU.mult))
    st.link(v.tensor_tensor(t, yh, rh, ALU.mult))
    st.link(v.tensor_scalar(rest, t, -1.0, 1.0, ALU.mult, ALU.add))
    less(yh, rl)
    less(yl, rh)
    less(yl, rl)
    less(y, rstd)
    st.link(v.tensor_tensor(t, y, rest, ALU.mult))
    st.link(v.tensor_tensor(rstd, y, t, ALU.add))


def moments(nc, g, tag):
    with ExitStack() as c:
        sb = lambda n, s=[P, T]: c.enter_context(nc.sbuf_tensor(tag + n, s, F32))
        diff, ve, root, half = sb("diff"), sb("ve"), sb("root"), sb("half")
        tmp = sb("tmp", [P, 6, T])
        chain, var_ready, root_ready = (g.sem(tag + n) for n in ("ln_chain", "var_ready", "root_ready"))
        block = c.enter_context(nc.Block())

        @block.scalar
        def _(act):
            nc.scalar.preload_act_table(ACT.Sqrt)
            act.wait_ge(var_ready, 1)
            nc.scalar.activation(root[:], ve[:], ACT.Sqrt).then_inc(root_ready, 1)

        @block.vector
        def _(dve):
            mean_even, m2_even, mean_odd, m2_odd = (g.stats[:, :, n] for n in (1, 2, 4, 5))
            st = Steps(dve, chain)
            st.link(nc.vector.tensor_tensor(diff[:], mean_even, mean_odd, ALU.subtract))
            st.link(nc.vector.tensor_tensor(g.mean[:], mean_even, mean_odd, ALU.add))
            st.link(nc.vector.tensor_single_scalar(g.mean[:], g.mean[:], 0.5, ALU.mult))
            st.link(nc.vector.tensor_tensor(half[:], m2_even, m2_odd, ALU.add))
            st.link(nc.vector.tensor_tensor(diff[:], diff[:], diff[:], ALU.mult))
            st.link(nc.vector.tensor_scalar(diff[:], diff[:], 0.25, EPS_LN, ALU.mult, ALU.add))
            nc.vector.scalar_tensor_tensor(out=ve[:], in0=half[:], scalar=1.0 / E, in1=diff[:], op0=ALU.mult,
                                           op1=ALU.add).then_inc(var_ready, 1)
            dve.wait_ge(root_ready, 1)
            exact_rsqrt(nc, st, g.rstd[:], ve[:], root[:], half[:], [tmp[:, n] for n in range(6)])


def normalise(nc, g, out, t):
    return nc.vector.tensor_scalar(out, g.H[:, bass.ds(t, 1), :].rearrange("p a e -> p (a e)"),
                                   g.mean[:, bass.ds(t, 1)],
                                   g.rstd[:, bass.ds(t, 1)], ALU.subtract, ALU.mult)


def layernorm(nc, g, Y, tag):
    moments(nc, g, tag)
    with nc.Block() as block:
        @block.vector
        def _(dve):
            with dve.Fori(0, B) as b:
                for t in range(TB):
                    normalise(nc, g, Y[:, bass.ds(b * TB + t, 1), :].rearrange("p a e -> p (a e)"), b * TB + t)


def quantise(nc, g, X, out, n, width, scale2, fold, tag, block=None, stack=None, ready=None):
    with ExitStack() as own:
        c = own if stack is None else stack
        sb = lambda nm, s, d=F32: c.enter_context(nc.sbuf_tensor(tag + nm, s, d))
        col = sb("col", [P, width])
        colb = sb("colb", [P, width])
        tmpc = sb("tmpc", [P, width])
        s1 = sb("s1", [P, width])
        s1i = sb("s1i", [P, width])
        rmax = sb("rmax", [P, n])
        tmpr = sb("tmpr", [P, n])
        s2i = sb("s2i", [P, n])
        lift = sb("lift", [P, n])
        chain = g.sem(tag + "q_chain")
        col_ready = g.sem(tag + "col_ready")
        col_all = g.sem(tag + "col_all")
        lift_ready, lifted = g.sem(tag + "lift_ready"), g.sem(tag + "lifted")
        if block is None:
            block = c.enter_context(nc.Block())
        full = [P, n, width]
        some = min(n, T // 4)
        by_col = lambda a: a[:].unsqueeze(1).broadcast_to(full)

        @block.gpsimd
        def _(pool):
            pool.wait_ge(col_ready, 1)
            nc.gpsimd.partition_all_reduce(colb[:], col[:], P, ABSMAX).then_inc(col_all, 1)

        @block.scalar
        def _(act):
            act.wait_ge(lift_ready, 1)
            for t in range(some, n):
                nc.scalar.activation(X[:, t], X[:, t], ACT.Copy, scale=lift[:, t:t + 1], bias=ROUND).then_inc(lifted, 1)

        @block.vector
        def _(dve):
            st = Steps(dve, chain)
            nc.vector.tensor_reduce(col[:], X.rearrange("p t e -> p e t"), AX, ALU.max,
                                    apply_absolute_value=True).then_inc(col_ready, 1)
            dve.wait_ge(col_all, 1)
            pow2_up(nc, st, s1[:], s1i[:], colb[:], EPS_Q, tmpc[:])
            st.link(nc.vector.tensor_tensor(X, X, by_col(s1i), ALU.mult))
            st.link(nc.vector.tensor_reduce(rmax[:], X, AX, ALU.max, apply_absolute_value=True))
            pow2_up(nc, st, scale2, s2i[:], rmax[:], EPS_Q, tmpr[:])
            nc.vector.tensor_single_scalar(lift[:], s2i[:], 128.0, ALU.mult).then_inc(lift_ready, 1)
            st.link(nc.vector.tensor_single_scalar(scale2, scale2, 1.0 / 128, ALU.mult))
            for lo in range(0, n, some):
                ts = slice(lo, lo + some)
                Xs, cols = X[:, ts], s1[:].unsqueeze(1).broadcast_to([P, some, width])
                if lo:
                    dve.wait_ge(lifted, lo)
                else:
                    dve.wait_ge(lift_ready, 1)
                    for t in range(some):
                        raised = nc.vector.tensor_scalar(X[:, t], X[:, t], lift[:, t:t + 1], ROUND, ALU.mult, ALU.add)
                    st.link(raised)
                st.link(nc.vector.tensor_single_scalar(Xs, Xs, ROUND + 127.0, ALU.min))
                back = nc.vector.scalar_tensor_tensor(out=Xs if fold else out[:, ts], in0=Xs, scalar=ROUND, in1=cols,
                                                      op0=ALU.subtract, op1=ALU.mult)
                if ready is not None:
                    back.then_inc(ready, some)
                if fold:
                    st.link(back)
                    nc.vector.tensor_tensor(out[:, ts], Xs, scale2[:, ts].unsqueeze(2).broadcast_to([P, some, width]), ALU.mult)


def in_turn(eng, steps):
    steps(0, 0, True, False)
    with eng.Fori(0, B // 2 - 1) as n:
        steps(n * 2 + 1, 1, True, True)
        steps(n * 2 + 2, 0, True, True)
    steps(B - 1, 1, True, True)
    steps(B, 0, False, True)


def qkv_quantised(nc, g, XQ, xs, b_attn):
    with ExitStack() as c:
        sb = lambda n, s, d=F32: c.enter_context(nc.sbuf_tensor(n, s, d))
        bias = sb("bias_a", [P, 3 * E])
        xT = sb("xT", [P, TB, EC, P], BF16)
        R = sb("R", [P, 2, TB, 3 * E])
        col, colb = sb("r_col", [P, 2, 3 * E]), sb("r_colb", [P, 2, 3 * E])
        tmpc = sb("r_tmpc", [P, 3 * E])
        cs, ci = sb("r_cs", [P, 2, 3 * E]), sb("r_ci", [P, 3 * E])
        rmax, tmpr, ri = (sb(n, [P, TB, 3 * HEADS]) for n in ("r_rmax", "r_tmpr", "r_ri"))
        rs = sb("r_rs", [P, 2, TB, 3 * HEADS])
        QP = sb("QP", [P, TB, HEADS, STRIP], BF16)
        KP = sb("KP", [P, TB, HEADS, STRIP], BF16)
        turned = sb("turned", [P, 2, HG, S], BF16)
        bias_in, x_turned, xT_ready, qkv_done, r_ready, waited = (g.sem(n) for n in (
            "bias_in", "x_turned", "xT_ready", "qkv_done", "r_ready", "col_waited"))
        pads_made, col_ready, col_all, scaled, lifted, rounded = (g.sem(n) for n in (
            "pads_made", "qkv_col_ready", "qkv_col_all", "scaled", "lifted", "rounded"))
        chain_a, chain_b, chain_c, columned, q_ready, kv_ready = (g.sem(n) for n in (
            "chain_a", "chain_b", "chain_c", "columned", "q_ready", "kv_ready"))
        strip_turned, strip_copied = (g.sem(n) for n in ("strip_turned", "strip_copied"))
        stored = [g.sem("stored0"), g.sem("stored1")]
        block = c.enter_context(nc.Block())
        by_head = lambda a: a.unsqueeze(3).broadcast_to([P, TB, HEADS, HD])
        bank = lambda n: g.PS[:, n, :].bitcast(BF16)
        goes_on = lambda b: not isinstance(b, int) or b < B - 1
        products = lambda b, this: () if not this else range(TB) if isinstance(b, int) and b == 0 else (2, 3)

        def parts(half):
            R4 = R[:, half].rearrange("p t (x h d) -> p t x h d", x=3, d=HD)
            return (R4, *(a.rearrange("p t (x h) -> p t x h", x=3) for a in (rmax[:], ri[:], rs[:, half], tmpr[:])))

        @block.sync
        def _(sp):
            sp.dma_start(bias[:], row(b_attn)).then_inc(bias_in, 16)
            with sp.Fori(0, B) as b:
                for s, dst in enumerate((g.QT, g.KT)):
                    sp.wait_ge(strip_copied, b * 8 + 4 * s + 6)
                    sp.dma_start(dst[bass.ds(b * HG, HG), :, :].rearrange("g p c -> p g c"),
                                 turned[:, s]).then_inc(stored[s], 16)
            for s in range(2):
                sp.wait_ge(stored[s], 16 * B)

        @block.gpsimd
        def _(pool):
            nc.gpsimd.memset(QP[:], 0.0).then_inc(pads_made, 1)
            nc.gpsimd.memset(KP[:], 0.0).then_inc(pads_made, 1)
            pool.wait_ge(pads_made, 2)
            nc.gpsimd.memset(QP[:, :, :, HD + 3:HD + 6], 1.0).then_inc(pads_made, 1)
            nc.gpsimd.memset(KP[:, :, :, HD:HD + 3], 1.0).then_inc(pads_made, 1)
            pool.wait_ge(pads_made, 4)

            def steps(b, half, this, last):
                if this:
                    pool.wait_ge(col_ready, b + 1)
                    pool.sem_inc(waited, 1)
                    nc.gpsimd.partition_all_reduce(colb[:, half], col[:, half], P, ABSMAX).then_inc(col_all, 1)
                if last:
                    R4, _, _, rsv, _ = parts(1 - half)
                    pool.wait_ge(columned, b)
                    if not (isinstance(b, int) and b == 1):
                        pool.wait_ge(strip_copied, b * 8 - 6)
                    nc.gpsimd.tensor_tensor(KP[:, :, :, 0:HD], R4[:, :, 1], by_head(rsv[:, :, 1]), ALU.mult).then_inc(kv_ready, 1)
                    nc.gpsimd.tensor_tensor(
                        g.V[:, bass.ds(b * TB - TB, TB), :].rearrange("p t (h d) -> p t h d", d=HD),
                        R4[:, :, 2], by_head(rsv[:, :, 2]), ALU.mult).then_inc(kv_ready, 1)

            in_turn(pool, steps)

        @block.tensor
        def _(pe):
            pe.sem_inc(strip_turned, 8)

            def turn(b):
                for t in range(TB):
                    at = b * TB + t
                    pe.wait_ge(xT_ready, at + 1)
                    for e in range(EC):
                        last = nc.tensor.transpose(bank(t % 2)[:, e * P:(e + 1) * P],
                                                   XQ[:, bass.ds(at, 1), e * P:(e + 1) * P].rearrange(
                                                       "p a c -> p (a c)"), g.ident[:])
                    last.then_inc(x_turned, 1)

            def product(b, t):
                at = b * TB + t
                pe.wait_ge(xT_ready, at + 3)
                pe.wait_ge(r_ready, at + 1)
                for e in range(EC):
                    for n, (lo, hi) in enumerate(((0, 512), (512, 768))):
                        last = nc.tensor.matmul(g.PS[:, 2 + 2 * (t % 2) + n, 0:hi - lo], xT[:, t, e, :],
                                                g.WA[:, e, lo:hi], start=(e == 0), stop=(e == EC - 1))
                last.then_inc(qkv_done, 1)

            turn(0)

            def steps(b, half, this, last_batch):
                for t in products(b, this):
                    product(b, t)
                for n in range(2 * HG) if last_batch else ():
                    s, hg = n // HG, n % HG
                    if n == 0:
                        pe.wait_ge(q_ready, b)
                    if n == HG:
                        pe.wait_ge(kv_ready, b * 2)
                    pe.wait_ge(strip_copied, b * 8 - 8 + n + 1)
                    for t in range(TB):
                        last = nc.tensor.transpose(bank(6 + n % 2)[:, t * P:(t + 1) * P],
                                                   (QP, KP)[s][:, t, hg * HG:(hg + 1) * HG, :].rearrange(
                                                       "p h d -> p (h d)"), g.ident[:])
                    last.then_inc(strip_turned, 1)
                if goes_on(b):
                    turn(b + 1)
                    product(b + 1, 0)
                    product(b + 1, 1)

            in_turn(pe, steps)

        @block.scalar
        def _(act):
            act.sem_inc(xT_ready, 2)
            act.sem_inc(strip_copied, 2)

            def copy_x(b):
                for t in range(TB):
                    act.wait_ge(x_turned, b * TB + t + 1)
                    nc.scalar.activation(xT[:, t].rearrange("p c n -> p (c n)"), bank(t % 2)[:, 0:EC * P],
                                         ACT.Copy).then_inc(xT_ready, 1)

            copy_x(0)

            def steps(b, half, this, last):
                for n in range(2 * HG) if last else ():
                    act.wait_ge(strip_turned, b * 8 + n + 1)
                    if n % HG == 0 and not (isinstance(b, int) and b == 1):
                        act.wait_ge(stored[n // HG], b * 16 - 16)
                    nc.scalar.activation(turned[:, n // HG, n % HG, :], bank(6 + n % 2)[:, 0:S],
                                         ACT.Copy).then_inc(strip_copied, 1)
                if goes_on(b):
                    copy_x(b + 1)
                if this:
                    act.wait_ge(scaled, b + 1)
                    nc.scalar.activation(R[:, half], R[:, half], ACT.Copy, scale=128.0, bias=ROUND).then_inc(lifted, 1)
                    act.wait_ge(lifted, b + 1)
                    nc.scalar.activation(R[:, half], R[:, half], ACT.Copy, bias=-ROUND).then_inc(rounded, 1)

            in_turn(act, steps)

        @block.vector
        def _(dve):
            dve.sem_inc(r_ready, 2)
            dve.wait_ge(bias_in, 16)
            dve.wait_ge(pads_made, 4)

            def steps(b, half, this, last):
                R4, rm, riv, rsv, tmv = parts(half)
                if this:
                    st = Steps(dve, chain_a, b, 5)
                    if not (isinstance(b, int) and b <= 1):
                        dve.wait_ge(kv_ready, b * 2 - 2)
                    for t in range(TB):
                        dve.wait_ge(qkv_done, b * TB + t + 1)
                        nc.vector.scalar_tensor_tensor(
                            out=R[:, half, t, :], in0=g.PS[:, 2 + 2 * (t % 2):4 + 2 * (t % 2), :].rearrange(
                                "p a c -> p (a c)")[:, 0:3 * E],
                            scalar=xs[:, bass.ds(b * TB + t, 1)], in1=bias[:], op0=ALU.mult, op1=ALU.add).then_inc(r_ready, 1)
                    dve.wait_ge(r_ready, b * TB + TB + 2)
                    st.link(nc.vector.tensor_reduce(rm[:, :, 1], R4[:, :, 1], AX, ALU.max, apply_absolute_value=True))
                    st.link(nc.vector.tensor_scalar(tmv[:, :, 1], rm[:, :, 1], EPS_Q, PRED, ALU.max, ALU.mult))
                    st.link(nc.vector.tensor_single_scalar(tmv[:, :, 1].bitcast(I32), tmv[:, :, 1].bitcast(I32), -(1 << 23),
                                                           ALU.bitwise_and))
                    st.link(nc.vector.tensor_scalar(riv[:, :, 1].bitcast(I32), tmv[:, :, 1].bitcast(I32), -1.0,
                                                    float(253 << 23), ALU.mult, ALU.add))
                    st.link(nc.vector.tensor_tensor(R4[:, :, 1], R4[:, :, 1], by_head(riv[:, :, 1]), ALU.mult))
                    st.close()
                    nc.vector.tensor_reduce(col[:, half], R[:, half].rearrange("p t n -> p n t"), AX, ALU.max,
                                            apply_absolute_value=True).then_inc(col_ready, 1)
                if last:
                    R4o, _, _, rso, _ = parts(1 - half)
                    dve.wait_ge(rounded, b)
                    for t in range(TB):
                        ins = nc.vector.scalar_tensor_tensor(out=R[:, 1 - half, t], in0=R[:, 1 - half, t], scalar=127.0,
                                                             in1=cs[:, 1 - half], op0=ALU.min, op1=ALU.mult)
                    ins.then_inc(columned, 1)
                    dve.wait_ge(columned, b)
                    if not (isinstance(b, int) and b == 1):
                        dve.wait_ge(strip_turned, b * 8 - 4)
                    nc.vector.tensor_tensor(QP[:, :, :, 0:HD], R4o[:, :, 0], by_head(rso[:, :, 0]), ALU.mult).then_inc(q_ready, 1)
                if this:
                    st = Steps(dve, chain_b, b, 13)
                    st.link(nc.vector.tensor_single_scalar(rsv[:, :, 1], tmv[:, :, 1], 2.0, ALU.mult))
                    dve.wait_ge(col_all, b + 1)
                    pow2_up(nc, st, cs[:, half], ci[:], colb[:, half], EPS_Q, tmpc[:])
                    st.link(nc.vector.tensor_tensor(R[:, half], R[:, half], ci[:].unsqueeze(1).broadcast_to([P, TB, 3 * E]),
                                                    ALU.mult))
                    nc.vector.tensor_reduce(rm[:, :, 0], R4[:, :, 0], AX, ALU.max, apply_absolute_value=True)
                    st.link(nc.vector.tensor_reduce(rm[:, :, 2], R4[:, :, 2], AX, ALU.max, apply_absolute_value=True))
                    pow2_up(nc, st, rsv[:, :, 0::2], riv[:, :, 0::2], rm[:, :, 0::2], EPS_Q, tmv[:, :, 0::2])
                    nc.vector.tensor_tensor(R4[:, :, 0], R4[:, :, 0], by_head(riv[:, :, 0]), ALU.mult)
                    st.link(nc.vector.tensor_tensor(R4[:, :, 2], R4[:, :, 2], by_head(riv[:, :, 2]), ALU.mult))
                    st.link(nc.vector.tensor_single_scalar(rs[:, half], rs[:, half], 1.0 / 128, ALU.mult))
                    nc.vector.tensor_single_scalar(rsv[:, :, 0], rsv[:, :, 0], HD ** -0.5, ALU.mult).then_inc(scaled, 1)
                    st.close()

            in_turn(dve, steps)


GRID = 1.5 * 2.0 ** 16


def load_groups(sp, g, qk, loaded, ready, tiles, other_loads=None):
    for hg in range(2):
        sp.dma_start(qk[:, hg, 0], g.QT[hg]).then_inc(loaded[hg], 16)
        sp.dma_start(qk[:, hg, 1], g.KT[hg]).then_inc(loaded[hg], 16)
    if other_loads is not None:
        other_loads()
    with sp.Fori(0, NG // 2 - 1) as n:
        for half in range(2):
            sp.wait_ge(ready, (n * 2 + half + 1) * tiles)
            for s, src in enumerate((g.QT, g.KT)):
                sp.dma_start(qk[:, half, s], src[bass.ds(n * 2 + half + 2, 1), :, :].rearrange("g p c -> p (g c)")
                             ).then_inc(loaded[half], 16)


def scores(nc, g, qk, half, t, by_query, heads, bank0):
    own, other = (0, 1) if by_query else (1, 0)
    lo, hi = (0, (t + 1) * P) if by_query else (t * P, S)
    for n, h in enumerate(heads):
        strip = slice(STRIP * h, STRIP * (h + 1))
        nc.tensor.matmul(g.PS[:, bank0 + n, 0:hi - lo], qk[strip, half, own, t * P:(t + 1) * P],
                         qk[strip, half, other, lo:hi], start=True, stop=False, skip_group_check=True)
    diag = hi - lo - P if by_query else 0
    for n, h in enumerate(heads):
        last = nc.tensor.matmul(g.PS[:, bank0 + n, diag:diag + P], g.ident[:],
                                g.mask_q[:] if by_query else g.mask_k[:], start=False, stop=True, skip_group_check=True)
    return last


def width(t, by_query):
    return (t + 1) * P if by_query else S - t * P


def score_maxima(nc, g, out, by_query, sums, tag, value_scale=None):
    with ExitStack() as c:
        qk = c.enter_context(nc.sbuf_tensor(tag + "qk", [P, 2, 2, S], BF16))
        sem = lambda n: g.sem(tag + n)
        loaded = [sem("loaded0"), sem("loaded1")]
        ready, maxed, free = sem("ready"), sem("maxed"), sem("free")
        block = c.enter_context(nc.Block())

        SETS = 4
        PER = HG * TB * 2

        def tiles():
            for u in range(PER):
                yield u, u // (2 * TB), u // 2 % TB, 2 * (u % 2)

        @block.sync
        def _(sp):
            load_groups(sp, g, qk, loaded, ready, 2 * TB)

        if value_scale is not None:
            @block.gpsimd
            def _(pool):
                with pool.Fori(0, B) as b:
                    for t in range(TB):
                        v = g.V[:, bass.ds(b * TB + t, 1), :].rearrange("p a (h d) -> p (a h) d", d=HD)
                        s = value_scale[:, t, bass.ds(b * HG, HG), :].rearrange("p g h -> p (g h)")
                        nc.gpsimd.tensor_tensor(v, v, s.unsqueeze(2).broadcast_to([P, HEADS, HD]), ALU.mult)

        @block.tensor
        def _(pe):
            with pe.Fori(0, B) as b:
                for u, hg, t, h in tiles():
                    if u % (2 * TB) == 0:
                        pe.wait_ge(loaded[hg % 2], b * 64 + 32 * (hg // 2) + 32)
                    pe.wait_ge(free, b * PER + u + 1)
                    scores(nc, g, qk, hg % 2, t, by_query, (h, h + 1), 2 * (u % SETS)).then_inc(ready, 1)

        @block.vector
        def _(dve):
            if sums is None:
                dve.sem_inc(free, SETS)
            with dve.Fori(0, B) as b:
                for u, hg, t, h in tiles():
                    dve.wait_ge(ready, b * PER + u + 1)
                    nc.vector.tensor_reduce(
                        out[:, t, bass.ds(b * HG + hg, 1), h:h + 2].rearrange("p g h -> p (g h)"),
                        g.PS[:, 2 * (u % SETS):2 * (u % SETS) + 2, 0:width(t, by_query)], AX, ALU.max,
                        negate=sums is not None).then_inc(free if sums is None else maxed, 1)

        if sums is not None:
            @block.scalar
            def _(act):
                nc.scalar.preload_act_table(ACT.Exp)
                act.sem_inc(free, SETS)
                with act.Fori(0, B) as b:
                    for u, hg, t, h in tiles():
                        act.wait_ge(maxed, b * PER + u + 1)
                        for n in range(2):
                            at = lambda a: a[:, t, bass.ds(b * HG + hg, 1), h + n:h + n + 1].rearrange("p g h -> p (g h)")
                            bank = g.PS[:, 2 * (u % SETS) + n, 0:width(t, by_query)]
                            last = nc.scalar.activation(bank, bank, ACT.Exp, bias=at(out), accum_out=at(sums))
                        last.then_inc(free, 1)


def row_terms(nc, g, term, dst, first, tag):
    with ExitStack() as c:
        part = c.enter_context(nc.sbuf_tensor(tag + "part", [P, 3, TB, NG * HG], BF16))
        rest = c.enter_context(nc.sbuf_tensor(tag + "rest", [P, TB, NG * HG], F32))
        across = c.enter_context(nc.sbuf_tensor(tag + "across", [P, 3, S], BF16))
        sem = lambda n: g.sem(tag + n)
        chain, parted, turned, copied, stored = (sem(n) for n in ("chain", "parted", "turned", "copied", "stored"))
        block = c.enter_context(nc.Block())

        @block.vector
        def _(dve):
            st = Steps(dve, chain)
            whole = term.rearrange("p t g h -> p t (g h)")
            left = whole
            for j in range(3):
                nc.vector.tensor_copy(part[:, j], left).then_inc(parted, 1)
                dve.wait_ge(parted, j + 1)
                if j < 2:
                    st.link(nc.vector.tensor_tensor(rest[:], left, part[:, j], ALU.subtract))
                    left = rest[:]

        @block.tensor
        def _(pe):
            for j in range(3):
                pe.wait_ge(parted, j + 1)
                for t in range(TB):
                    last = nc.tensor.transpose(g.PS[:, j, :].bitcast(BF16)[:, t * P:(t + 1) * P], part[:, j, t], g.ident[:])
                last.then_inc(turned, 1)

        @block.scalar
        def _(act):
            for j in range(3):
                act.wait_ge(turned, j + 1)
                nc.scalar.activation(across[:, j], g.PS[:, j, :].bitcast(BF16)[:, 0:S], ACT.Copy).then_inc(copied, 1)

        @block.sync
        def _(sp):
            for j in range(3):
                sp.wait_ge(copied, j + 1)
                sp.dma_start(dst.rearrange("g (h r) c -> (g h) r c", r=STRIP)[:, first + j, :],
                             across[:, j]).then_inc(stored, 16)
            sp.wait_ge(stored, 48)


def log_sums(nc, g, lse, neg_max, sums):
    ln_ready = g.sem("ln_ready")
    with nc.sbuf_tensor("lns", [P, TB, NG, HG], F32) as lns, nc.Block() as block:
        @block.scalar
        def _(act):
            nc.scalar.activation(lns[:], sums, ACT.Ln).then_inc(ln_ready, 1)

        @block.vector
        def _(dve):
            dve.wait_ge(ln_ready, 1)
            nc.vector.tensor_tensor(lse, neg_max, lns[:], ALU.subtract)


def log_scales(nc, g, scale, neg_ln, logs, extra, tag):
    with ExitStack() as c:
        tmp = c.enter_context(nc.sbuf_tensor(tag + "tmp", [P, TB, NG, HG], F32))
        sem = lambda n: g.sem(tag + n)
        chain, exp_ready, scale_ready, ln_ready = (sem(n) for n in ("chain", "exp_ready", "scale_ready", "ln_ready"))
        block = c.enter_context(nc.Block())

        @block.scalar
        def _(act):
            nc.scalar.activation(scale, logs, ACT.Exp).then_inc(exp_ready, 1)
            act.wait_ge(scale_ready, 1)
            nc.scalar.activation(neg_ln, scale, ACT.Ln).then_inc(ln_ready, 1)

        @block.vector
        def _(dve):
            st = Steps(dve, chain)
            dve.wait_ge(exp_ready, 1)
            st.link(nc.vector.tensor_scalar(tmp[:], scale, EPS_Q, SLACK, ALU.max, ALU.mult))
            st.link(nc.vector.tensor_single_scalar(tmp[:].bitcast(I32), tmp[:].bitcast(I32), -(1 << 23), ALU.bitwise_and))
            nc.vector.tensor_single_scalar(scale, tmp[:], 2.0, ALU.mult).then_inc(scale_ready, 1)
            dve.wait_ge(ln_ready, 1)
            if extra is None:
                nc.vector.tensor_single_scalar(neg_ln, neg_ln, -1.0, ALU.mult)
            else:
                nc.vector.scalar_tensor_tensor(out=neg_ln, in0=neg_ln, scalar=-1.0, in1=extra, op0=ALU.mult, op1=ALU.add)


def weighted_values(nc, g, O, s2, ffn):
    with ExitStack() as c:
        raw = c.enter_context(nc.sbuf_tensor("f_raw", [P, FFN_COLUMNS], I32))
        ffn_in = g.sem("ffn_in")
        qk = c.enter_context(nc.sbuf_tensor("d_qk", [P, 2, 2, S], BF16))
        probs = c.enter_context(nc.sbuf_tensor("probs", [P, 3, 2, S], F32))
        steps = c.enter_context(nc.sbuf_tensor("steps", [P, 2, TB, HG, S], BF16))
        sem = lambda n: g.sem("d_" + n)
        loaded = [sem("loaded0"), sem("loaded1")]
        ready, exped, rounded, clipped, summed, read = (sem(n) for n in (
            "ready", "exped", "rounded", "clipped", "summed", "read"))
        block = c.enter_context(nc.Block())
        PER = HG * TB * 2
        prev = lambda u: u - 3 if u >= 3 else (-2, -1, -2)[u]

        def behind_one(eng, batch):
            batch(0, False)
            with eng.Fori(1, B) as b:
                batch(b, True)

        @block.sync
        def _(sp):
            def ffn_weights():
                for n, src in enumerate(ffn[0:2]):
                    sp.dma_start(raw[:, n * EC * HIDDEN:(n + 1) * EC * HIDDEN].rearrange("p (c n) -> p c n", c=EC),
                                 src.rearrange("(c p) n -> p c n", p=P)).then_inc(ffn_in, 16)
                sp.dma_start(raw[:, 2 * EC * HIDDEN:].rearrange("p (c n) -> p c n", c=HC),
                             ffn[2].rearrange("(c p) n -> p c n", p=P)).then_inc(ffn_in, 16)

            load_groups(sp, g, qk, loaded, ready, 2 * TB, ffn_weights)

        @block.gpsimd
        def _(pool):
            pool.wait_ge(ffn_in, 48)
            nc.gpsimd.tensor_copy(g.WF[:], raw[:])

        @block.tensor
        def _(pe):
            def sum_up(b, hg):
                pe.wait_ge(clipped, (b * HG + hg + 1) * TB)
                pe.wait_ge(read, b * HG + hg + 1)
                for q in range(TB):
                    for h in range(HG):
                        for k in range(q + 1):
                            last = nc.tensor.matmul(
                                g.PS[:, 6 + hg % 2, (q * HG + h) * HD:(q * HG + h + 1) * HD],
                                steps[:, hg % 2, k, h, (q - k) * P:(q - k + 1) * P],
                                g.V[:, bass.ds(b * TB + k, 1), (hg * HG + h) * HD:(hg * HG + h + 1) * HD].rearrange(
                                    "p a c -> p (a c)"), start=(k == 0), stop=(k == q))
                last.then_inc(summed, 1)

            pe.sem_inc(summed, 2)

            def batch(b, behind):
                for hg in range(HG):
                    pe.wait_ge(loaded[hg % 2], b * 64 + 32 * (hg // 2) + 32)
                    for t in range(TB):
                        for n in range(2):
                            u = (hg * TB + t) * 2 + n
                            pe.wait_ge(exped, b * PER + prev(u) + 3)
                            scores(nc, g, qk, hg % 2, t, False, (2 * n, 2 * n + 1), 2 * (u % 3)).then_inc(ready, 1)
                    if hg > 0:
                        sum_up(b, hg - 1)
                    elif behind:
                        sum_up(b - 1, HG - 1)

            behind_one(pe, batch)
            sum_up(B - 1, HG - 1)

        @block.scalar
        def _(act):
            nc.scalar.preload_act_table(ACT.Exp)
            act.sem_inc(exped, 2)
            with act.Fori(0, B) as b:
                for u in range(PER):
                    w = width(u // 2 % TB, False)
                    act.wait_ge(ready, b * PER + u + 1)
                    act.wait_ge(rounded, b * PER + prev(u) + 3)
                    nc.scalar.activation(probs[:, u % 3, :, 0:w], g.PS[:, 2 * (u % 3):2 * (u % 3) + 2, 0:w],
                                         ACT.Exp).then_inc(exped, 1)

        @block.vector
        def _(dve):
            def read_out(b, hg):
                at = b * HG + hg
                dve.wait_ge(summed, at + 3)
                tiles = [P, TB, HG, HD]
                nc.vector.tensor_tensor(
                    O[:, bass.ds(b * TB, TB), hg * HG * HD:(hg + 1) * HG * HD].rearrange("p t (h d) -> p t h d", d=HD),
                    g.PS[:, 6 + hg % 2, 0:TB * HG * HD].rearrange("p (t h d) -> p t h d", h=HG, d=HD),
                    s2[:, :, bass.ds(at, 1), :].rearrange("p t g h -> p t (g h)").unsqueeze(3).broadcast_to(tiles),
                    ALU.mult).then_inc(read, 1)

            dve.sem_inc(rounded, 2)
            dve.sem_inc(read, 2)

            def batch(b, behind):
                for hg in range(HG):
                    dve.wait_ge(summed, b * HG + hg + 1)
                    for t in range(TB):
                        w = width(t, False)
                        for n in range(2):
                            u = (hg * TB + t) * 2 + n
                            dve.wait_ge(exped, b * PER + u + 3)
                            nc.vector.tensor_scalar(steps[:, hg % 2, t, 2 * n:2 * n + 2, 0:w], probs[:, u % 3, :, 0:w],
                                                    GRID, GRID, ALU.add, ALU.subtract).then_inc(rounded, 1)
                        dve.wait_ge(rounded, b * PER + u + 3)
                        nc.vector.tensor_single_scalar(steps[:, hg % 2, t, :, 0:w], steps[:, hg % 2, t, :, 0:w],
                                                       127.0 / 128, ALU.min).then_inc(clipped, 1)
                    if hg > 0:
                        read_out(b, hg - 1)
                    elif behind:
                        read_out(b - 1, HG - 1)

            behind_one(dve, batch)
            read_out(B - 1, HG - 1)


HIDDEN = 768
HC = HIDDEN // P
FFN_COLUMNS = 2 * EC * HIDDEN + HC * E
FFN_SCALE = 1.0 / 127.0
EXPERTS, EH = 32, 64
TOPK = 8
SLOT_TILES = 64
assert T + EXPERTS - 1 < SLOT_TILES
GONE = -3e38


def projection(nc, g, O, OQ, os, b_proj):
    with ExitStack() as c:
        bias = c.enter_context(nc.sbuf_tensor("bias_p", [P, E], F32))
        oT = c.enter_context(nc.sbuf_tensor("oT", [P, TB, EC, P], BF16))
        sem = lambda n: g.sem("p_" + n)
        bias_in, biased, turned, copied, done, read, quantised = (sem(n) for n in (
            "bias_in", "biased", "turned", "copied", "done", "read", "quantised"))
        block = c.enter_context(nc.Block())
        quantise(nc, g, O[:], OQ[:], T, E, os[:], False, "o_", block, c, quantised)

        @block.sync
        def _(sp):
            sp.dma_start(bias[:], row(b_proj)).then_inc(bias_in, 16)

        @block.gpsimd
        def _(pool):
            pool.wait_ge(bias_in, 16)
            with pool.Fori(0, B) as b:
                h = g.H[:, bass.ds(b * TB, TB), :]
                nc.gpsimd.tensor_tensor(h, h, bias[:].unsqueeze(1).broadcast_to([P, TB, E]), ALU.add).then_inc(biased, 1)

        @block.tensor
        def _(pe):
            def turn(at, t):
                pe.wait_ge(quantised, at + 1)
                pe.wait_ge(copied, at + 1)
                for e in range(EC):
                    last = nc.tensor.transpose(g.PS[:, t % 2, :].bitcast(BF16)[:, e * P:(e + 1) * P],
                                               OQ[:, bass.ds(at, 1), e * P:(e + 1) * P].rearrange("p a c -> p (a c)"),
                                               g.ident[:])
                last.then_inc(turned, 1)

            def product(at, t):
                pe.wait_ge(copied, at + 3)
                pe.wait_ge(read, at + 1)
                for e in range(EC):
                    last = nc.tensor.matmul(g.PS[:, 2 + t, 0:E], oT[:, t, e, :], g.WP[:, e, :],
                                            start=(e == 0), stop=(e == EC - 1))
                last.then_inc(done, 1)

            turn(0, 0)

            def batch(b, more):
                for t in range(TB):
                    if more or t + 1 < TB:
                        turn(b * TB + t + 1, t + 1)
                    product(b * TB + t, t)

            batches(pe, batch)

        @block.scalar
        def _(act):
            act.sem_inc(copied, 2)
            with act.Fori(0, B) as b:
                for t in range(TB):
                    at = b * TB + t
                    act.wait_ge(turned, at + 1)
                    nc.scalar.activation(oT[:, t].rearrange("p c n -> p (c n)"),
                                         g.PS[:, t % 2, :].bitcast(BF16)[:, 0:EC * P], ACT.Copy).then_inc(copied, 1)

        @block.vector
        def _(dve):
            dve.sem_inc(read, TB)
            with dve.Fori(0, B) as b:
                dve.wait_ge(biased, b + 1)
                for t in range(TB):
                    at = b * TB + t
                    dve.wait_ge(done, at + 1)
                    h = g.H[:, bass.ds(at, 1), :].rearrange("p a e -> p (a e)")
                    nc.vector.scalar_tensor_tensor(out=h, in0=g.PS[:, 2 + t, 0:E], scalar=os[:, bass.ds(at, 1)],
                                                   in1=h, op0=ALU.mult, op1=ALU.add).then_inc(read, 1)
                    if t:
                        dve.wait_ge(read, at + TB)
                        statistics(nc, g, at - 1)
                dve.wait_ge(read, b * TB + 2 * TB)
                statistics(nc, g, b * TB + TB - 1)


def batches(eng, batch):
    with eng.Fori(0, B - 1) as b:
        batch(b, True)
    batch(B - 1, False)


def turn_batch(pe, nc, g, Y, bank, turned):
    for e in range(EC):
        for t in range(TB):
            last = nc.tensor.transpose(g.PS[:, bank + e, t * P:(t + 1) * P], Y[:, t, e * P:(e + 1) * P], g.identf[:])
        last.then_inc(turned, 1)


def feed_forward(nc, g, YS, attn):
    Y_UP, H_DOWN = 2048.0, 0.25
    with ExitStack() as c:
        sb = lambda n, s, d=F32: c.enter_context(nc.sbuf_tensor("f_" + n, s, d))
        w = g.WF
        wg, wu = (w[:, n * EC * HIDDEN:(n + 1) * EC * HIDDEN].rearrange("p (c n) -> p c n", c=EC) for n in range(2))
        wd = w[:, 2 * EC * HIDDEN:].rearrange("p (c n) -> p c n", c=HC)
        Y, yT, hT = sb("Y", [P, TB, E]), sb("yT", [P, 2, EC, S], F16), sb("hT", [P, 2, HC, S], F16)
        gate, h = sb("gate", [P, 2, S]), sb("h", [P, 2, S])
        zero = sb("zero", [P, 16, E])
        sem = lambda n: g.sem("f_" + n)
        w_in, normed, turned, y_hi, y_lo, up_done, silu_done, h_ready, h_hi, h_lo, down_done, added = (
            sem(n) for n in ("w_in", "normed", "turned", "y_hi", "y_lo", "up_done", "silu_done", "h_ready",
                             "h_hi", "h_lo", "down_done", "added"))
        zero_made, zeroed = sem("zero_made"), sem("zeroed")
        block = c.enter_context(nc.Block())

        @block.sync
        def _(sp):
            for n, src in enumerate(attn):
                sp.dma_start(g.WT[:, n], src.rearrange("(c p) n -> p c n", p=P)).then_inc(w_in, 16)
            sp.wait_ge(zero_made, 1)
            for n in range(SLOT_TILES // 16):
                sp.dma_start(YS[n * 16:(n + 1) * 16].rearrange("a p e -> p a e"), zero[:]).then_inc(zeroed, 16)
            sp.wait_ge(zeroed, SLOT_TILES)
            sp.wait_ge(w_in, 16 * len(attn))

        @block.gpsimd
        def _(pool):
            nc.gpsimd.memset(zero[:], 0.0).then_inc(zero_made, 1)

        @block.tensor
        def _(pe):
            pe.wait_ge(normed, TB)
            turn_batch(pe, nc, g, Y, 0, turned)

            def batch(b, more):
                pe.wait_ge(y_hi, b * EC + EC)
                pe.wait_ge(y_lo, b * EC + EC)
                for n in range(HC):
                    pe.wait_ge(h_ready, b * HC + n + 1)
                    for x, wx in enumerate((wg, wu)):
                        for k in range(2 * EC):
                            e, part = k // 2, k % 2
                            last = nc.tensor.matmul(g.PS[:, 2 + 2 * (n % 2) + x, :], wx[:, e, n * P:(n + 1) * P],
                                                    yT[:, part, e], start=(k == 0), stop=(k == 2 * EC - 1))
                    last.then_inc(up_done, 1)
                if more:
                    pe.wait_ge(normed, b * TB + 2 * TB)
                    turn_batch(pe, nc, g, Y, 0, turned)

                def down(t, chunks):
                    if 0 in chunks:
                        pe.wait_ge(added, b * TB + t + 1)
                    for n in chunks:
                        for part in range(2):
                            last = nc.tensor.matmul(g.PS[:, 6 + t % 2, 0:E], hT[:, part, n, t * P:(t + 1) * P], wd[:, n],
                                                    start=(n == 0 and part == 0), stop=(n == HC - 1 and part == 1),
                                                    skip_group_check=True)
                    if HC - 1 in chunks:
                        last.then_inc(down_done, 1)

                pe.wait_ge(h_hi, b * HC + HC)
                pe.wait_ge(h_lo, b * HC + HC)
                down(0, range(HC - 2))
                down(1, range(HC - 2))
                pe.wait_ge(h_hi, b * HC + HC + 2)
                pe.wait_ge(h_lo, b * HC + HC + 2)
                down(0, [HC - 2, HC - 1])
                down(1, [HC - 2, HC - 1])
                down(2, range(HC))
                down(3, range(HC))

            batches(pe, batch)

        @block.scalar
        def _(act):
            nc.scalar.preload_act_table(ACT.Silu)
            act.sem_inc(h_hi, 2)

            def y_high(b):
                for e in range(EC):
                    act.wait_ge(turned, b * EC + e + 1)
                    nc.scalar.activation(yT[:, 0, e], g.PS[:, e, :], ACT.Copy, scale=Y_UP).then_inc(y_hi, 1)

            def h_high(b, n):
                act.wait_ge(h_ready, b * HC + n + 3)
                nc.scalar.activation(hT[:, 0, n], h[:, n % 2], ACT.Copy).then_inc(h_hi, 1)

            y_high(0)

            def batch(b, more):
                for n in range(HC):
                    act.wait_ge(up_done, b * HC + n + 1)
                    act.wait_ge(h_ready, b * HC + n + 1)
                    nc.scalar.activation(gate[:, n % 2], g.PS[:, 2 + 2 * (n % 2), :], ACT.Silu, scale=FFN_SCALE / Y_UP
                                         ).then_inc(silu_done, 1)
                    if n:
                        h_high(b, n - 1)
                h_high(b, HC - 1)
                if more:
                    y_high(b + 1)

            batches(act, batch)

        @block.vector
        def _(dve):
            for s in (h_ready, h_lo, added):
                dve.sem_inc(s, 2)

            def norms(b):
                for t in range(TB):
                    normalise(nc, g, Y[:, t], b * TB + t).then_inc(normed, 1)

            def y_low(b):
                for e in range(EC):
                    dve.wait_ge(y_hi, b * EC + e + 1)
                    nc.vector.scalar_tensor_tensor(out=yT[:, 1, e], in0=g.PS[:, e, :], scalar=Y_UP, in1=yT[:, 0, e],
                                                   op0=ALU.mult, op1=ALU.subtract).then_inc(y_lo, 1)

            def h_low(b, n):
                dve.wait_ge(h_ready, b * HC + n + 3)
                dve.wait_ge(h_hi, b * HC + n + 3)
                nc.vector.tensor_tensor(hT[:, 1, n], h[:, n % 2], hT[:, 0, n], ALU.subtract).then_inc(h_lo, 1)

            norms(0)
            y_low(0)

            def batch(b, more):
                if more:
                    dve.wait_ge(turned, b * EC + EC)
                    norms(b + 1)
                for n in range(HC):
                    dve.wait_ge(silu_done, b * HC + n + 1)
                    dve.wait_ge(h_ready, b * HC + n + 1)
                    dve.wait_ge(h_hi, b * HC + n + 1)
                    dve.wait_ge(h_lo, b * HC + n + 1)
                    nc.vector.scalar_tensor_tensor(out=h[:, n % 2], in0=g.PS[:, 3 + 2 * (n % 2), :],
                                                   scalar=FFN_SCALE / Y_UP * H_DOWN, in1=gate[:, n % 2],
                                                   op0=ALU.mult, op1=ALU.mult).then_inc(h_ready, 1)
                    if n:
                        h_low(b, n - 1)
                h_low(b, HC - 1)
                if more:
                    y_low(b + 1)
                for t in range(TB):
                    at = b * TB + t
                    dve.wait_ge(down_done, at + 1)
                    hh = g.H[:, bass.ds(at, 1), :].rearrange("p a e -> p (a e)")
                    nc.vector.scalar_tensor_tensor(out=hh, in0=g.PS[:, 6 + t % 2, 0:E], scalar=FFN_SCALE / H_DOWN, in1=hh,
                                                   op0=ALU.mult, op1=ALU.add).then_inc(added, 1)
                    if t:
                        dve.wait_ge(added, at + 2)
                        statistics(nc, g, at - 1)
                dve.wait_ge(added, b * TB + TB + 2)
                statistics(nc, g, b * TB + TB - 1)

            batches(dve, batch)


def sparse_attention(nc, g, bq, bk, bv, bo):
    with ExitStack() as c:
        sb = lambda n, s, d=F32: c.enter_context(nc.sbuf_tensor("t_" + n, s, d))
        W = g.WT
        bqk, bvo = sb("bqk", [P, 2, EC]), sb("bvo", [P, 2, E])
        mask = sb("mask", [P, S])
        Y, yT, qkT, V1 = sb("Y", [P, TB, E]), sb("yT", [P, EC, S]), sb("qkT", [P, 2, 2, EC, S]), sb("V1", [P, 2, TB, E])
        sc, left, ex, pr = sb("sc", [P, S]), sb("left", [P, S]), sb("ex", [P, 2, S]), sb("pr", [P, 2, S])
        top, ntop, total, rec = sb("top", [P, TOPK]), sb("ntop", [P, 2]), sb("total", [P, TB]), sb("rec", [P, TB])
        pT, avT = sb("pT", [P, TB, S]), sb("avT", [P, EC, S])
        sem = lambda n: g.sem("t_" + n)
        b_in, masked, normed, biased, turned, copied, qk_done, qk_ready, v_done, v_ready = (sem(n) for n in (
            "b_in", "masked", "normed", "biased", "turned", "copied", "qk_done", "qk_ready", "v_done", "v_ready"))
        s_done, s_ready, top_ready, exped, p_ready, p_turned, p_copied, av_done, av_ready, o_done, added, chain, norm_ready = (
            sem(n) for n in ("s_done", "s_ready", "top_ready", "exped", "p_ready", "p_turned", "p_copied", "av_done",
                             "av_ready", "o_done", "added", "chain", "norm_ready"))
        waited = g.sem("t_waited")
        block = c.enter_context(nc.Block())
        LINKS = 2 * TB + 1

        @block.sync
        def _(sp):
            for n, src in enumerate((bq, bk)):
                sp.dma_start(bqk[:, n, :], src).then_inc(b_in, 16)
            for n, src in enumerate((bv, bo)):
                sp.dma_start(bvo[:, n, :], row(src)).then_inc(b_in, 16)

        @block.gpsimd
        def _(pool):
            st = Steps(pool, masked)
            st.link(nc.gpsimd.memset(mask[:], 0.0))
            st.link(nc.gpsimd.affine_select(out=mask[:, S - P:], in_=mask[:, S - P:], compare_op=ALU.is_ge, fill=NEG,
                                            base=0, pattern=[[-1, P]], channel_multiplier=1))
            pool.wait_ge(b_in, 16 * 4)
            with pool.Fori(0, B) as b:
                pool.wait_ge(normed, b * TB + TB)
                h = g.H[:, bass.ds(b * TB, TB), :]
                nc.gpsimd.tensor_tensor(h, h, bvo[:, 1].unsqueeze(1).broadcast_to([P, TB, E]), ALU.add).then_inc(biased, 1)

        def in_steps(eng, step):
            step(0, 0, True, False)
            with eng.Fori(0, B // 2 - 1) as n:
                step(n * 2 + 1, 1, True, True)
                step(n * 2 + 2, 0, True, True)
            step(B - 1, 1, False, True)

        @block.tensor
        def _(pe):
            pe.sem_inc(p_turned, 2)

            def turn(b):
                pe.wait_ge(normed, b * TB + TB)
                pe.wait_ge(av_ready, b * EC + EC)
                turn_batch(pe, nc, g, Y, 0, turned)

            def queries_keys(b, half, x):
                for d in range(EC):
                    if x == 0:
                        pe.wait_ge(copied, b * EC + EC)
                    else:
                        pe.wait_ge(qk_ready, b * 4 + d + 1)
                    for e in range(EC):
                        last = nc.tensor.matmul(g.PS[:, d, :], W[:, x, e, d * P:(d + 1) * P], yT[:, e],
                                                start=(e == 0), stop=(e == EC - 1))
                    last.then_inc(qk_done, 1)

            def values(b):
                for n in range(2):
                    pe.wait_ge(qk_ready, b * 4 + n + 3)
                    for t in (2 * n, 2 * n + 1):
                        for e in range(EC):
                            last = nc.tensor.matmul(g.PS[:, n, t % 2 * E:(t % 2 + 1) * E], yT[:, e, t * P:(t + 1) * P],
                                                    W[:, 2, e], start=(e == 0), stop=(e == EC - 1))
                    last.then_inc(v_done, 1)

            def scores(b, half, t):
                w = (t + 1) * P
                pe.wait_ge(qk_ready, b * 4 + 4)
                pe.wait_ge(s_ready, b * TB + t + 1)
                for d in range(EC):
                    last = nc.tensor.matmul(g.PS[:, 2 + t % 2, 0:w], qkT[:, half, 0, d, t * P:w], qkT[:, half, 1, d, 0:w],
                                            start=(d == 0), stop=(d == EC - 1))
                last.then_inc(s_done, 1)

            def turn_probs(b, t):
                pe.wait_ge(p_ready, b * TB + t + 1)
                pe.wait_ge(p_copied, b * TB + t + 1)
                for k in range(t + 1):
                    last = nc.tensor.transpose(g.PS[:, 4 + t % 2, k * P:(k + 1) * P], pr[:, t % 2, k * P:(k + 1) * P],
                                               g.identf[:])
                last.then_inc(p_turned, 1)

            def weighted(b, half, ahead):
                pe.wait_ge(p_copied, b * TB + TB + 2)
                pe.wait_ge(v_ready, b * 2 + (4 if ahead else 2))
                for d in range(EC):
                    for k in range(TB):
                        last = nc.tensor.matmul(g.PS[:, d, k * P:S], V1[:, half, k, d * P:(d + 1) * P], pT[:, k, k * P:S],
                                                start=(k == 0), stop=(k == TB - 1))
                    last.then_inc(av_done, 1)

            def projected(b):
                pe.wait_ge(av_ready, b * EC + 3 * EC)
                for t in range(TB):
                    pe.wait_ge(added, b * TB + t + 1)
                    for d in range(EC):
                        last = nc.tensor.matmul(g.PS[:, 6 + t % 2, 0:E], avT[:, d, t * P:(t + 1) * P], W[:, 3, d],
                                                start=(d == 0), stop=(d == EC - 1))
                    last.then_inc(o_done, 1)

            turn(0)
            queries_keys(0, 0, 0)
            queries_keys(0, 0, 1)
            values(0)

            def step(b, half, ahead, behind):
                scores(b, half, 0)
                if ahead:
                    turn(b + 1)
                scores(b, half, 1)
                if ahead:
                    queries_keys(b + 1, 1 - half, 0)
                turn_probs(b, 0)
                scores(b, half, 2)
                scores(b, half, 3)
                if ahead:
                    queries_keys(b + 1, 1 - half, 1)
                turn_probs(b, 1)
                if ahead:
                    values(b + 1)
                turn_probs(b, 2)
                turn_probs(b, 3)
                if behind:
                    projected(b - 1)
                weighted(b, half, ahead)

            in_steps(pe, step)
            projected(B - 1)

        @block.scalar
        def _(act):
            nc.scalar.preload_act_table(ACT.Exp)
            act.sem_inc(p_copied, 2)
            act.sem_inc(av_ready, 2 * EC)
            act.wait_ge(b_in, 16 * 4)

            def copy_y(b):
                for e in range(EC):
                    act.wait_ge(turned, b * EC + e + 1)
                    nc.scalar.activation(yT[:, e], g.PS[:, e, :], ACT.Copy).then_inc(copied, 1)

            def copy_queries_keys(b, half, x):
                for d in range(EC):
                    act.wait_ge(qk_done, b * 4 + 2 * x + d + 1)
                    nc.scalar.activation(qkT[:, half, x, d], g.PS[:, d, :], ACT.Identity,
                                         bias=bqk[:, x, d:d + 1]).then_inc(qk_ready, 1)

            def exponentials(b, t):
                w = (t + 1) * P
                act.wait_ge(top_ready, b * TB + t + 1)
                nc.scalar.activation(ex[:, t % 2, 0:w], sc[:, 0:w], ACT.Exp, bias=ntop[:, t % 2:t % 2 + 1]).then_inc(exped, 1)

            def copy_probs(b, t):
                act.wait_ge(p_turned, b * TB + t + 3)
                nc.scalar.activation(pT[:, 0:t + 1, t * P:(t + 1) * P],
                                     g.PS[:, 4 + t % 2, 0:(t + 1) * P].rearrange("p (k q) -> p k q", q=P),
                                     ACT.Copy).then_inc(p_copied, 1)

            copy_y(0)
            copy_queries_keys(0, 0, 0)
            copy_queries_keys(0, 0, 1)

            def step(b, half, ahead, behind):
                exponentials(b, 0)
                if ahead:
                    copy_y(b + 1)
                exponentials(b, 1)
                if ahead:
                    copy_queries_keys(b + 1, 1 - half, 0)
                copy_probs(b, 0)
                exponentials(b, 2)
                if ahead:
                    copy_queries_keys(b + 1, 1 - half, 1)
                copy_probs(b, 1)
                exponentials(b, 3)
                copy_probs(b, 2)
                copy_probs(b, 3)
                for d in range(EC):
                    act.wait_ge(av_done, b * EC + d + 1)
                    nc.scalar.activation(avT[:, d], g.PS[:, d, :], ACT.Copy).then_inc(av_ready, 1)

            in_steps(act, step)

        @block.vector
        def _(dve):
            for s in (s_ready, added):
                dve.sem_inc(s, 2)

            def norms(b, first=False):
                if not first:
                    dve.wait_ge(turned, b * EC)
                for t in range(TB):
                    normalise(nc, g, Y[:, t], b * TB + t).then_inc(normed, 1)

            def copy_values(b, half):
                for n in range(2):
                    dve.wait_ge(v_done, b * 2 + n + 1)
                    nc.vector.tensor_tensor(V1[:, half, 2 * n:2 * n + 2], g.PS[:, n, :].rearrange("p (t e) -> p t e", t=2),
                                            bvo[:, 0:1].broadcast_to([P, 2, E]), ALU.add).then_inc(v_ready, 1)

            def largest(b, t, st):
                w = (t + 1) * P
                dve.wait_ge(s_done, b * TB + t + 1)
                nc.vector.scalar_tensor_tensor(out=sc[:, 0:w], in0=g.PS[:, 2 + t % 2, 0:w], scalar=E ** -0.5,
                                               in1=mask[:, S - w:], op0=ALU.mult, op1=ALU.add).then_inc(s_ready, 1)
                dve.wait_ge(s_ready, b * TB + t + 3)
                dve.sem_inc(waited, 1)
                st.link(nc.vector.max(out=top[:], in_=sc[:, 0:w]))
                nc.vector.tensor_single_scalar(ntop[:, t % 2:t % 2 + 1], top[:, 0:1], -1.0, ALU.mult).then_inc(top_ready, 1)
                st.link(nc.vector.match_replace(out=left[:, 0:w], in_to_replace=top[:], in_values=sc[:, 0:w],
                                                imm_value=GONE))
                dve.wait_ge(exped, b * TB + t + 1)
                dve.wait_ge(p_turned, b * TB + t + 1)
                nc.vector.scalar_tensor_tensor(out=pr[:, t % 2, 0:w], in0=left[:, 0:w], scalar=GONE / 2, in1=ex[:, t % 2, 0:w],
                                               op0=ALU.is_lt, op1=ALU.mult, accum_out=total[:, t:t + 1]).then_inc(p_ready, 1)

            def add(b):
                dve.wait_ge(biased, b + 1)
                for t in range(TB):
                    at = b * TB + t
                    dve.wait_ge(o_done, at + 1)
                    h = g.H[:, bass.ds(at, 1), :].rearrange("p a e -> p (a e)")
                    nc.vector.scalar_tensor_tensor(out=h, in0=g.PS[:, 6 + t % 2, 0:E], scalar=rec[:, t:t + 1], in1=h,
                                                   op0=ALU.mult, op1=ALU.add).then_inc(added, 1)
                    if t:
                        dve.wait_ge(added, at + 2)
                        statistics(nc, g, at - 1)
                dve.wait_ge(added, b * TB + TB + 2)
                statistics(nc, g, b * TB + TB - 1)

            norms(0, first=True)
            dve.wait_ge(b_in, 16 * 4)
            dve.wait_ge(masked, 2)
            copy_values(0, 0)

            def step(b, half, ahead, behind):
                st = Steps(dve, chain, b, LINKS)
                if ahead:
                    norms(b + 1)
                for t in range(TB):
                    largest(b, t, st)
                if ahead:
                    copy_values(b + 1, 1 - half)
                if behind:
                    add(b - 1)
                dve.wait_ge(p_ready, b * TB + TB)
                st.link(nc.vector.reciprocal(rec[:], total[:]))

            in_steps(dve, step)
            add(B - 1)




UNROLL, LEAD = 8, 6


def choose_experts(nc, g, YA, chosen, router_wT, router_b):
    with ExitStack() as c:
        sb = lambda n, s, d=F32: c.enter_context(nc.sbuf_tensor("r_" + n, s, d))
        rw, rb = sb("rw", [P, EC, EXPERTS]), sb("rb", [P, EXPERTS])
        left, leftf = sb("left", [P, EXPERTS], I32), sb("leftf", [P, EXPERTS])
        Y, yT = sb("Y", [P, 2, TB, E]), sb("yT", [P, 2, EC, S])
        logit, best, first = sb("logit", [P, T, EXPERTS]), sb("best", [P, T]), sb("first", [P, T])
        sem = lambda n: g.sem("r_" + n)
        w_in, left_ready, normed, kept, turned, copied, l_done, l_read, chain = (sem(n) for n in (
            "w_in", "left_ready", "normed", "kept", "turned", "copied", "l_done", "l_read", "chain"))
        block = c.enter_context(nc.Block())
        full = [P, T, EXPERTS]

        @block.sync
        def _(sp):
            sp.dma_start(rw[:], router_wT.rearrange("(c p) x -> p c x", p=P)).then_inc(w_in, 16)
            sp.dma_start(rb[:], row(router_b)).then_inc(w_in, 16)

        @block.gpsimd
        def _(pool):
            nc.gpsimd.iota(left[:], pattern=[[-1, EXPERTS]], base=EXPERTS, channel_multiplier=0).then_inc(left_ready, 1)
            with pool.Fori(0, B // 2) as n:
                for half in range(2):
                    b = n * 2 + half
                    pool.wait_ge(normed, b * TB + TB)
                    nc.gpsimd.tensor_copy(YA[:, bass.ds(b * TB, TB), :], Y[:, half]).then_inc(kept, 1)

        @block.tensor
        def _(pe):
            pe.sem_inc(l_read, 2)
            pe.wait_ge(w_in, 32)

            def turn(b, half):
                pe.wait_ge(normed, b * TB + TB)
                turn_batch(pe, nc, g, Y[:, half], 2 * half, turned)

            def logits(b, half):
                pe.wait_ge(copied, b * EC + EC)
                pe.wait_ge(l_read, b + 1)
                for t in range(TB):
                    for e in range(EC):
                        last = nc.tensor.matmul(g.PS[:, 4 + half, t * EXPERTS:(t + 1) * EXPERTS],
                                                yT[:, half, e, t * P:(t + 1) * P], rw[:, e], start=(e == 0), stop=(e == EC - 1))
                last.then_inc(l_done, 1)

            turn(0, 0)
            with pe.Fori(0, B // 2 - 1) as n:
                for half in range(2):
                    turn(n * 2 + half + 1, 1 - half)
                    logits(n * 2 + half, half)
            turn(B - 1, 1)
            logits(B - 2, 0)
            logits(B - 1, 1)

        @block.scalar
        def _(act):
            with act.Fori(0, B // 2) as n:
                for half in range(2):
                    b = n * 2 + half
                    for e in range(EC):
                        act.wait_ge(turned, b * EC + 2 * EC + e + 1)
                        act.wait_ge(l_read, b + 1)
                        nc.scalar.activation(yT[:, half, e], g.PS[:, 2 * half + e, :], ACT.Copy).then_inc(copied, 1)

        @block.vector
        def _(dve):
            dve.sem_inc(kept, 2)
            dve.sem_inc(turned, 2 * EC)
            dve.wait_ge(w_in, 32)
            dve.wait_ge(left_ready, 1)
            nc.vector.tensor_copy(leftf[:], left[:]).then_inc(chain, 1)
            dve.wait_ge(chain, 1)

            def norms(b, half):
                dve.wait_ge(kept, b + 1)
                dve.wait_ge(turned, b * EC + EC)
                for t in range(TB):
                    normalise(nc, g, Y[:, half, t], b * TB + t).then_inc(normed, 1)

            def read(b, half):
                dve.wait_ge(l_done, b + 1)
                nc.vector.tensor_tensor(logit[:, bass.ds(b * TB, TB), :],
                                        g.PS[:, 4 + half, 0:TB * EXPERTS].rearrange("p (t x) -> p t x", t=TB),
                                        rb[:].unsqueeze(1).broadcast_to([P, TB, EXPERTS]), ALU.add).then_inc(l_read, 1)

            norms(0, 0)
            norms(1, 1)
            with dve.Fori(0, B // 2 - 1) as n:
                for half in range(2):
                    norms(n * 2 + half + 2, half)
                    read(n * 2 + half, half)
            read(B - 2, 0)
            read(B - 1, 1)
            dve.wait_ge(l_read, B + 2)
            st = Steps(dve, chain, base=1)
            st.link(nc.vector.tensor_reduce(best[:], logit[:], AX, ALU.max))
            st.link(nc.vector.tensor_tensor(logit[:], logit[:], best[:].unsqueeze(2).broadcast_to(full), ALU.is_ge))
            st.link(nc.vector.tensor_tensor(logit[:], logit[:], leftf[:].unsqueeze(1).broadcast_to(full), ALU.mult))
            st.link(nc.vector.tensor_reduce(first[:], logit[:], AX, ALU.max))
            nc.vector.tensor_tensor(chosen[:].rearrange("p x t -> p t x"), logit[:],
                                    first[:].unsqueeze(2).broadcast_to(full), ALU.is_equal)


def slots_by_expert(nc, g, chosen, slots, tile_expert, b1s, b1):
    with ExitStack() as c:
        sb = lambda n, s, d=F32: c.enter_context(nc.sbuf_tensor("s_" + n, s, d))
        tri, ones = sb("tri", [P, P], BF16), sb("ones", [P, P], BF16)
        number, numberf = sb("number", [P, SLOT_TILES], I32), sb("numberf", [P, SLOT_TILES])
        within = sb("within", [P, EXPERTS, T])
        upto, before = sb("upto", [P, EXPERTS, T]), sb("before", [P, EXPERTS, T])
        tiles, ends, starts, base = (sb(n, [P, EXPERTS]) for n in ("tiles", "ends", "starts", "base"))
        row_of, reached, expert = sb("row_of", [P, T]), sb("reached", [1, SLOT_TILES, EXPERTS]), sb("expert", [1, SLOT_TILES])
        bounds, hot, bias1 = sb("bounds", [EXPERTS, 2]), sb("hot", [EXPERTS, SLOT_TILES]), sb("bias1", [EXPERTS, EH])
        sem = lambda n: g.sem("s_" + n)
        b_in, made, counted, ends_ready, ends_turned, hot_ready, b_done, chain = (sem(n) for n in (
            "b_in", "made", "counted", "ends_ready", "ends_turned", "hot_ready", "b_done", "chain"))
        block = c.enter_context(nc.Block())
        flat = lambda a: a.rearrange("p x t -> p (x t)")
        banks = lambda n: g.PS[:, n:n + 2, :].rearrange("p a c -> p (a c)")
        prefix, counts = banks(0), banks(2)

        @block.sync
        def _(sp):
            sp.dma_start(bias1[:], b1).then_inc(b_in, 16)

        @block.gpsimd
        def _(pool):
            st = Steps(pool, made)
            st.link(nc.gpsimd.memset(tri[:], 1.0))
            st.link(nc.gpsimd.affine_select(out=tri[:], in_=tri[:], compare_op=ALU.is_ge, fill=0.0, base=-1,
                                            pattern=[[1, P]], channel_multiplier=-1))
            st.link(nc.gpsimd.memset(ones[:], 1.0))
            st.link(nc.gpsimd.memset(within[:], 1.0))
            st.link(nc.gpsimd.memset(within[:, :, 0:1], 0.0))
            st.link(nc.gpsimd.iota(number[:], pattern=[[1, SLOT_TILES]], base=0, channel_multiplier=0))

        @block.tensor
        def _(pe):
            pe.wait_ge(made, 3)
            for n, left in ((0, tri), (2, ones)):
                for h in range(2):
                    last = nc.tensor.matmul(g.PS[:, n + h, :], left[:], flat(chosen[:])[:, h * 512:(h + 1) * 512],
                                            start=True, stop=True)
            last.then_inc(counted, 1)
            pe.wait_ge(ends_ready, 1)
            for n, x in enumerate((ends, starts)):
                last = nc.tensor.transpose(g.PS[0:EXPERTS, 4, n * EXPERTS:(n + 1) * EXPERTS], x[0:EXPERTS, :],
                                           g.identf[0:EXPERTS, 0:EXPERTS])
            last.then_inc(ends_turned, 1)
            pe.wait_ge(hot_ready, 1)
            pe.wait_ge(b_in, 16)
            nc.tensor.matmul(g.PS[0:EH, 5, 0:SLOT_TILES], bias1[:], hot[:], start=True, stop=True).then_inc(b_done, 1)

        @block.vector
        def _(dve):
            v = nc.vector
            st = Steps(dve, chain)
            dve.wait_ge(made, 6)
            st.link(v.tensor_copy(numberf[:], number[:]))
            dve.wait_ge(counted, 1)
            st.link(v.tensor_tensor_scan(flat(upto[:]), flat(within[:]), counts, 0.0, ALU.mult, ALU.add))
            st.link(v.tensor_scalar(tiles[:], upto[:, :, T - 1], 1.0 / P, 63.5 / P, ALU.mult, ALU.add))
            st.link(v.tensor_single_scalar(tiles[:], tiles[:], ROUND, ALU.add))
            st.link(v.tensor_single_scalar(tiles[:], tiles[:], ROUND, ALU.subtract))
            st.link(v.tensor_tensor_scan(ends[:], within[:, 0, 1:2].broadcast_to([P, EXPERTS]), tiles[:], 0.0, ALU.mult, ALU.add))
            v.tensor_tensor(starts[:], ends[:], tiles[:], ALU.subtract).then_inc(ends_ready, 1)
            st.link(v.tensor_tensor(flat(before[:]), flat(upto[:]), counts, ALU.subtract))
            st.link(v.tensor_tensor(flat(before[:]), flat(before[:]), prefix, ALU.add))
            dve.wait_ge(ends_ready, 1)
            st.link(v.tensor_single_scalar(base[:], starts[:], float(P), ALU.mult))
            st.link(v.tensor_tensor(before[:], before[:], base[:].unsqueeze(2).broadcast_to([P, EXPERTS, T]), ALU.add))
            st.link(v.tensor_tensor(before[:], before[:], chosen[:], ALU.mult))
            st.link(v.tensor_reduce(row_of[:], before[:].rearrange("p x t -> p t x"), AX, ALU.add))
            v.tensor_copy(slots[:], row_of[:])
            dve.wait_ge(ends_turned, 1)
            st.link(v.tensor_copy(bounds[:], g.PS[0:EXPERTS, 4, 0:2 * EXPERTS:EXPERTS]))
            st.link(v.tensor_scalar(hot[:], numberf[0:EXPERTS, :], bounds[:, 1:2], None, ALU.is_ge))
            v.scalar_tensor_tensor(out=hot[:], in0=numberf[0:EXPERTS, :], scalar=bounds[:, 0:1], in1=hot[:],
                                   op0=ALU.is_lt, op1=ALU.mult).then_inc(hot_ready, 1)
            full = [1, SLOT_TILES, EXPERTS]
            st.link(v.tensor_tensor(reached[:], numberf[0:1].unsqueeze(2).broadcast_to(full),
                                    ends[0:1].unsqueeze(1).broadcast_to(full), ALU.is_ge))
            st.link(v.tensor_reduce(expert[:], reached[:], AX, ALU.add))
            v.tensor_single_scalar(tile_expert[:], expert[:], float(EXPERTS - 1), ALU.min)
            dve.wait_ge(b_done, 1)
            v.tensor_copy(b1s[:], g.PS[0:EH, 5, 0:SLOT_TILES])


def expert_tiles(nc, g, out, YA, YS, RS, slots, tile_expert, b1s, W12):
    with ExitStack() as c:
        sb = lambda n, s, d=F32: c.enter_context(nc.sbuf_tensor("e_" + n, s, d))
        y, w = sb("y", [P, UNROLL, E]), sb("w", [P, UNROLL, EC * EH + E])
        yT, hT, res = sb("yT", [P, 2, EC, P]), sb("hT", [EH + 1, 2, P]), sb("res", [P, UNROLL, E])
        sem = lambda n: g.sem("e_" + n)
        scattered, ones_made, turned, copied, h_done, h_ready, y_done, res_ready = (sem(n) for n in (
            "scattered", "ones_made", "turned", "copied", "h_done", "h_ready", "y_done", "res_ready"))
        added, written = sem("added"), sem("written")
        w_in = [sem(f"w_in{j}") for j in range(UNROLL)]
        y_in, stored = ({j: sem(f"{n}{j}") for j in range(0, UNROLL, 2)} for n in ("y_in", "stored"))
        gathered = [sem(f"gathered{b}") for b in range(B)]
        block = c.enter_context(nc.Block())
        BODIES = SLOT_TILES // UNROLL
        two_tiles = lambda ap, s: ap[bass.ds(s, 2)].rearrange("a p e -> p a e")

        def bodies(eng, body):
            with eng.Fori(0, BODIES - 1) as i:
                body(i, True)
            body(BODIES - 1, False)

        @block.sync
        def _(sp):
            def load(s, j):
                e = sp.value_load(tile_expert[0:1, bass.ds(s, 1)], min_val=0, max_val=EXPERTS - 1)
                sp.wait_ge(y_done, s + 1)
                sp.dma_start(w[:, j], W12[bass.ds(e, 1)].rearrange("a p n -> (a p) n")).then_inc(w_in[j], 16)

            with sp.Fori(0, BODIES) as i:
                for j in range(UNROLL):
                    load(i * UNROLL + j, j)
            o = out.rearrange("b (t p) e -> b p t e", p=P)
            for b in range(B):
                sp.wait_ge(added, b + 1)
                sp.dma_start(o[b], YA[:, b * TB:(b + 1) * TB, :]).then_inc(written, 16)
            sp.wait_ge(written, 16 * B)

        @block.gpsimd
        def _(pool):
            rows = YS.rearrange("a p e -> (a p) e")
            for t in range(T):
                nc.gpsimd.indirect_dma_start(out=rows, out_offset=bass.IndirectOffsetOnAxis(ap=slots[:, t:t + 1], axis=0),
                                             in_=YA[:, t, :], in_offset=None).then_inc(scattered, 16)
            for j in range(0, UNROLL, 2):
                pool.wait_ge(stored[j], 16 * BODIES + 16)
            rows = RS.rearrange("a p e -> (a p) e")
            for t in range(T):
                nc.gpsimd.indirect_dma_start(out=YA[:, t, :], out_offset=None, in_=rows,
                                             in_offset=bass.IndirectOffsetOnAxis(ap=slots[:, t:t + 1], axis=0)
                                             ).then_inc(gathered[t // TB], 16)

        @block.tensor
        def _(pe):
            pe.sem_inc(y_done, UNROLL)
            pe.sem_inc(h_done, 2)

            def turn(i, s, j):
                pe.wait_ge(w_in[j], i * 16 + 16)
                if j % 2 == 0:
                    pe.wait_ge(y_in[j], i * 16 + 16)
                pe.wait_ge(copied, s + 1)
                for e in range(EC):
                    last = nc.tensor.transpose(g.PS[:, j % 2, e * P:(e + 1) * P], y[:, j, e * P:(e + 1) * P], g.identf[:])
                last.then_inc(turned, 1)

            def first(s, j):
                pe.wait_ge(copied, s + 3)
                pe.wait_ge(h_ready, s + 1)
                for e in range(EC):
                    last = nc.tensor.matmul(g.PS[0:EH, 2 + j % 2, 0:P], w[:, j, e * EH:(e + 1) * EH], yT[:, j % 2, e],
                                            start=(e == 0), stop=(e == EC - 1))
                last.then_inc(h_done, 1)

            def second(s, j):
                pe.wait_ge(h_ready, s + 3)
                pe.wait_ge(res_ready, s + 1)
                nc.tensor.matmul(g.PS[:, 4 + j % 2, 0:E], hT[:, j % 2], w[0:EH + 1, j, EC * EH:], start=True, stop=True).then_inc(y_done, 1)

            turn(0, 0, 0)
            turn(0, 1, 1)
            first(0, 0)

            def body(i, more):
                for j in range(UNROLL):
                    s = i * UNROLL + j
                    if more or j + 2 < UNROLL:
                        turn(i + (j + 2) // UNROLL, s + 2, (j + 2) % UNROLL)
                    if more or j + 1 < UNROLL:
                        first(s + 1, (j + 1) % UNROLL)
                    second(s, j)

            bodies(pe, body)

        @block.scalar
        def _(act):
            for j in range(0, UNROLL, 2):
                act.sem_inc(stored[j], 16)

            def load(s, j):
                act.wait_ge(y_done, s + 2)
                act.dma_start(y[:, j:j + 2], two_tiles(YS, s)).then_inc(y_in[j], 16)

            def store(s, j):
                act.wait_ge(res_ready, s + 4)
                act.dma_start(two_tiles(RS, s), res[:, j:j + 2]).then_inc(stored[j], 16)

            act.wait_ge(scattered, 16 * T)
            for s in range(0, LEAD, 2):
                load(s, s)

            def body(i, more):
                for j in range(0, UNROLL, 2):
                    s = i * UNROLL + j
                    if more or j + LEAD < UNROLL:
                        load(s + LEAD, (j + LEAD) % UNROLL)
                    store(s, j)

            bodies(act, body)

        @block.vector
        def _(dve):
            dve.sem_inc(h_ready, 2)
            dve.sem_inc(copied, 2)
            dve.sem_inc(res_ready, 2)
            nc.vector.memset(hT[EH:EH + 1], 1.0).then_inc(ones_made, 1)
            dve.wait_ge(ones_made, 1)

            def copy(s, j):
                dve.wait_ge(turned, s + 1)
                dve.wait_ge(h_done, s + 1)
                nc.vector.tensor_copy(yT[:, j % 2], g.PS[:, j % 2, 0:E].rearrange("p (c n) -> p c n", c=EC)).then_inc(copied, 1)

            def relu(s, j):
                dve.wait_ge(h_done, s + 3)
                dve.wait_ge(y_done, s + UNROLL - 1)
                nc.vector.tensor_scalar(hT[0:EH, j % 2], g.PS[0:EH, 2 + j % 2, 0:P], b1s[:, bass.ds(s, 1)], 0.0,
                                        ALU.add, ALU.max).then_inc(h_ready, 1)

            copy(0, 0)
            copy(1, 1)
            relu(0, 0)

            def body(i, more):
                for j in range(UNROLL):
                    s = i * UNROLL + j
                    if more or j + 2 < UNROLL:
                        copy(s + 2, (j + 2) % UNROLL)
                    if more or j + 1 < UNROLL:
                        relu(s + 1, (j + 1) % UNROLL)
                    dve.wait_ge(y_done, s + UNROLL + 1)
                    if j % 2 == 0:
                        dve.wait_ge(stored[j], i * 16 + 16)
                    nc.vector.tensor_single_scalar(res[:, j], g.PS[:, 4 + j % 2, 0:E], 0.0, ALU.max).then_inc(res_ready, 1)

            bodies(dve, body)
            for b in range(B):
                dve.wait_ge(gathered[b], 16 * TB)
                ts = slice(b * TB, (b + 1) * TB)
                nc.vector.tensor_tensor(YA[:, ts], YA[:, ts], g.H[:, ts], ALU.add).then_inc(added, 1)


def routed_experts(nc, g, out, YS, RS, router_wT, router_b, W12, b1):
    with ExitStack() as c:
        sb = lambda n, s, d=F32: c.enter_context(nc.sbuf_tensor(n, s, d))
        YA, chosen = sb("YA", [P, T, E]), sb("chosen", [P, EXPERTS, T], BF16)
        slots, tile_expert, b1s = sb("slots", [P, T], I32), sb("tile_expert", [1, SLOT_TILES], I32), sb("b1s", [EH, SLOT_TILES])
        choose_experts(nc, g, YA, chosen, router_wT, router_b)
        slots_by_expert(nc, g, chosen, slots, tile_expert, b1s, b1)
        expert_tiles(nc, g, out, YA, YS, RS, slots, tile_expert, b1s, W12)


class Buffers:

    def __init__(self, nc):
        self.nc, self.sems = nc, []

    def sem(self, name):
        self.sems.append(self.nc.alloc_semaphore(name))
        return self.sems[-1]

    def free_sems(self):
        self.nc.clear_and_free_semaphores(self.sems)
        self.nc.all_engine_barrier()
        self.sems = []


def tower(nc, a, out):
    layer0 = lambda *names: (a["L0_" + n] for n in names)
    layer1 = lambda *names: (a["L1_" + n] for n in names)
    with ExitStack() as c:
        g = Buffers(nc)
        sb = lambda n, s, d=F32: c.enter_context(nc.sbuf_tensor(n, s, d))
        g.H = sb("H", [P, T, E])
        g.stats, g.mean, g.rstd = sb("stats", [P, T, 6]), sb("mean", [P, T]), sb("rstd", [P, T])
        g.V = sb("V", [P, T, E], BF16)
        g.ident, g.identf = sb("ident", [P, P], BF16), sb("identf", [P, P])
        g.mask_q, g.mask_k = sb("mask_q", [P, P], BF16), sb("mask_k", [P, P], BF16)
        g.WA, g.WP = sb("WA", [P, EC, 3 * E], BF16), sb("WP", [P, EC, E], BF16)
        g.WF, g.WT = sb("WF", [P, FFN_COLUMNS], F16), sb("WT", [P, 4, EC, E])
        g.PS = c.enter_context(nc.psum_tensor("PS", [P, 8, 512], F32))
        dram = lambda n, s, d: nc.dram_tensor(n, s, d, kind="Internal").ap()
        g.QT, g.KT = dram("QT", (NG, P, S), BF16), dram("KT", (NG, P, S), BF16)
        YS, RS = dram("YS", (SLOT_TILES, P, E), F32), dram("RS", (SLOT_TILES, P, E), F32)

        with ExitStack() as c2:
            sb2 = lambda n, s, d=F32: c2.enter_context(nc.sbuf_tensor(n, s, d))
            X, XQ, xs = sb2("X", [P, T, E]), sb2("XQ", [P, T, E], BF16), sb2("xs", [P, T])
            wa, wp = sb2("wa_f", [P, EC, 3 * E]), sb2("wp_f", [P, EC, E])
            constants_and_tokens(nc, g, a["x"], a["L0_tok_weights"], wa, wp, *layer0("attn_w_attn", "attn_w_proj"))
            layernorm(nc, g, X[:], "a_")
            quantise(nc, g, X[:], XQ[:], T, E, xs[:], False, "x_")
            qkv_quantised(nc, g, XQ, xs, a["L0_attn_b_attn"])

        with ExitStack() as c2:
            O = c2.enter_context(nc.sbuf_tensor("O", [P, T, E], F32))
            small = lambda n: c2.enter_context(nc.sbuf_tensor(n, [P, TB, NG, HG], F32))[:]
            neg_max, sums, lse = small("neg_max"), small("sums"), small("lse")
            key_max, key_scale, key_ln = small("key_max"), small("key_scale"), small("key_ln")
            q_max, q_scale, q_ln = small("q_max"), small("q_scale"), small("q_ln")
            score_maxima(nc, g, neg_max, True, sums, "sa_")
            log_sums(nc, g, lse, neg_max, sums)
            row_terms(nc, g, lse, g.QT, HD, "ra_")
            score_maxima(nc, g, key_max, False, None, "sb_")
            log_scales(nc, g, key_scale, key_ln, key_max, None, "lb_")
            row_terms(nc, g, key_ln, g.KT, HD + 3, "rb_")
            score_maxima(nc, g, q_max, True, None, "sc_", value_scale=key_scale)
            log_scales(nc, g, q_scale, q_ln, q_max, lse, "lc_")
            row_terms(nc, g, q_ln, g.QT, HD, "rc_")
            weighted_values(nc, g, O, q_scale, [*layer0("ffn_w_gate", "ffn_w_up", "ffn_w_down")])
            OQ = c2.enter_context(nc.sbuf_tensor("OQ", [P, T, E], BF16))
            os = c2.enter_context(nc.sbuf_tensor("os", [P, T], F32))
            projection(nc, g, O, OQ, os, a["L0_attn_b_proj"])
        g.free_sems()

        moments(nc, g, "m1_")
        feed_forward(nc, g, YS, [*layer1("attn_Wq", "attn_Wk", "attn_Wv", "attn_Wo")])
        moments(nc, g, "m2_")
        sparse_attention(nc, g, *layer1("attn_bq", "attn_bk", "attn_bv", "attn_bo"))
        moments(nc, g, "m3_")
        routed_experts(nc, g, out, YS, RS, *layer1("ffn_router_w", "ffn_router_b", "ffn_weights1", "ffn_bias1"))


def kernel(**inputs):
    import concourse.bacc as bacc
    from concourse.bass_utils import run_bass_kernel_spmd

    nc = bacc.Bacc("TRN2", target_bir_lowering=False, num_devices=1)
    arrays, args = {}, {}
    for name, value in inputs.items():
        v = np.asarray(value)
        if name in ("L0_ffn_w_gate", "L0_ffn_w_up", "L0_ffn_w_down", "L1_ffn_router_w"):
            v = v.T
        elif name in ("L1_attn_bq", "L1_attn_bk"):
            v = v.reshape(-1, P).T
        elif name in ("L1_ffn_weights2", "L1_ffn_bias2"):
            continue
        elif name == "L1_ffn_weights1":
            both = np.zeros((EXPERTS, P, EC * EH + E), v.dtype)
            both[:, :, 0:EC * EH] = v.reshape(EXPERTS, EC, P, EH).transpose(0, 2, 1, 3).reshape(EXPERTS, P, EC * EH)
            both[:, 0:EH, EC * EH:] = np.asarray(inputs["L1_ffn_weights2"])
            both[:, EH, EC * EH:] = np.asarray(inputs["L1_ffn_bias2"])
            v = both
        v = np.ascontiguousarray(v)
        arrays["in_" + name] = v
        args[name] = nc.dram_tensor("in_" + name, v.shape, mybir.dt.from_np(v.dtype), kind="ExternalInput").ap()
    out = nc.dram_tensor("out", (B, S, E), F32, kind="ExternalOutput").ap()
    tower(nc, args, out)
    return run_bass_kernel_spmd(nc, [arrays], core_ids=[0]).results[0]["out"]
```
